# Optimizing a Trainium2 kernel written in Bass

```python
import numpy as np
import jax
import jax.numpy as jnp

def _softmax(x, axis=-1):
    return jax.nn.softmax(x, axis=axis)

def _gelu(x):
    return jax.nn.gelu(x, approximate=True)

def _silu(x):
    return jax.nn.silu(x)

def _sigmoid(x):
    return jax.nn.sigmoid(x)

def _layernorm(x, axis=-1, eps=1e-05):
    m = jnp.mean(x, axis=axis, keepdims=True)
    v = jnp.var(x, axis=axis, keepdims=True)
    return (x - m) / jnp.sqrt(v + eps)

def _scatter_add(tgt, idx, src, axis=0):
    return tgt.at[idx].add(src)

def _segment_sum(src, seg, n):
    return jax.ops.segment_sum(src, seg, n)
kernel_name = 'mk_xattn_ffn_d2_seqx_r4_63d3e3'

def setup_inputs(seed: int=0):
    np.random.seed(seed)
    _w = jnp.asarray

    def _rec_inputs():
        import jax
        import jax.numpy as jnp
        _rk = jax.random.key(seed)
        x = 7.22e-05 + 1 * jax.random.normal(jax.random.fold_in(_rk, 1), (4, 512, 256), jnp.float32)
        _lenS = 512 - jax.random.randint(jax.random.fold_in(_rk, 7), (4,), 0, max(1, 512 // 4) + 1, jnp.int32)
        _lenS2 = 512 - jax.random.randint(jax.random.fold_in(_rk, 8), (4,), 0, max(1, 512 // 4) + 1, jnp.int32)
        _ctx_1024P = jax.random.normal(jax.random.fold_in(_rk, 11), (4, 16, 256), jnp.float32)
        _ctx_1024c = jax.random.dirichlet(jax.random.fold_in(_rk, 511), 0.3 * jnp.ones((16,), jnp.float32), (4, 512))
        _ctx_1024t = jnp.einsum('bsk,bkd->bsd', _ctx_1024c, _ctx_1024P)
        _ctx_1024t = _ctx_1024t * jax.lax.rsqrt(jnp.mean(jnp.square(_ctx_1024t)) + 1e-12) * 0.953939
        ctx_1024 = 4.13588e-05 + 0.999923 * (_ctx_1024t + 0.3 * jax.random.normal(jax.random.fold_in(_rk, 611), (4, 512, 256), jnp.float32))
        _validS = jnp.arange(512)[None, :] < _lenS[:, None]
        _validS2 = jnp.arange(512)[None, :] < _lenS2[:, None]
        _causal = jnp.tril(jnp.ones((512, 512), dtype=bool))
        mask_Bx1xSxS2_ik0 = jnp.where(jnp.broadcast_to(_validS2[:, None, None, :], (4, 1, 512, 512)), 0, 1).astype(jnp.int32)
        return (x, ctx_1024, mask_Bx1xSxS2_ik0)
    x, ctx_1024, mask_Bx1xSxS2_ik0 = _rec_inputs()

    def _L0_xattn_setup():
        import jax, jax.numpy as jnp
        import numpy as np
        B, S, D, H = (4, 512, 256, 16)
        DK = D // H

        def _split_heads(x):
            b, s, _ = x.shape
            return x.reshape(b, s, H, DK).transpose(0, 2, 1, 3)
        key = jax.random.key(seed)
        ks = jax.random.split(key, 8)
        Q = jax.random.normal(ks[0], (B, S, D), dtype=jnp.float32)
        K = jax.random.normal(ks[1], (B, S, D), dtype=jnp.float32)
        V = jax.random.normal(ks[2], (B, S, D), dtype=jnp.float32)
        mask = jnp.broadcast_to(jnp.tril(jnp.ones((S, S), dtype=jnp.int32))[None, None], (B, 1, S, S))
        scale = 1.0 / np.sqrt(D)
        W_Q = jax.random.normal(ks[3], (D, D), dtype=jnp.float32) * scale
        W_K = jax.random.normal(ks[4], (D, D), dtype=jnp.float32) * scale
        W_V = jax.random.normal(ks[5], (D, D), dtype=jnp.float32) * scale
        W_O = jax.random.normal(ks[6], (D, D), dtype=jnp.float32) * scale
        return {'Q': Q, 'K': K, 'V': V, 'mask': mask, 'W_Q': W_Q, 'W_K': W_K, 'W_V': W_V, 'W_O': W_O}
    _L0_xattn_all = _L0_xattn_setup()
    _L0_xattn_in = {k: v for k, v in _L0_xattn_all.items() if k in ('W_Q', 'W_K', 'W_V', 'W_O')}
    del _L0_xattn_all

    def _L0_ffn_setup():
        import jax, jax.numpy as jnp
        import numpy as np
        B, S, H, NH, E, F = (4, 256, 256, 16, 8, 1024)
        D = H // NH
        EPS = 1e-05

        def _layernorm(x, g, b):
            mu = jnp.mean(x, axis=-1, keepdims=True)
            var = jnp.var(x, axis=-1, keepdims=True)
            return (x - mu) * jax.lax.rsqrt(var + EPS) * g + b
        key = jax.random.key(seed)
        ks = jax.random.split(key, 16)
        s = 0.02
        return {'x': jax.random.normal(ks[0], (B, S, H), jnp.float32), 'ln1_g': jnp.ones((H,), jnp.float32), 'ln1_b': jnp.zeros((H,), jnp.float32), 'ln2_g': jnp.ones((H,), jnp.float32), 'ln2_b': jnp.zeros((H,), jnp.float32), 'wq': jax.random.normal(ks[1], (H, H), jnp.float32) * s, 'bq': jnp.zeros((H,), jnp.float32), 'wk': jax.random.normal(ks[2], (H, H), jnp.float32) * s, 'bk': jnp.zeros((H,), jnp.float32), 'wv': jax.random.normal(ks[3], (H, H), jnp.float32) * s, 'bv': jnp.zeros((H,), jnp.float32), 'wo': jax.random.normal(ks[4], (H, H), jnp.float32) * s, 'bo': jnp.zeros((H,), jnp.float32), 'gate_w': jax.random.normal(ks[5], (H, E), jnp.float32) * s, 'gate_b': jnp.zeros((E,), jnp.float32), 'w1': jax.random.normal(ks[6], (E, H, F), jnp.float32) * s, 'b1': jnp.zeros((E, F), jnp.float32), 'w2': jax.random.normal(ks[7], (E, F, H), jnp.float32) * s, 'b2': jnp.zeros((E, H), jnp.float32)}
    _L0_ffn_all = _L0_ffn_setup()
    _L0_ffn_in = {k: v for k, v in _L0_ffn_all.items() if k in ('ln1_g', 'ln1_b', 'ln2_g', 'ln2_b', 'wq', 'bq', 'wk', 'bk', 'wv', 'bv', 'wo', 'bo', 'gate_w', 'gate_b', 'w1', 'b1', 'w2', 'b2')}
    del _L0_ffn_all

    def _L1_xattn_setup():
        import jax, jax.numpy as jnp
        import numpy as np
        D_MODEL = 256
        NUM_HEADS = 16
        HEAD_DIM = D_MODEL // NUM_HEADS
        B, S = (4, 512)
        key = jax.random.key(seed)
        ks = jax.random.split(key, 11)
        scale = 1.0 / np.sqrt(D_MODEL)
        inp = {'query': jax.random.normal(ks[0], (B, S, D_MODEL), dtype=jnp.float32), 'key': jax.random.normal(ks[1], (B, S, D_MODEL), dtype=jnp.float32), 'value': jax.random.normal(ks[2], (B, S, D_MODEL), dtype=jnp.float32), 'Wq': jax.random.normal(ks[3], (D_MODEL, D_MODEL), dtype=jnp.float32) * scale, 'bq': jnp.zeros((D_MODEL,), dtype=jnp.float32), 'Wk': jax.random.normal(ks[4], (D_MODEL, D_MODEL), dtype=jnp.float32) * scale, 'bk': jnp.zeros((D_MODEL,), dtype=jnp.float32), 'Wv': jax.random.normal(ks[5], (D_MODEL, D_MODEL), dtype=jnp.float32) * scale, 'bv': jnp.zeros((D_MODEL,), dtype=jnp.float32), 'Wo': jax.random.normal(ks[6], (D_MODEL, D_MODEL), dtype=jnp.float32) * scale, 'bo': jnpp.zeros((D_MODEL,), dtype=jnp.float32) if False else jnp.zeros((D_MODEL,), dtype=jnp.float32)}
        return inp
    _L1_xattn_all = _L1_xattn_setup()
    _L1_xattn_in = {k: v for k, v in _L1_xattn_all.items() if k in ('Wq', 'bq', 'Wk', 'bk', 'Wv', 'bv', 'Wo', 'bo')}
    del _L1_xattn_all

    def _L1_ffn_setup():
        import jax, jax.numpy as jnp
        import numpy as np
        B, S, D, E = (4, 1024, 256, 8)
        key = jax.random.key(seed)
        k1, k2, k3, k4, k5 = jax.random.split(key, 5)
        scale = 1.0 / np.sqrt(D)
        return {'x': jax.random.normal(k1, (B, S, D), dtype=jnp.float32), 'Wg': jax.random.normal(k2, (D, D), dtype=jnp.float32) * scale, 'bg': jnp.zeros((D,), dtype=jnp.float32), 'We': jax.random.normal(k3, (E, D, D), dtype=jnp.float32) * scale, 'be': jnp.zeros((E, D), dtype=jnp.float32)}
    _L1_ffn_all = _L1_ffn_setup()
    _L1_ffn_in = {k: v for k, v in _L1_ffn_all.items() if k in ('Wg', 'bg', 'We', 'be')}
    del _L1_ffn_all
    return {'x': x, 'ctx_1024': ctx_1024, 'mask_Bx1xSxS2_ik0': mask_Bx1xSxS2_ik0, 'L0_xattn_W_Q': _L0_xattn_in['W_Q'], 'L0_xattn_W_K': _L0_xattn_in['W_K'], 'L0_xattn_W_V': _L0_xattn_in['W_V'], 'L0_xattn_W_O': _L0_xattn_in['W_O'], 'L0_ffn_ln1_g': _L0_ffn_in['ln1_g'], 'L0_ffn_ln1_b': _L0_ffn_in['ln1_b'], 'L0_ffn_ln2_g': _L0_ffn_in['ln2_g'], 'L0_ffn_ln2_b': _L0_ffn_in['ln2_b'], 'L0_ffn_wq': _L0_ffn_in['wq'], 'L0_ffn_bq': _L0_ffn_in['bq'], 'L0_ffn_wk': _L0_ffn_in['wk'], 'L0_ffn_bk': _L0_ffn_in['bk'], 'L0_ffn_wv': _L0_ffn_in['wv'], 'L0_ffn_bv': _L0_ffn_in['bv'], 'L0_ffn_wo': _L0_ffn_in['wo'], 'L0_ffn_bo': _L0_ffn_in['bo'], 'L0_ffn_gate_w': _L0_ffn_in['gate_w'], 'L0_ffn_gate_b': _L0_ffn_in['gate_b'], 'L0_ffn_w1': _L0_ffn_in['w1'], 'L0_ffn_b1': _L0_ffn_in['b1'], 'L0_ffn_w2': _L0_ffn_in['w2'], 'L0_ffn_b2': _L0_ffn_in['b2'], 'L1_xattn_Wq': _L1_xattn_in['Wq'], 'L1_xattn_bq': _L1_xattn_in['bq'], 'L1_xattn_Wk': _L1_xattn_in['Wk'], 'L1_xattn_bk': _L1_xattn_in['bk'], 'L1_xattn_Wv': _L1_xattn_in['Wv'], 'L1_xattn_bv': _L1_xattn_in['bv'], 'L1_xattn_Wo': _L1_xattn_in['Wo'], 'L1_xattn_bo': _L1_xattn_in['bo'], 'L1_ffn_Wg': _L1_ffn_in['Wg'], 'L1_ffn_bg': _L1_ffn_in['bg'], 'L1_ffn_We': _L1_ffn_in['We'], 'L1_ffn_be': _L1_ffn_in['be']}

def reference(x, ctx_1024, mask_Bx1xSxS2_ik0, L0_xattn_W_Q, L0_xattn_W_K, L0_xattn_W_V, L0_xattn_W_O, L0_ffn_ln1_g, L0_ffn_ln1_b, L0_ffn_ln2_g, L0_ffn_ln2_b, L0_ffn_wq, L0_ffn_bq, L0_ffn_wk, L0_ffn_bk, L0_ffn_wv, L0_ffn_bv, L0_ffn_wo, L0_ffn_bo, L0_ffn_gate_w, L0_ffn_gate_b, L0_ffn_w1, L0_ffn_b1, L0_ffn_w2, L0_ffn_b2, L1_xattn_Wq, L1_xattn_bq, L1_xattn_Wk, L1_xattn_bk, L1_xattn_Wv, L1_xattn_bv, L1_xattn_Wo, L1_xattn_bo, L1_ffn_Wg, L1_ffn_bg, L1_ffn_We, L1_ffn_be):
    import jax
    import jax.numpy as jnp

    def _L0_xattn_ref(Q, K, V, mask, W_Q, W_K, W_V, W_O):
        import jax, jax.numpy as jnp
        import numpy as np
        B, S, D, H = (4, 512, 256, 16)
        DK = D // H

        def _split_heads(x):
            b, s, _ = x.shape
            return x.reshape(b, s, H, DK).transpose(0, 2, 1, 3)
        q = _split_heads(Q @ W_Q.T)
        k = _split_heads(K @ W_K.T)
        v = _split_heads(V @ W_V.T)
        scores = jnp.einsum('bhqd,bhkd->bhqk', q, k) / jnp.sqrt(jnp.float32(DK))
        scores = jnp.where(mask == 0, -jnp.inf, scores)
        weights = jax.nn.softmax(scores, axis=-1)
        weights = jnp.nan_to_num(weights, nan=0.0)
        attn = jnp.einsum('bhqk,bhkd->bhqd', weights, v)
        attn = attn.transpose(0, 2, 1, 3).reshape(Q.shape[0], Q.shape[1], D)
        return attn @ W_O.T

    def _L0_ffn_ref(x, ln1_g, ln1_b, ln2_g, ln2_b, wq, bq, wk, bk, wv, bv, wo, bo, gate_w, gate_b, w1, b1, w2, b2):
        import jax, jax.numpy as jnp
        import numpy as np
        B, S, H, NH, E, F = (4, 256, 256, 16, 8, 1024)
        D = H // NH
        EPS = 1e-05

        def _layernorm(x, g, b):
            mu = jnp.mean(x, axis=-1, keepdims=True)
            var = jnp.var(x, axis=-1, keepdims=True)
            return (x - mu) * jax.lax.rsqrt(var + EPS) * g + b
        b, s, h = x.shape
        hn = _layernorm(x, ln1_g, ln1_b)
        q = (hn @ wq + bq).reshape(b, s, NH, D).transpose(0, 2, 1, 3)
        k = (hn @ wk + bk).reshape(b, s, NH, D).transpose(0, 2, 1, 3)
        v = (hn @ wv + bv).reshape(b, s, NH, D).transpose(0, 2, 1, 3)
        scores = jnp.einsum('bhqd,bhkd->bhqk', q, k) / jnp.sqrt(jnp.float32(D))
        attn = jax.nn.softmax(scores, axis=-1)
        o = jnp.einsum('bhqk,bhkd->bhqd', attn, v)
        o = o.transpose(0, 2, 1, 3).reshape(b, s, h)
        x = x + (o @ wo + bo)
        hn2 = _layernorm(x, ln2_g, ln2_b).reshape(-1, h)
        logits = hn2 @ gate_w + gate_b
        idx = jnp.argmax(logits, axis=-1)
        mid = jax.nn.relu(jnp.einsum('th,ehf->etf', hn2, w1) + b1[:, None, :])
        y = jnp.einsum('etf,efh->eth', mid, w2) + b2[:, None, :]
        moe = y[idx, jnp.arange(hn2.shape[0])]
        return x + moe.reshape(b, s, h)

    def _L1_xattn_ref(query, key, value, Wq, bq, Wk, bk, Wv, bv, Wo, bo):
        import jax, jax.numpy as jnp
        import numpy as np
        D_MODEL = 256
        NUM_HEADS = 16
        HEAD_DIM = D_MODEL // NUM_HEADS
        B, S = (4, 512)

        def split_heads(x):
            b, s, _ = x.shape
            return x.reshape(b, s, NUM_HEADS, HEAD_DIM).transpose(0, 2, 1, 3)
        q = split_heads(query @ Wq.T + bq)
        k = split_heads(key @ Wk.T + bk)
        v = split_heads(value @ Wv.T + bv)
        scores = jnp.einsum('bhqd,bhkd->bhqk', q, k) / np.sqrt(HEAD_DIM).astype(np.float32)
        attn = jax.nn.softmax(scores, axis=-1)
        ctx = jnp.einsum('bhqk,bhkd->bhqd', attn, v)
        b = ctx.shape[0]
        ctx = ctx.transpose(0, 2, 1, 3).reshape(b, -1, D_MODEL)
        return ctx @ Wo.T + bo

    def _L1_ffn_ref(x, Wg, bg, We, be):
        import jax, jax.numpy as jnp
        import numpy as np
        B, S, D, E = (4, 1024, 256, 8)
        probs = jax.nn.softmax(x @ Wg + bg, axis=-1)
        idx = jnp.argmax(probs, axis=-1)
        p = jnp.take_along_axis(probs, idx[..., None], axis=-1)[..., 0]
        e_idx = idx % We.shape[0]
        h = jax.nn.relu(jnp.einsum('bsd,edf->besf', x, We) + be[None, :, None, :])
        onehot = jax.nn.one_hot(e_idx, We.shape[0], dtype=x.dtype)
        out = jnp.einsum('besf,bse->bsf', h, onehot) * p[..., None]
        return out
    x = x + _L0_xattn_ref(_layernorm(x, axis=-1), ctx_1024, ctx_1024, mask_Bx1xSxS2_ik0, L0_xattn_W_Q, L0_xattn_W_K, L0_xattn_W_V, L0_xattn_W_O)
    x = x + _L0_ffn_ref(_layernorm(x, axis=-1), L0_ffn_ln1_g, L0_ffn_ln1_b, L0_ffn_ln2_g, L0_ffn_ln2_b, L0_ffn_wq, L0_ffn_bq, L0_ffn_wk, L0_ffn_bk, L0_ffn_wv, L0_ffn_bv, L0_ffn_wo, L0_ffn_bo, L0_ffn_gate_w, L0_ffn_gate_b, L0_ffn_w1, L0_ffn_b1, L0_ffn_w2, L0_ffn_b2)
    x = x + _L1_xattn_ref(_layernorm(x, axis=-1), ctx_1024, ctx_1024, L1_xattn_Wq, L1_xattn_bq, L1_xattn_Wk, L1_xattn_bk, L1_xattn_Wv, L1_xattn_bv, L1_xattn_Wo, L1_xattn_bo)
    x = x + _L1_ffn_ref(_layernorm(x, axis=-1), L1_ffn_Wg, L1_ffn_bg, L1_ffn_We, L1_ffn_be)
    return x

_drawn_inputs = setup_inputs


def setup_inputs(seed=0):
    import zlib

    import numpy as np

    out = dict(_drawn_inputs(seed))
    spreads = {'L0_ffn_ln1_g': (1.0, 0.6),
     'L0_ffn_ln1_b': (0.0, 0.755),
     'L0_ffn_ln2_g': (1.0, 0.2),
     'L0_ffn_ln2_b': (0.0, 0.275),
     'L0_ffn_bq': (0.0, 0.8),
     'L0_ffn_bk': (0.0, 0.8),
     'L0_ffn_bv': (0.0, 0.419),
     'L0_ffn_bo': (0.0, 0.1),
     'L0_ffn_gate_b': (0.0, 0.1),
     'L0_ffn_b1': (0.0, 0.445),
     'L0_ffn_b2': (0.0, 0.1),
     'L1_xattn_bq': (0.0, 0.8),
     'L1_xattn_bk': (0.0, 0.8),
     'L1_xattn_bv': (0.0, 0.1),
     'L1_xattn_bo': (0.0, 0.1),
     'L1_ffn_bg': (0.0, 0.8),
     'L1_ffn_be': (0.0, 0.8)}
    factors = {'L0_ffn_wq': 8.0, 'L0_ffn_wk': 8.0, 'L1_ffn_Wg': 5.094, 'L1_ffn_We': 4.949}
    for name, (base, spread) in spreads.items():
        noise = np.random.default_rng([zlib.crc32(name.encode()), seed]).standard_normal(out[name].shape)
        drawn = base * np.exp(spread * noise) if base else spread * noise
        out[name] = jnp.asarray(drawn.astype(out[name].dtype))
    for name, factor in factors.items():
        out[name] = (out[name] * factor).astype(out[name].dtype)
    return out
```

```python
from contextlib import ExitStack

import numpy as np

import concourse.bass as bass
from concourse import mybir

F32 = mybir.dt.float32
BF16 = mybir.dt.bfloat16
I32 = mybir.dt.int32
U32 = mybir.dt.uint32
ALU = mybir.AluOpType
ACT = mybir.ActivationFunctionType
AX = mybir.AxisListType

P = 128
B, S, D, H = 4, 512, 256, 16
DK = D // H
T = S // P
C = D // P
HG = 4
NG = H // HG
GW = HG * DK
TERMS = 6
ROWS = TERMS * DK
PARTS = 3
KROWS = ROWS + PARTS
VW = 32
E = 8
F = 1024
FT = F // P
NT = B * T
SLOTS = NT + E - 1
EPS = 1e-5
MASKED = -(2.0 ** 100)
FLOOR = -1e29
SCALE = float(DK) ** -0.5


class Signal:

    def __init__(self, sem, per, lead=0):
        self.sem, self.per, self.lead = sem, per, lead

    def at(self, i, k=0):
        return i * self.per + (self.lead + k)


def wait_alone(eng, sem, value, passed):
    eng.wait_ge(sem, value)
    eng.sem_inc(passed, 1)


class Memory:

    def __init__(self, nc, ctx):
        def sb(name, shape, dt=F32):
            return ctx.enter_context(nc.sbuf_tensor(name, shape, dt))

        self.x = sb("x", [P, B, T, D])
        self.w = [sb(f"w{i}", [P, 4, C, D]) for i in range(2)]
        self.r1 = sb("r1", [P, C * E * F])
        self.r2 = sb("r2", [P, 24576])
        self.cols = sb("cols", [P, 20])
        self.rows = sb("rows", [P, 5, D])
        self.gate = sb("gate", [P, C, D])
        self.ident = sb("ident", [P, P])
        self.identb = sb("identb", [P, P], BF16)
        self.neghalf = sb("neghalf", [P, T])
        self.stats = sb("stats", [P, T, 6])
        self.mv = sb("mv", [P, T, 2])
        self.var = sb("var", [P, T])
        self.rstd = sb("rstd", [P, T])
        self.mv_in = sb("mv_in", [P, B, T, 2])
        self.rstd_in = sb("rstd_in", [P, B, T])
        self.m = sb("m", [P, 2, T, HG])
        self.mres = sb("mres", [P, T, HG])
        self.mparts = sb("mparts", [P, T, PARTS, HG], BF16)
        self.mT = sb("mT", [PARTS * HG, S], BF16)
        self.den = sb("den", [P, T, HG])
        self.rden = sb("rden", [P, T, HG])
        self.tri = sb("tri", [P, P])
        self.ones = sb("ones", [P, P])
        self.zero = sb("zero", [SLOTS, P], I32)
        self.count_i = sb("count_i", [P, SLOTS + T], I32)
        self.count = sb("count", [P, SLOTS + T])
        self.token = sb("token", [P, NT], I32)
        self.b1c = sb("b1c", [P, E * FT])
        self.top8 = sb("top8", [P, T, 8])
        self.idx8 = sb("idx8", [P, T, 8], U32)
        self.expert_u = sb("expert_u", [P, T], U32)
        self.ntop = sb("ntop", [P, T])
        self.sum = sb("sum", [P, T])
        self.expert = sb("expert", [P, B, T])
        self.prob = sb("prob", [P, B, T])
        self.onehot = sb("onehot", [P, NT, E])
        self.tiles = sb("tiles", [P, NT, E])
        self.place = sb("place", [P, NT, E])
        self.more = sb("more", [P, SLOTS, E])
        self.total = sb("total", [P, E])
        self.need = sb("need", [P, E])
        self.end = sb("end", [P, E])
        self.start = sb("start", [P, E])
        self.pos = sb("pos", [P, NT])
        self.pos_u = sb("pos_u", [P, NT], U32)
        self.slot_f = sb("slot_f", [P, SLOTS])
        self.slot_e = sb("slot_e", [P, SLOTS], I32)
        self.inv = sb("inv", [P, SLOTS], U32)
        self.ps = ctx.enter_context(nc.psum_tensor("ps", [P, 8, 512], F32))
        self._r1 = self._r2 = 0

        at = [0]

        def take(region, words, shape, dt=F32):
            n = at[0]
            at[0] += words
            assert at[0] <= region.shape[1], (at[0], region.shape)
            v = region[:, n:n + words]
            if dt is not F32:
                v = v.bitcast(dt)
            if len(shape) == 1:
                return v
            names = "abcd"[:len(shape)]
            kw = dict(zip(names[1:], shape[1:]))
            return v.rearrange(f"p ({' '.join(names)}) -> p {' '.join(names)}", **kw)

        self.hn = take(self.r1, T * D, [T, D])
        self.hT = take(self.r1, C * S, [C, S])
        self.cin = take(self.r1, T * D, [T, D])
        self.cT = take(self.r1, C * S, [C, S])
        self.parts = [take(self.r1, PARTS * S // 2, [PARTS, S], BF16) for _ in range(2 * C)]
        self.res = [take(self.r1, S, [S]) for _ in range(2)]
        self.mb_all = take(self.r1, B * T * S // 2, [B, T, S], BF16)
        self.mint = take(self.r1, T * S, [T, S], I32)
        self.mbS = take(self.r1, T * S // 2, [T, S], BF16)
        self.mbT = take(self.r1, T * S // 2, [T, S], BF16)
        self.w1 = self.r1[:, :].rearrange("p (c e f) -> p c e f", c=C, e=E)
        self.we = self.r1[:, 0:C * E * D].rearrange("p (c e f) -> p c e f", c=C, e=E)

        at[0] = 0
        self.probs = take(self.r2, T * HG * S, [T, HG, S])
        self.qst = [take(self.r2, HG * S // 2, [HG, S], BF16) for _ in range(NG)]
        self.kst = [take(self.r2, HG * S // 2, [HG, S], BF16) for _ in range(NG)]
        self.v = take(self.r2, B * NG * T * GW, [B, NG, T, GW])
        self.vg = [take(self.r2, T * HG * VW, [T, HG, VW]) for _ in range(2)]
        self.ot = take(self.r2, S, [S])
        self.o = take(self.r2, T * D, [T, D])
        self.oT = take(self.r2, C * S, [C, S])
        self.junk = [take(self.r2, S // 2, [S], BF16) for _ in range(2)]
        at[0] = 0
        self.w2 = take(self.r2, FT * E * D, [FT, E, D])
        self.xg = [take(self.r2, D, [D]) for _ in range(2)]
        self.xT = [take(self.r2, C * P, [C, P]) for _ in range(2)]
        self.mid = take(self.r2, F, [F])
        self.midT = take(self.r2, FT * P, [FT, P])
        self.y = [take(self.r2, D, [D]) for _ in range(2)]
        self.rn = take(self.r2, T * D, [T, D])
        self.rnT = take(self.r2, C * S, [C, S])
        self.logits = self.mid.rearrange("p (t d) -> p t d", t=T)
        self.exps = self.midT.rearrange("p f n -> p (f n)").rearrange("p (t d) -> p t d", t=T)
        self.b2 = take(self.r2, E * D, [E, D])
        self.yg = self.r2[:, 0:NT * D].rearrange("p (t d) -> p t d", t=NT)


class Attention:

    def __init__(self, nc, ctx, stage, mem, dram, name, w, cross, norms, affine, cols, rows, masked, self_block):
        self.mem, self.dram, self.name = mem, dram, name
        self.w, self.cross, self.norms, self.affine = mem.w[w], cross, norms, affine
        self.cols, self.rows, self.masked, self.self_block = cols, rows, masked, self_block

        self.used = []

        def sig(what, per, lead=0, kept=stage):
            self.used.append(kept.enter_context(nc.semaphore(f"{name}_{what}")))
            return Signal(self.used[-1], per, lead)

        self.passed = {eng: stage.enter_context(nc.semaphore(f"{name}_{eng}_passed")) for eng in ("dve", "pool")}
        self.stat = [sig(f"stat{n}", T) for n in range(norms)]
        self.aggr = [sig(f"aggr{n}", T) for n in range(norms)]
        self.vare = [sig(f"vare{n}", 1) for n in range(norms)]
        self.rs = [sig(f"rs{n}", 1) for n in range(norms)]
        self.first_norm = sig("first_norm", T)
        self.hn_ready = sig("hn_ready", T)
        self.hT_ps = sig("hT_ps", C, C)
        self.hT_ready = sig("hT_ready", C, C)
        self.c_loaded = sig("c_loaded", 16, kept=ctx)
        self.cT_ps = sig("cT_ps", C, C)
        self.cT_ready = sig("cT_ready", C, C)
        self.qk_ps = sig("qk_ps", 2 * C, 2 * C)
        self.hi = sig("hi", 2 * C)
        self.r1 = sig("r1", 2 * C)
        self.midp = sig("midp", 2 * C)
        self.lo = sig("lo", 2 * C, 2 * C)
        self.stored = sig("stored", 16 * 12, 16 * 12)
        self.v_ps = sig("v_ps", 2)
        self.v_ready = sig("v_ready", 2, 2)
        self.mask_loaded = sig("mask_loaded", 16, kept=ctx)
        self.mask_bias = sig("mask_bias", 1, 1)
        self.preset = sig("preset", 1)
        self.stacks = [sig(f"stacks{s}", 32) for s in range(NG)]
        self.shift = [sig(f"shift{s}", 16) for s in range(NG)]
        self.s_ps = sig("s_ps", 16)
        self.s_max = sig("s_max", 16, 2)
        self.m_hi = sig("m_hi", 1)
        self.m_res = sig("m_res", 1)
        self.m_mid = sig("m_mid", 1)
        self.m_lo = sig("m_lo", 1)
        self.m_ps = sig("m_ps", 1)
        self.m_sb = sig("m_sb", 1)
        self.st_ps = sig("st_ps", 8)
        self.p_exp = sig("p_exp", 8, 2)
        self.vg_ready = sig("vg_ready", 1)
        self.pv = sig("pv", T, T)
        self.ot_sb = sig("ot_sb", 1, 1)
        self.ot_ps = sig("ot_ps", 1, 1)
        self.den = sig("den", 1)
        self.rden = sig("rden", 1)
        self.o_ready = sig("o_ready", 1)
        self.oT_ps = sig("oT_ps", C)
        self.oT_sb = sig("oT_sb", C)
        self.op_ps = sig("op_ps", 2)
        self.op_used = sig("op_used", 2)
        self.step = [sig(f"step{n}", 2) for n in range(4)] if self_block else []
        self.acc_ready = sig("acc_ready", 2)
        self.acc_stored = sig("acc_stored", 32, 32)
        self.mbS_ready = sig("mbS_ready", 1)
        self.mbT_ready = sig("mbT_ready", 1)




def project_vector(dve, a):
    mem = a.mem
    ps = mem.ps
    for s in range(NG):
        dve.memset(mem.kst[s][ROWS:P, :, :], 1.0)
    for g in range(2):
        dve.memset(mem.vg[g][:, :, :, DK:VW], 0.0)
    dve.sem_inc(a.v_ready.sem, a.v_ready.lead)
    dve.sem_inc(a.lo.sem, a.lo.lead)
    if a.masked:
        dve.sem_inc(a.mask_bias.sem, a.mask_bias.lead)
    with dve.Fori(0, B) as b:
        for n in range(a.norms):
            for t in range(T):
                src = mem.x[:, b, t, :] if n == 0 else mem.hn[:, t, :]
                if n == 1:
                    dve.wait_ge(a.first_norm.sem, a.first_norm.at(b, t + 1))
                dve.bn_stats(mem.stats[:, t, :], src).then_inc(a.stat[n].sem, 1)
            for t in range(T):
                wait_alone(dve, a.stat[n].sem, a.stat[n].at(b, t + 1), a.passed["dve"])
                dve.bn_aggr(mem.mv[:, t, :], mem.stats[:, t, :]).then_inc(a.aggr[n].sem, 1)
            wait_alone(dve, a.rs[n].sem, a.rs[n].at(b, 1), a.passed["dve"])
            last = n == a.norms - 1
            if not last:
                dve.tensor_copy(mem.mv_in[:, b, :, :], mem.mv[:, :, :])
                dve.tensor_copy(mem.rstd_in[:, b, :], mem.rstd[:, :])
            for t in range(T):
                if n == 0 and t == 0:
                    dve.wait_ge(a.hT_ps.sem, a.hT_ps.at(b))
                src = mem.x[:, b, t, :] if n == 0 else mem.hn[:, t, :]
                out = dve.tensor_scalar(mem.hn[:, t, :], src, mem.mv[:, t, 0:1], mem.rstd[:, t:t + 1],
                                        ALU.subtract, ALU.mult)
                sig = a.hn_ready if last else a.first_norm
                out.then_inc(sig.sem, 1)
        if a.masked:
            dve.wait_ge(a.mask_loaded.sem, a.mask_loaded.at(b, 16))
            dve.tensor_scalar(mem.mb_all[:, b, :, :], mem.mint[:, :, :], 0.0, MASKED, ALU.is_equal,
                              ALU.mult).then_inc(a.mask_bias.sem, 1)
        for n in range(2 * C):
            bias = mem.cols[:, a.cols["qk"] + n:a.cols["qk"] + n + 1]
            dve.wait_ge(a.hi.sem, a.hi.at(b, n + 1))
            if n >= 2:
                dve.wait_ge(a.lo.sem, a.lo.at(b, n - 1))
            dve.scalar_tensor_tensor(mem.res[n % 2], ps[:, 2 + n, :], bias, mem.parts[n][:, 0, :],
                                     ALU.add, ALU.subtract).then_inc(a.r1.sem, 1)
            dve.wait_ge(a.midp.sem, a.midp.at(b, n + 1))
            dve.tensor_tensor(mem.parts[n][:, 2, :], mem.res[n % 2], mem.parts[n][:, 1, :],
                              ALU.subtract).then_inc(a.lo.sem, 1)
        for k in range(2):
            dve.wait_ge(a.v_ps.sem, a.v_ps.at(b, k + 1))
            for t in range(2):
                out = mem.v[:, b, :, 2 * k + t, :]
                got = ps[:, 6 + k, t * D:(t + 1) * D].rearrange("p (g d) -> p g d", g=NG)
                if a.rows is None:
                    ins = dve.tensor_copy(out, got)
                else:
                    row = mem.rows[:, a.rows, :].rearrange("p (g d) -> p g d", g=NG)
                    ins = dve.tensor_tensor(out, got, row, ALU.add)
            ins.then_inc(a.v_ready.sem, 1)


def project_gpsimd(pool, a):
    mem = a.mem
    with pool.Fori(0, B) as b:
        if a.cross:
            pool.wait_ge(a.cT_ps.sem, a.cT_ps.at(b))
            pool.dma_start(mem.cin[:, :, :], a.dram["ctx"][b]).then_inc(a.c_loaded.sem, 16)
        if a.masked:
            pool.wait_ge(a.mask_bias.sem, a.mask_bias.at(b))
            pool.dma_start(mem.mint[:, :, :], a.dram["mask"][b]).then_inc(a.mask_loaded.sem, 16)
        for n in range(a.norms):
            wait_alone(pool, a.aggr[n].sem, a.aggr[n].at(b, T), a.passed["pool"])
            pool.tensor_scalar(mem.var[:, :], mem.mv[:, :, 1], EPS, None, ALU.add).then_inc(a.vare[n].sem, 1)
            pool.wait_ge(a.vare[n].sem, a.vare[n].at(b, 1))
            pool.tensor_tensor(mem.rstd[:, :], mem.var[:, :], mem.neghalf[:, :], ALU.pow).then_inc(a.rs[n].sem, 1)
        for n in range(2 * C):
            wait_alone(pool, a.r1.sem, a.r1.at(b, n + 1), a.passed["pool"])
            pool.tensor_copy(mem.parts[n][:, 1, :], mem.res[n % 2]).then_inc(a.midp.sem, 1)


def project_scalar(act, a):
    mem = a.mem
    ps = mem.ps
    act.sem_inc(a.hT_ready.sem, a.hT_ready.lead)
    act.sem_inc(a.cT_ready.sem, a.cT_ready.lead)
    with act.Fori(0, B) as b:
        for c in range(C):
            act.wait_ge(a.hT_ps.sem, a.hT_ps.at(b, c + 1))
            if c == 0:
                act.wait_ge(a.qk_ps.sem, a.qk_ps.at(b))
            if a.affine is None:
                ins = act.activation(mem.hT[:, c, :], ps[:, c, :], ACT.Copy)
            else:
                g, s = a.affine + c, a.affine + C + c
                ins = act.activation(mem.hT[:, c, :], ps[:, c, :], ACT.Identity, bias=mem.cols[:, s:s + 1],
                                     scale=mem.cols[:, g:g + 1])
            ins.then_inc(a.hT_ready.sem, 1)
        if a.cross:
            for c in range(C):
                act.wait_ge(a.cT_ps.sem, a.cT_ps.at(b, c + 1))
                act.activation(mem.cT[:, c, :], ps[:, 6 + c, :], ACT.Copy).then_inc(a.cT_ready.sem, 1)
        for n in range(2 * C):
            act.wait_ge(a.qk_ps.sem, a.qk_ps.at(b, n + 1))
            if n == 0:
                act.wait_ge(a.stored.sem, a.stored.at(b))
            bias = mem.cols[:, a.cols["qk"] + n:a.cols["qk"] + n + 1]
            act.activation(mem.parts[n][:, 0, :], ps[:, 2 + n, :], ACT.Identity, bias=bias).then_inc(a.hi.sem, 1)


def project_tensor(pe, a):
    mem = a.mem
    ps = mem.ps
    pe.sem_inc(a.hT_ps.sem, a.hT_ps.lead)
    pe.sem_inc(a.cT_ps.sem, a.cT_ps.lead)
    pe.sem_inc(a.qk_ps.sem, a.qk_ps.lead)
    kv = mem.cT if a.cross else mem.hT
    with pe.Fori(0, B) as b:
        pe.wait_ge(a.hT_ready.sem, a.hT_ready.at(b))
        pe.wait_ge(a.hn_ready.sem, a.hn_ready.at(b, T))
        for c in range(C):
            for t in range(T):
                ins = pe.transpose(ps[:, c, t * P:(t + 1) * P], mem.hn[:, t, c * P:(c + 1) * P], mem.ident[:, :])
            ins.then_inc(a.hT_ps.sem, 1)
        pe.wait_ge(a.v_ready.sem, a.v_ready.at(b))
        if a.cross:
            pe.wait_ge(a.c_loaded.sem, a.c_loaded.at(b, 16))
            for c in range(C):
                for t in range(T):
                    ins = pe.transpose(ps[:, 6 + c, t * P:(t + 1) * P], mem.cin[:, t, c * P:(c + 1) * P],
                                       mem.ident[:, :])
                ins.then_inc(a.cT_ps.sem, 1)
        pe.wait_ge(a.hT_ready.sem, a.hT_ready.at(b, C))
        pe.wait_ge(a.lo.sem, a.lo.at(b))

        def qk(n, src):
            for c in range(C):
                ins = pe.matmul(ps[:, 2 + n, :], a.w[:, n // C, c, (n % C) * P:(n % C + 1) * P], src[:, c, :],
                                start=(c == 0), stop=(c == C - 1))
            return ins

        def values():
            for k in range(2):
                for t in range(2):
                    for c in range(C):
                        ins = pe.matmul(ps[:, 6 + k, t * D:(t + 1) * D],
                                        kv[:, c, (2 * k + t) * P:(2 * k + t + 1) * P], a.w[:, 2, c, :],
                                        start=(c == 0), stop=(c == C - 1))
                ins.then_inc(a.v_ps.sem, 1)

        if a.cross:
            for n in range(C):
                qk(n, mem.hT).then_inc(a.qk_ps.sem, 1)
            pe.wait_ge(a.cT_ready.sem, a.cT_ready.at(b, C))
            for n in range(C, 2 * C):
                qk(n, kv).then_inc(a.qk_ps.sem, 1)
            values()
        else:
            values()
            for n in range(2 * C):
                qk(n, kv).then_inc(a.qk_ps.sem, 1)


def project_sync(sp, a):
    mem = a.mem
    sp.sem_inc(a.stored.sem, a.stored.lead)
    with sp.Fori(0, B) as b:
        for n in range(2 * C):
            half = slice((n % C) * P, (n % C + 1) * P)
            out = a.dram["q" if n < C else "k"][b, half, :, :]
            sp.wait_ge(a.lo.sem, a.lo.at(b, n + 1))
            runs = ((0, 3), (3, 5), (5, 6))
            for i, (r0, r1) in enumerate(runs):
                if n < C:
                    src = mem.parts[n][:, 0:r1 - r0, :]
                else:
                    src = mem.parts[n][:, i:i + 1, :].to_broadcast([P, r1 - r0, S])
                sp.dma_start(out[:, r0:r1, :], src).then_inc(a.stored.sem, 16)
    sp.wait_ge(a.stored.sem, a.stored.at(B))



ST = (0, 2)
SB = (4, 5)
OB = 6
MISC = 7
U = 8


def attend_sync(sp, a):
    mem = a.mem

    def load(b, g):
        for dst, src in ((mem.qst[g], a.dram["q"]), (mem.kst[g], a.dram["k"])):
            rows = src[b, g * GW:(g + 1) * GW, :, :].rearrange("(h r) t n -> (r t) h n", h=HG)
            sp.dma_start(dst[0:ROWS, :, :], rows).then_inc(a.stacks[g].sem, 16)

    def shift(b, g):
        G = NG * b + g
        sp.wait_ge(a.m_sb.sem, a.m_sb.at(G, 1))
        sp.dma_start(mem.qst[g][ROWS:KROWS, :, :], mem.mT[:, :]).then_inc(a.shift[g].sem, 16)

    def body(b, first, last):
        for g in range(NG):
            G = NG * b + g
            ahead = (b, g + 2) if g < 2 else (b + 1, g - 2)
            if not (last and g >= 2):
                if not (first and g < 2):
                    sp.wait_ge(a.st_ps.sem, a.st_ps.at(G - 1))
                load(*ahead)
            if a.self_block and g == 2 and not first:
                store(b - 1)
            if not (last and g == NG - 1):
                shift(*((b, g + 1) if g < NG - 1 else (b + 1, 0)))

    def store(b):
        for k in range(2):
            sp.wait_ge(a.acc_ready.sem, a.acc_ready.at(b, k + 1))
            sp.dma_start(a.dram["acc"][b, :, 2 * k:2 * k + 2, :], mem.hn[:, 2 * k:2 * k + 2, :])\
              .then_inc(a.acc_stored.sem, 16)

    if a.self_block:
        sp.sem_inc(a.acc_stored.sem, a.acc_stored.lead)
    load(0, 0)
    load(0, 1)
    shift(0, 0)
    body(0, True, False)
    with sp.Fori(1, B - 1) as b:
        body(b, False, False)
    body(B - 1, False, True)
    if a.self_block:
        store(B - 1)
        sp.wait_ge(a.acc_stored.sem, a.acc_stored.at(B))


def attend_gpsimd(pool, a):
    mem = a.mem

    def gather(b, g):
        G = NG * b + g
        if not (type(b) is int and G < 2):
            wait_alone(pool, a.pv.sem, a.pv.at(G - 1), a.passed["pool"])
        pool.tensor_copy(mem.vg[g % 2][:, :, :, 0:DK],
                         mem.v[:, b, g, :, :].rearrange("p t (h d) -> p t h d", h=HG)).then_inc(a.vg_ready.sem, 1)

    for g in range(2):
        pool.memset(mem.vg[g][:, :, :, DK:DK + 1], 1.0).then_inc(a.preset.sem, 1)
    pool.wait_ge(a.preset.sem, 2)
    for g in range(NG):
        gather(0, g)
    with pool.Fori(1, B) as b:
        for g in range(NG):
            gather(b, g)


def attend_scalar(act, a):
    mem = a.mem
    ps = mem.ps

    def exps(G, u):
        act.wait_ge(a.st_ps.sem, a.st_ps.at(G, u + 1))
        act.wait_ge(a.pv.sem, a.pv.at(G - 1, u // 2 + 1))
        bank = ST[u % 2]
        act.activation(mem.probs[:, u // 2, 2 * (u % 2):2 * (u % 2) + 2, :], ps[:, bank:bank + 2, :], ACT.Exp,
                       scale=SCALE).then_inc(a.p_exp.sem, 1)

    def out_copy(G):
        act.wait_ge(a.pv.sem, a.pv.at(G, T))
        act.wait_ge(a.ot_ps.sem, a.ot_ps.at(G))
        act.activation(mem.ot, ps[:, OB, :], ACT.Copy).then_inc(a.ot_sb.sem, 1)

    def maxima(G, before=None):
        act.wait_ge(a.m_ps.sem, a.m_ps.at(G, 1))
        if before is not None:
            b, g = before
            act.wait_ge(a.shift[g].sem, a.shift[g].at(b, 16))
        act.activation(mem.mT[:, :], ps[0:PARTS * HG, MISC, 0:S // 2].bitcast(BF16), ACT.Copy)\
           .then_inc(a.m_sb.sem, 1)

    def oT_copy(b, c):
        act.wait_ge(a.oT_ps.sem, a.oT_ps.at(b, c + 1))
        act.activation(mem.oT[:, c, :], ps[:, MISC, :], ACT.Copy).then_inc(a.oT_sb.sem, 1)

    def body(b, first, last):
        for g in range(NG):
            G = NG * b + g
            for u in range(U):
                exps(G, u)
                if u == 0 and g == 1 and not first:
                    oT_copy(b - 1, 0)
                if u == 2 and not (first and g == 0):
                    out_copy(G - 1)
                if u == 2 and not (last and g == NG - 1):
                    maxima(G + 1, (b, g))
                if u == 3 and g == 1 and not first:
                    oT_copy(b - 1, 1)

    act.sem_inc(a.p_exp.sem, a.p_exp.lead)
    act.sem_inc(a.ot_sb.sem, a.ot_sb.lead)
    maxima(0)
    body(0, True, False)
    with act.Fori(1, B - 1) as b:
        body(b, False, False)
    body(B - 1, False, True)
    out_copy(B * NG - 1)
    oT_copy(B - 1, 0)
    oT_copy(B - 1, 1)


def attend_tensor(pe, a):
    mem = a.mem
    ps = mem.ps
    misc = [None]

    def take_misc():
        if misc[0] is not None:
            pe.wait_ge(*misc[0])

    def scores(G, g, v):
        h, t = v // T, v % T
        pe.wait_ge(a.s_max.sem, a.s_max.at(G, v - 1))
        pe.matmul(ps[:, SB[v % 2], :], mem.qst[g][0:ROWS, h, t * P:(t + 1) * P], mem.kst[g][0:ROWS, h, :],
                  start=True, stop=True).then_inc(a.s_ps.sem, 1)

    def transposed_scores(G, g, b, u):
        kt, pair = u // 2, u % 2
        pe.wait_ge(a.p_exp.sem, a.p_exp.at(G, u - 1))
        if u == 0:
            pe.wait_ge(a.shift[g].sem, a.shift[g].at(b, 16))
            if a.masked and g == 0:
                pe.wait_ge(a.mbT_ready.sem, a.mbT_ready.at(b, 1))
        for j in range(2):
            h = 2 * pair + j
            out = ps[:, ST[pair] + j, :]
            ins = pe.matmul(out, mem.kst[g][0:KROWS, h, kt * P:(kt + 1) * P], mem.qst[g][0:KROWS, h, :],
                            start=True, stop=not a.masked)
            if a.masked:
                for t in range(T):
                    ins = pe.matmul(out[:, t * P:(t + 1) * P], mem.mbT[:, t, kt * P:(kt + 1) * P], mem.identb[:, :],
                                    start=False, stop=(t == T - 1))
        ins.then_inc(a.st_ps.sem, 1)

    def products(G, g, kt):
        pe.wait_ge(a.p_exp.sem, a.p_exp.at(G, 2 * kt + 2))
        if kt == 0:
            pe.wait_ge(a.vg_ready.sem, a.vg_ready.at(G, 1))
            pe.wait_ge(a.ot_sb.sem, a.ot_sb.at(G))
        for h in range(HG):
            ins = pe.matmul(ps[h * VW:(h + 1) * VW, OB, :], mem.vg[g % 2][:, kt, h, :], mem.probs[:, kt, h, :],
                            start=(kt == 0), stop=(kt == T - 1))
        ins.then_inc(a.pv.sem, 1)

    def maxima(G):
        pe.wait_ge(a.m_lo.sem, a.m_lo.at(G, 1))
        take_misc()
        for t in range(T):
            ins = pe.transpose(ps[0:PARTS * HG, MISC, t * P // 2:(t + 1) * P // 2].bitcast(BF16),
                               mem.mparts[:, t, :, :].rearrange("p a h -> p (a h)"), mem.identb[:, :])
        ins.then_inc(a.m_ps.sem, 1)
        misc[0] = (a.m_sb.sem, a.m_sb.at(G, 1))

    def turn(G):
        pe.wait_ge(a.ot_sb.sem, a.ot_sb.at(G, 1))
        take_misc()
        for t in range(T):
            ins = pe.transpose(ps[:, MISC, t * P:(t + 1) * P], mem.ot[:, t * P:(t + 1) * P], mem.ident[:, :])
        ins.then_inc(a.ot_ps.sem, 1)
        misc[0] = (a.o_ready.sem, a.o_ready.at(G, 1))

    def turn_out(b, c):
        pe.wait_ge(a.o_ready.sem, a.o_ready.at(NG * b + NG - 1, 1))
        take_misc()
        for t in range(T):
            ins = pe.transpose(ps[:, MISC, t * P:(t + 1) * P], mem.o[:, t, c * P:(c + 1) * P], mem.ident[:, :])
        ins.then_inc(a.oT_ps.sem, 1)
        misc[0] = (a.oT_sb.sem, a.oT_sb.at(b, c + 1))

    def project_out(b, k):
        pe.wait_ge(a.oT_sb.sem, a.oT_sb.at(b, C))
        take_misc()
        for t in range(2):
            for c in range(C):
                ins = pe.matmul(ps[:, MISC, t * D:(t + 1) * D], mem.oT[:, c, (2 * k + t) * P:(2 * k + t + 1) * P],
                                a.w[:, 3, c, :], start=(c == 0), stop=(c == C - 1))
        ins.then_inc(a.op_ps.sem, 1)
        misc[0] = (a.op_used.sem, a.op_used.at(b, k + 1))

    def body(b, first, last):
        if not first:
            misc[0] = (a.o_ready.sem, a.o_ready.at(NG * b - 2, 1))
        for g in range(NG):
            G = NG * b + g
            for u in range(U):
                transposed_scores(G, g, b, u)
                if not (last and g >= 2):
                    if u == 0:
                        s = (g + 2) % NG
                        pe.wait_ge(a.stacks[s].sem, a.stacks[s].at(b if g < 2 else b + 1, 32))
                    for v in (2 * u, 2 * u + 1):
                        scores(G + 2, (g + 2) % NG, v)
                if u == 1 and not (first and g == 0):
                    products(G - 1, (g - 1) % NG, T - 1)
                if u >= 3 and u % 2:
                    products(G, g, (u - 3) // 2)
                if g == 1 and not first and u == 0:
                    turn_out(b - 1, 0)
                if u == 2 and not (last and g == NG - 1):
                    maxima(G + 1)
                if g == 1 and not first and u == 3:
                    turn_out(b - 1, 1)
                if u == 5 and not (first and g == 0):
                    turn(G - 1)
                if g == 1 and not first and u >= 6:
                    project_out(b - 1, u - 6)

    pe.sem_inc(a.pv.sem, a.pv.lead)
    pe.sem_inc(a.ot_ps.sem, a.ot_ps.lead)
    for G in range(2):
        pe.wait_ge(a.stacks[G].sem, a.stacks[G].at(0, 32))
        for v in range(HG * T):
            scores(G, G, v)
    maxima(0)
    body(0, True, False)
    with pe.Fori(1, B - 1) as b:
        body(b, False, False)
    body(B - 1, False, True)
    G = B * NG - 1
    products(G, NG - 1, T - 1)
    turn(G)
    for c in range(C):
        turn_out(B - 1, c)
    for k in range(2):
        project_out(B - 1, k)


def attend_vector(dve, a):
    mem = a.mem
    ps = mem.ps

    def top(G, v):
        h, t = v // T, v % T
        wait_alone(dve, a.s_ps.sem, a.s_ps.at(G, v + 1), a.passed["dve"])
        out = mem.m[:, 0, t, h:h + 1]
        if a.masked:
            ins = dve.tensor_tensor_reduce(mem.junk[v % 2], ps[:, SB[v % 2], :], mem.mbS[:, t, :], 1.0, FLOOR, ALU.add,
                                           ALU.max, out)
        else:
            ins = dve.tensor_reduce(out, ps[:, SB[v % 2], :], AX.X, ALU.max)
        ins.then_inc(a.s_max.sem, 1)

    def split(G):
        dve.wait_ge(a.s_max.sem, a.s_max.at(G, HG * T))
        if not (type(G) is int and G < 1):
            dve.wait_ge(a.m_ps.sem, a.m_ps.at(G))
        m = mem.m[:, 0, :, :]
        hi, mid, lo = (mem.mparts[:, :, i, :] for i in range(PARTS))
        dve.tensor_scalar(hi, m, -1.0, None, ALU.mult).then_inc(a.m_hi.sem, 1)
        dve.wait_ge(a.m_hi.sem, a.m_hi.at(G, 1))
        dve.scalar_tensor_tensor(mem.mres[:, :, :], m, -1.0, hi, ALU.mult, ALU.subtract).then_inc(a.m_res.sem, 1)
        dve.wait_ge(a.m_res.sem, a.m_res.at(G, 1))
        dve.tensor_copy(mid, mem.mres[:, :, :]).then_inc(a.m_mid.sem, 1)
        dve.wait_ge(a.m_mid.sem, a.m_mid.at(G, 1))
        dve.tensor_tensor(lo, mem.mres[:, :, :], mid, ALU.subtract).then_inc(a.m_lo.sem, 1)

    def normalise(G, b, g, first):
        dve.wait_ge(a.ot_ps.sem, a.ot_ps.at(G, 1))
        if g == 0 and not first:
            dve.wait_ge(a.oT_ps.sem, a.oT_ps.at(b - 1, C))
        got = ps[:, MISC, :].rearrange("p (t h d) -> p t h d", t=T, h=HG)
        dve.tensor_scalar(mem.den[:, :, :], got[:, :, :, DK], 1e-30, None, ALU.max).then_inc(a.den.sem, 1)
        dve.wait_ge(a.den.sem, a.den.at(G, 1))
        dve.reciprocal(mem.rden[:, :, :], mem.den[:, :, :]).then_inc(a.rden.sem, 1)
        dve.wait_ge(a.rden.sem, a.rden.at(G, 1))
        out = mem.o[:, :, g * GW:(g + 1) * GW].rearrange("p t (h d) -> p t h d", h=HG)
        dve.tensor_tensor(out, got[:, :, :, 0:DK], mem.rden[:, :, :].unsqueeze(3).to_broadcast([P, T, HG, DK]),
                          ALU.mult).then_inc(a.o_ready.sem, 1)

    def residual(b, k):
        two = slice(2 * k, 2 * k + 2)
        x = mem.x[:, b, two, :]
        got = ps[:, MISC, :].rearrange("p (t d) -> p t d", t=2)
        row = None if a.rows is None else mem.rows[:, a.rows + 1:a.rows + 2, :].to_broadcast([P, 2, D])
        if not a.self_block:
            dve.wait_ge(a.op_ps.sem, a.op_ps.at(b, k + 1))
            ins = dve.tensor_tensor(x, got, x, ALU.add)
            ins.then_inc(a.op_used.sem, 1)
            if row is not None:
                dve.wait_ge(a.op_used.sem, a.op_used.at(b, k + 1))
                dve.tensor_tensor(x, x, row, ALU.add)
            return
        y, u = mem.hn[:, two, :], mem.cin[:, two, :]
        for t in range(2 * k, 2 * k + 2):
            ins = dve.tensor_scalar(mem.cin[:, t, :], mem.x[:, b, t, :], mem.mv_in[:, b, t, 0:1],
                                    mem.rstd_in[:, b, t:t + 1], ALU.subtract, ALU.mult)
        ins.then_inc(a.step[0].sem, 1)
        dve.wait_ge(a.step[0].sem, a.step[0].at(b, k + 1))
        dve.tensor_tensor(u, u, row, ALU.add).then_inc(a.step[1].sem, 1)
        dve.wait_ge(a.step[1].sem, a.step[1].at(b, k + 1))
        dve.wait_ge(a.op_ps.sem, a.op_ps.at(b, k + 1))
        dve.tensor_tensor(u, got, u, ALU.add).then_inc(a.op_used.sem, 1)
        dve.wait_ge(a.op_used.sem, a.op_used.at(b, k + 1))
        dve.wait_ge(a.acc_stored.sem, a.acc_stored.at(b))
        dve.tensor_tensor(y, x, u, ALU.add).then_inc(a.acc_ready.sem, 1)
        wait_alone(dve, a.acc_ready.sem, a.acc_ready.at(b, k + 1), a.passed["dve"])
        dve.tensor_copy(x, u).then_inc(a.step[2].sem, 1)

    def mask_of(b, which):
        if which == "S":
            dve.tensor_copy(mem.mbS[:, :, :], mem.mb_all[:, b, :, :]).then_inc(a.mbS_ready.sem, 1)
            dve.wait_ge(a.mbS_ready.sem, a.mbS_ready.at(b, 1))
        else:
            if type(b) is not int or b:
                wait_alone(dve, a.st_ps.sem, a.st_ps.at(NG * b), a.passed["dve"])
            dve.tensor_copy(mem.mbT[:, :, :], mem.mb_all[:, b, :, :]).then_inc(a.mbT_ready.sem, 1)

    def body(b, first, last):
        for g in range(NG):
            G = NG * b + g
            if a.masked and g == 0 and not first:
                mask_of(b, "T")
            if a.masked and g == 2 and not last:
                mask_of(b + 1, "S")
            for u in range(U):
                if not (last and g >= 2):
                    top(G + 2, 2 * u)
                    top(G + 2, 2 * u + 1)
                if u == 0 and g == 2 and not first:
                    residual(b - 1, 1)
                if u == 6 and not (first and g == 0):
                    normalise(G - 1, b if g else b - 1, (g - 1) % NG, first)
                if u == 7 and g == 1 and not first:
                    residual(b - 1, 0)
            if not (last and g >= 2):
                split(G + 2)

    dve.sem_inc(a.s_max.sem, a.s_max.lead)
    if a.masked:
        mask_of(0, "S")
        mask_of(0, "T")
    for G in range(2):
        for v in range(HG * T):
            top(G, v)
        split(G)
    body(0, True, False)
    with dve.Fori(1, B - 1) as b:
        body(b, False, False)
    body(B - 1, False, True)
    normalise(B * NG - 1, B - 1, NG - 1, False)
    residual(B - 1, 0)
    residual(B - 1, 1)




class Mixture:

    def __init__(self, nc, ctx, stage, mem, dram, name, affine, gate_width, row, hidden):
        self.mem, self.dram, self.name, self.affine = mem, dram, name, affine
        self.width, self.row, self.hidden = gate_width, row, hidden

        self.used = []

        def sig(what, per, lead=0, kept=stage):
            self.used.append(kept.enter_context(nc.semaphore(f"{name}_{what}")))
            return Signal(self.used[-1], per, lead)

        self.passed = {eng: stage.enter_context(nc.semaphore(f"{name}_{eng}_passed")) for eng in ("dve", "pool")}
        self.stat = sig("stat", T)
        self.aggr = sig("aggr", T)
        self.vare = sig("vare", 1)
        self.rs = sig("rs", 1)
        self.rn_ready = sig("rn_ready", T)
        self.rn_stored = sig("rn_stored", 16, 16)
        self.rnT_ps = sig("rnT_ps", C, C)
        self.rnT_ready = sig("rnT_ready", C, C)
        self.g_ps = sig("g_ps", 2, 2)
        self.logit = sig("logit", 2, 2)
        self.top = sig("top", T)
        self.index = sig("index", T)
        self.chosen = sig("chosen", 1)
        self.ntop = sig("ntop", 1)
        self.exps = sig("exps", T, T)
        self.prob = sig("prob", 1)
        self.route = sig("route", 1)
        self.onehot = sig("onehot", 1)
        self.counts = sig("counts", 1)
        self.routed = sig("routed", 1)
        self.cleared = sig("cleared", 16)
        self.scattered = sig("scattered", 16, kept=ctx)
        self.inv_loaded = sig("inv_loaded", 16)
        self.weights = sig("weights", 16)
        self.gathered = [sig(f"gathered{j}", 16, kept=ctx) for j in range(2)]
        self.tx_ps = sig("tx_ps", 1, 2)
        self.xT_ready = sig("xT_ready", 1, 1)
        self.h_ps = sig("h_ps", 2)
        self.mid_ready = sig("mid_ready", 2, 2)
        self.tm_ps = sig("tm_ps", 2, 2)
        self.midT_ready = sig("midT_ready", 2, 2)
        self.y_ps = sig("y_ps", 1, 1)
        self.y_sum = sig("y_sum", 1, 1)
        self.y_ready = sig("y_ready", 1)
        self.y_stored = [sig(f"y_stored{j}", 16, 16) for j in range(2)]
        self.fetched = sig("fetched", 16, kept=ctx)
        self.acc_loaded = sig("acc_loaded", 16)
        self.x_ready = sig("x_ready", 1)
        self.out_stored = sig("out_stored", 16)


def gate_vector(dve, m):
    mem = m.mem
    ps = mem.ps
    dve.sem_inc(m.logit.sem, m.logit.lead)
    with dve.Fori(0, B) as b:
        for t in range(T):
            dve.bn_stats(mem.stats[:, t, :], mem.x[:, b, t, :]).then_inc(m.stat.sem, 1)
        for t in range(T):
            wait_alone(dve, m.stat.sem, m.stat.at(b, t + 1), m.passed["dve"])
            dve.bn_aggr(mem.mv[:, t, :], mem.stats[:, t, :]).then_inc(m.aggr.sem, 1)
        dve.wait_ge(m.rs.sem, m.rs.at(b, 1))
        dve.wait_ge(m.rnT_ps.sem, m.rnT_ps.at(b))
        dve.wait_ge(m.rn_stored.sem, m.rn_stored.at(b))
        for t in range(T):
            dve.tensor_scalar(mem.rn[:, t, :], mem.x[:, b, t, :], mem.mv[:, t, 0:1], mem.rstd[:, t:t + 1],
                              ALU.subtract, ALU.mult).then_inc(m.rn_ready.sem, 1)
        if m.hidden is None:
            dve.wait_ge(m.exps.sem, m.exps.at(b))
        for k in range(2):
            dve.wait_ge(m.g_ps.sem, m.g_ps.at(b, k + 1))
            got = ps[:, 2 + k, 0:2 * m.width].rearrange("p (t d) -> p t d", t=2)
            row = mem.rows[:, m.row:m.row + 1, 0:m.width].to_broadcast([P, 2, m.width])
            dve.tensor_tensor(mem.logits[:, 2 * k:2 * k + 2, 0:m.width], got, row, ALU.add).then_inc(m.logit.sem, 1)
        for t in range(T):
            wait_alone(dve, m.logit.sem, m.logit.at(b, t // 2 + 1), m.passed["dve"])
            dve.max(mem.top8[:, t, :], mem.logits[:, t, 0:m.width]).then_inc(m.top.sem, 1)
        for t in range(T):
            wait_alone(dve, m.top.sem, m.top.at(b, t + 1), m.passed["dve"])
            dve.max_index(mem.idx8[:, t, :], mem.top8[:, t, :], mem.logits[:, t, 0:m.width]).then_inc(m.index.sem, 1)
        dve.wait_ge(m.index.sem, m.index.at(b, T))
        dve.tensor_scalar(mem.expert_u[:, :], mem.idx8[:, :, 0], E - 1, None, ALU.bitwise_and).then_inc(m.chosen.sem, 1)
        wait_alone(dve, m.chosen.sem, m.chosen.at(b, 1), m.passed["dve"])
        dve.tensor_copy(mem.expert[:, b, :], mem.expert_u[:, :])
        if m.hidden is None:
            dve.tensor_scalar(mem.ntop[:, :], mem.top8[:, :, 0], -1.0, None, ALU.mult).then_inc(m.ntop.sem, 1)
            dve.wait_ge(m.exps.sem, m.exps.at(b, T))
            dve.reciprocal(mem.prob[:, b, :], mem.sum[:, :]).then_inc(m.prob.sem, 1)


def gate_gpsimd(pool, m):
    mem = m.mem
    with pool.Fori(0, B) as b:
        wait_alone(pool, m.aggr.sem, m.aggr.at(b, T), m.passed["pool"])
        pool.tensor_scalar(mem.var[:, :], mem.mv[:, :, 1], EPS, None, ALU.add).then_inc(m.vare.sem, 1)
        pool.wait_ge(m.vare.sem, m.vare.at(b, 1))
        pool.tensor_tensor(mem.rstd[:, :], mem.var[:, :], mem.neghalf[:, :], ALU.pow).then_inc(m.rs.sem, 1)


def gate_scalar(act, m):
    mem = m.mem
    ps = mem.ps
    act.sem_inc(m.rnT_ready.sem, m.rnT_ready.lead)
    act.sem_inc(m.exps.sem, m.exps.lead)
    with act.Fori(0, B) as b:
        for c in range(C):
            act.wait_ge(m.rnT_ps.sem, m.rnT_ps.at(b, c + 1))
            act.wait_ge(m.g_ps.sem, m.g_ps.at(b))
            if m.affine is None:
                ins = act.activation(mem.rnT[:, c, :], ps[:, c, :], ACT.Copy)
            else:
                g, s = m.affine + c, m.affine + C + c
                ins = act.activation(mem.rnT[:, c, :], ps[:, c, :], ACT.Identity, bias=mem.cols[:, s:s + 1],
                                     scale=mem.cols[:, g:g + 1])
            ins.then_inc(m.rnT_ready.sem, 1)
        if m.hidden is None:
            act.wait_ge(m.ntop.sem, m.ntop.at(b, 1))
            for t in range(T):
                act.activation(mem.exps[:, t, :], mem.logits[:, t, :], ACT.Exp, bias=mem.ntop[:, t:t + 1],
                               accum_out=mem.sum[:, t:t + 1]).then_inc(m.exps.sem, 1)


def gate_tensor(pe, m):
    mem = m.mem
    ps = mem.ps
    pe.sem_inc(m.rnT_ps.sem, m.rnT_ps.lead)
    pe.sem_inc(m.g_ps.sem, m.g_ps.lead)
    with pe.Fori(0, B) as b:
        pe.wait_ge(m.rnT_ready.sem, m.rnT_ready.at(b))
        pe.wait_ge(m.rn_ready.sem, m.rn_ready.at(b, T))
        for c in range(C):
            for t in range(T):
                ins = pe.transpose(ps[:, c, t * P:(t + 1) * P], mem.rn[:, t, c * P:(c + 1) * P], mem.ident[:, :])
            ins.then_inc(m.rnT_ps.sem, 1)
        pe.wait_ge(m.rnT_ready.sem, m.rnT_ready.at(b, C))
        pe.wait_ge(m.logit.sem, m.logit.at(b))
        for k in range(2):
            for t in range(2):
                for c in range(C):
                    ins = pe.matmul(ps[:, 2 + k, t * m.width:(t + 1) * m.width],
                                    mem.rnT[:, c, (2 * k + t) * P:(2 * k + t + 1) * P], mem.gate[:, c, 0:m.width],
                                    start=(c == 0), stop=(c == C - 1))
            ins.then_inc(m.g_ps.sem, 1)


def gate_sync(sp, m):
    mem = m.mem
    sp.sem_inc(m.rn_stored.sem, m.rn_stored.lead)
    with sp.Fori(0, B) as b:
        sp.wait_ge(m.rn_ready.sem, m.rn_ready.at(b, T))
        sp.dma_start(m.dram["rows"].rearrange("(b t p) d -> b p t d", b=B, t=T)[b], mem.rn[:, :, :])\
          .then_inc(m.rn_stored.sem, 16)
    sp.wait_ge(m.rn_stored.sem, m.rn_stored.at(B))


def route_vector(dve, m):
    mem = m.mem
    ps = mem.ps
    done = [0]

    def then(ins):
        done[0] += 1
        ins.then_inc(m.route.sem, 1)
        dve.wait_ge(m.route.sem, done[0])

    expert = mem.expert[:, :, :].rearrange("p b t -> p (b t)")
    dve.tensor_tensor(mem.onehot[:, :, :], expert.unsqueeze(2).to_broadcast([P, NT, E]),
                      mem.count[:, 0:E].unsqueeze(1).to_broadcast([P, NT, E]), ALU.is_equal).then_inc(m.onehot.sem, 1)
    dve.wait_ge(m.counts.sem, 1)
    then(dve.tensor_copy(mem.tiles[:, :, :], ps[:, 1, 0:NT * E].rearrange("p (t e) -> p t e", t=NT)))
    then(dve.memset(mem.place[:, 0, :], 0.0))
    for t in range(1, NT):
        then(dve.tensor_tensor(mem.place[:, t, :], mem.place[:, t - 1, :], mem.tiles[:, t - 1, :], ALU.add))
    then(dve.tensor_tensor(mem.total[:, :], mem.place[:, NT - 1, :], mem.tiles[:, NT - 1, :], ALU.add))
    under = mem.tiles[:, :, :].rearrange("p t e -> p (t e)").rearrange("p (e t) -> p e t", e=E)
    then(dve.tensor_scalar(mem.total[:, :], mem.total[:, :], 1.0 / P, None, ALU.mult))
    then(dve.tensor_tensor(under, mem.total[:, :].unsqueeze(2).to_broadcast([P, E, NT]),
                           mem.count[:, 0:NT].unsqueeze(1).to_broadcast([P, E, NT]), ALU.is_gt))
    then(dve.tensor_reduce(mem.need[:, :], under, AX.X, ALU.add))
    then(dve.tensor_copy(mem.end[:, 0:1], mem.need[:, 0:1]))
    for e in range(1, E):
        then(dve.tensor_tensor(mem.end[:, e:e + 1], mem.end[:, e - 1:e], mem.need[:, e:e + 1], ALU.add))
    then(dve.tensor_tensor(mem.start[:, :], mem.end[:, :], mem.need[:, :], ALU.subtract))
    then(dve.tensor_scalar(mem.start[:, :], mem.start[:, :], float(P), None, ALU.mult))
    then(dve.tensor_tensor(mem.place[:, :, :], mem.place[:, :, :],
                           mem.start[:, :].unsqueeze(1).to_broadcast([P, NT, E]), ALU.add))
    then(dve.tensor_tensor(mem.place[:, :, :], ps[:, 0, 0:NT * E].rearrange("p (t e) -> p t e", t=NT),
                           mem.place[:, :, :], ALU.add))
    then(dve.tensor_tensor(mem.place[:, :, :], mem.place[:, :, :], mem.onehot[:, :, :], ALU.mult))
    then(dve.tensor_reduce(mem.pos[:, :], mem.place[:, :, :], AX.X, ALU.add))
    dve.tensor_copy(mem.pos_u[:, :], mem.pos[:, :]).then_inc(m.routed.sem, 1)
    then(dve.tensor_tensor(mem.more[:, :, :], mem.count[:, 0:SLOTS].unsqueeze(2).to_broadcast([P, SLOTS, E]),
                           mem.end[:, :].unsqueeze(1).to_broadcast([P, SLOTS, E]), ALU.is_ge))
    then(dve.tensor_reduce(mem.slot_f[:, :], mem.more[:, :, :], AX.X, ALU.add))
    dve.tensor_scalar(mem.slot_e[:, :], mem.slot_f[:, :], float(E - 1), None, ALU.min).then_inc(m.routed.sem, 1)


def route_tensor(pe, m):
    mem = m.mem
    pe.wait_ge(m.onehot.sem, 1)
    onehot = mem.onehot[:, :, :].rearrange("p t e -> p (t e)")
    pe.matmul(mem.ps[:, 0, 0:NT * E], mem.tri[:, :], onehot, start=True, stop=True)
    pe.matmul(mem.ps[:, 1, 0:NT * E], mem.ones[:, :], onehot, start=True, stop=True).then_inc(m.counts.sem, 1)


def route_sync(sp, m, nc):
    mem = m.mem
    sp.dma_start(m.dram["inv"].rearrange("(s p) o -> s (p o)", p=P), mem.zero[:, :].bitcast(U32)).then_inc(m.cleared.sem, 16)
    sp.wait_ge(m.scattered.sem, 16 * NT)
    with nc.allow_non_contiguous_dma(reason="a table of four-byte indices, turned"):
        sp.dma_start(mem.inv[:, :], m.dram["inv"].rearrange("(s p) o -> p (s o)", p=P)).then_inc(m.inv_loaded.sem, 16)
    sp.wait_ge(m.inv_loaded.sem, 16)


def route_gpsimd(pool, m):
    mem = m.mem
    pool.wait_ge(m.cleared.sem, 16)
    pool.wait_ge(m.routed.sem, 1)
    for t in range(NT):
        pool.indirect_dma_start(m.dram["inv"], bass.IndirectOffsetOnAxis(ap=mem.pos_u[:, t:t + 1], axis=0),
                                mem.token[:, t:t + 1].bitcast(U32), None).then_inc(m.scattered.sem, 16)


def expert_of(eng, m, s):
    return eng.value_load(m.mem.slot_e[0:1, bass.ds(s, 1)], min_val=0, max_val=E - 1)


def each_slot(eng, body):
    pairs = (SLOTS - 3) // 2
    with eng.Fori(0, pairs) as i:
        for j in range(2):
            body(i * 2 + j, j, i)
    for s in range(2 * pairs, SLOTS):
        body(s, s % 2, s // 2)


def expert_sync(sp, m):
    mem = m.mem
    for j in range(2):
        sp.sem_inc(m.y_stored[j].sem, m.y_stored[j].lead)
    out = m.dram["y"].rearrange("(s p) d -> s p d", p=P)

    def body(s, j, i):
        ready = m.y_sum if m.hidden is not None else m.y_ready
        sp.wait_ge(ready.sem, ready.at(s, 1))
        sp.dma_start(out[s], mem.y[j]).then_inc(m.y_stored[j].sem, 16)

    each_slot(sp, body)
    for j in range(2):
        sp.wait_ge(m.y_stored[j].sem, m.y_stored[j].at((SLOTS + 1 - j) // 2))


def expert_gpsimd(pool, m):
    mem = m.mem
    for s in range(SLOTS):
        if s >= 2:
            pool.wait_ge(m.tx_ps.sem, m.tx_ps.at(s - 1))
        pool.indirect_dma_start(mem.xg[s % 2], None, m.dram["rows"],
                                bass.IndirectOffsetOnAxis(ap=mem.inv[:, s:s + 1], axis=0))\
            .then_inc(m.gathered[s % 2].sem, 16)


def expert_scalar(act, m):
    mem = m.mem
    ps = mem.ps
    act.sem_inc(m.xT_ready.sem, m.xT_ready.lead)
    act.sem_inc(m.midT_ready.sem, m.midT_ready.lead)

    def turned(s, j):
        act.wait_ge(m.tx_ps.sem, m.tx_ps.at(s, 1))
        if m.hidden is None:
            act.wait_ge(m.y_ps.sem, m.y_ps.at(s - 1))
            act.activation(mem.xT[j].rearrange("p c n -> p (c n)"), ps[:, 0, 0:C * P], ACT.Copy)\
               .then_inc(m.xT_ready.sem, 1)
            return
        for c in range(C):
            g, sh = m.affine + c, m.affine + C + c
            ins = act.activation(mem.xT[j][:, c, :], ps[:, 0, c * P:(c + 1) * P], ACT.Identity,
                                 bias=mem.cols[:, sh:sh + 1], scale=mem.cols[:, g:g + 1])
        ins.then_inc(m.xT_ready.sem, 1)

    def hidden(s):
        e = expert_of(act, m, s)
        act.wait_ge(m.y_ps.sem, m.y_ps.at(s))
        for f in range(FT):
            if f % 4 == 0:
                act.wait_ge(m.tm_ps.sem, m.tm_ps.at(s, f // 4 + 1))
            ins = act.activation(mem.midT[:, f, :], ps[:, 3 + f // 4, (f % 4) * P:(f % 4 + 1) * P], ACT.Relu,
                                 bias=mem.b1c[:, bass.ds(e * FT + f, 1)])
            if f % 4 == 3:
                ins.then_inc(m.midT_ready.sem, 1)

    def body(s, j, i):
        if m.hidden is not None:
            hidden(s)
        if type(s) is not int or s + 2 < SLOTS:
            turned(s + 2, j)

    turned(0, 0)
    turned(1, 1)
    each_slot(act, body)


def expert_vector(dve, m):
    mem = m.mem
    ps = mem.ps
    dve.sem_inc(m.mid_ready.sem, m.mid_ready.lead)
    dve.sem_inc(m.y_sum.sem, m.y_sum.lead)

    def hidden(s):
        for k in range(2):
            dve.wait_ge(m.h_ps.sem, m.h_ps.at(s, k + 1))
            if k == 0:
                dve.wait_ge(m.tm_ps.sem, m.tm_ps.at(s))
            dve.tensor_copy(mem.mid[:, k * 512:(k + 1) * 512], ps[:, 1 + k, :]).then_inc(m.mid_ready.sem, 1)

    def out(s, j, i):
        e = expert_of(dve, m, s)
        dve.wait_ge(m.y_ps.sem, m.y_ps.at(s, 1))
        dve.wait_ge(m.y_stored[j].sem, m.y_stored[j].at(i))
        bias = mem.b2[:, bass.ds(e, 1), :].rearrange("p e d -> p (e d)")
        dve.tensor_tensor(mem.y[j], ps[:, 5, 0:D], bias, ALU.add).then_inc(m.y_sum.sem, 1)
        if m.hidden is None:
            dve.wait_ge(m.y_sum.sem, m.y_sum.at(s, 1))
            dve.tensor_scalar(mem.y[j], mem.y[j], 0.0, None, ALU.max).then_inc(m.y_ready.sem, 1)

    def body(s, j, i):
        if m.hidden is not None and (type(s) is not int or s + 1 < SLOTS):
            hidden(s + 1)
        out(s, j, i)

    if m.hidden is not None:
        hidden(0)
    each_slot(dve, body)


def expert_tensor(pe, m):
    mem = m.mem
    ps = mem.ps
    pe.sem_inc(m.tx_ps.sem, m.tx_ps.lead)
    pe.sem_inc(m.tm_ps.sem, m.tm_ps.lead)
    pe.sem_inc(m.y_ps.sem, m.y_ps.lead)
    pe.wait_ge(m.weights.sem, m.weights.at(0, 48 if m.hidden is not None else 32))

    def turn_in(s, j, i):
        pe.wait_ge(m.gathered[j].sem, m.gathered[j].at(i, 16))
        pe.wait_ge(m.xT_ready.sem, m.xT_ready.at(s))
        for c in range(C):
            ins = pe.transpose(ps[:, 0, c * P:(c + 1) * P], mem.xg[j][:, c * P:(c + 1) * P], mem.ident[:, :])
        ins.then_inc(m.tx_ps.sem, 1)

    def up(s, j):
        e = expert_of(pe, m, s)
        pe.wait_ge(m.xT_ready.sem, m.xT_ready.at(s, 1))
        pe.wait_ge(m.mid_ready.sem, m.mid_ready.at(s))
        for k in range(2):
            for c in range(C):
                w = mem.w1[:, c, bass.ds(e, 1), k * 512:(k + 1) * 512].rearrange("p e f -> p (e f)")
                ins = pe.matmul(ps[:, 1 + k, :], mem.xT[j][:, c, :], w, start=(c == 0), stop=(c == C - 1))
            ins.then_inc(m.h_ps.sem, 1)

    def turn_mid(s):
        pe.wait_ge(m.midT_ready.sem, m.midT_ready.at(s))
        for f in range(FT):
            if f % 4 == 0:
                pe.wait_ge(m.mid_ready.sem, m.mid_ready.at(s, f // 4 + 1))
            ins = pe.transpose(ps[:, 3 + f // 4, (f % 4) * P:(f % 4 + 1) * P], mem.mid[:, f * P:(f + 1) * P],
                               mem.ident[:, :])
            if f % 4 == 3:
                ins.then_inc(m.tm_ps.sem, 1)

    def down(s, j):
        e = expert_of(pe, m, s)
        pe.wait_ge(m.y_sum.sem, m.y_sum.at(s))
        if m.hidden is None:
            pe.wait_ge(m.xT_ready.sem, m.xT_ready.at(s, 1))
            for c in range(C):
                w = mem.we[:, c, bass.ds(e, 1), :].rearrange("p e d -> p (e d)")
                ins = pe.matmul(ps[:, 5, 0:D], mem.xT[j][:, c, :], w, start=(c == 0), stop=(c == C - 1))
        else:
            for f in range(FT):
                if f % 4 == 0:
                    pe.wait_ge(m.midT_ready.sem, m.midT_ready.at(s, f // 4 + 1))
                w = mem.w2[:, f, bass.ds(e, 1), :].rearrange("p e d -> p (e d)")
                ins = pe.matmul(ps[:, 5, 0:D], mem.midT[:, f, :], w, start=(f == 0), stop=(f == FT - 1))
        ins.then_inc(m.y_ps.sem, 1)

    def body(s, j, i):
        if m.hidden is not None:
            turn_mid(s)
            if type(s) is not int or s + 1 < SLOTS:
                up(s + 1, 1 - j)
        down(s, j)
        if type(s) is not int or s + 2 < SLOTS:
            turn_in(s + 2, j, i + 1)

    turn_in(0, 0, 0)
    if m.hidden is not None:
        up(0, 0)
    turn_in(1, 1, 0)
    each_slot(pe, body)


def combine_gpsimd(pool, m):
    mem = m.mem
    for t in range(NT):
        pool.indirect_dma_start(mem.yg[:, t, :], None, m.dram["y"],
                                bass.IndirectOffsetOnAxis(ap=mem.pos_u[:, t:t + 1], axis=0)).then_inc(m.fetched.sem, 16)


def combine_sync(sp, m, out):
    mem = m.mem
    if m.hidden is not None:
        for b in range(B):
            sp.dma_start(mem.x[:, b, :, :], m.dram["acc"][b]).then_inc(m.acc_loaded.sem, 16)
    if out is not None:
        for b in range(B):
            sp.wait_ge(m.x_ready.sem, b + 1)
            sp.dma_start(out[b].rearrange("(t p) d -> p t d", p=P), mem.x[:, b, :, :]).then_inc(m.out_stored.sem, 16)
        sp.wait_ge(m.out_stored.sem, 16 * B)


def combine_vector(dve, m):
    mem = m.mem
    dve.wait_ge(m.fetched.sem, 16 * NT)
    if m.hidden is not None:
        dve.wait_ge(m.acc_loaded.sem, 16 * B)
    for b in range(B):
        if m.hidden is not None:
            ins = dve.tensor_tensor(mem.x[:, b, :, :], mem.x[:, b, :, :], mem.yg[:, b * T:(b + 1) * T, :], ALU.add)
        else:
            for t in range(T):
                ins = dve.scalar_tensor_tensor(mem.x[:, b, t, :], mem.yg[:, b * T + t, :], mem.prob[:, b, t:t + 1],
                                               mem.x[:, b, t, :], ALU.mult, ALU.add)
        ins.then_inc(m.x_ready.sem, 1)



WA, WB, WC = 0, 1, 0


def program(nc, x, ctx_in, mask, wa, wb, wc, cols, rows, b1c, b2, gate0, w1, w2, gate1, we, be, out):
    dram = {
        "ctx": ctx_in.rearrange("b (t p) d -> b p t d", p=P),
        "mask": mask.rearrange("b o (t p) k -> b p (o t) k", p=P),
        "q": nc.dram_tensor("q_parts", (B, D, TERMS, S), BF16, kind="Internal").ap(),
        "k": nc.dram_tensor("k_parts", (B, D, TERMS, S), BF16, kind="Internal").ap(),
        "acc": nc.dram_tensor("residual", (B, P, T, D), F32, kind="Internal").ap(),
        "rows": nc.dram_tensor("token_rows", (NT * P, D), F32, kind="Internal").ap(),
        "inv": nc.dram_tensor("slot_tokens", (SLOTS * P, 1), U32, kind="Internal").ap(),
        "y": nc.dram_tensor("slot_out", (SLOTS * P, D), F32, kind="Internal").ap(),
    }
    with ExitStack() as ctx:
        mem = Memory(nc, ctx)
        loaded = ctx.enter_context(nc.semaphore("loaded"))
        setup = ctx.enter_context(nc.semaphore("setup"))

        with nc.Block() as block:

            @block.sync
            def _(sp):
                for b in range(B):
                    sp.dma_start(mem.x[:, b, :, :], x[b].rearrange("(t p) d -> p t d", p=P)).then_inc(loaded, 16)
                sp.dma_start(mem.w[WA][:, :, :, :], wa).then_inc(loaded, 16)
                sp.dma_start(mem.cols[:, :], cols).then_inc(loaded, 16)
                sp.dma_start(mem.rows[:, :, :], rows[0]).then_inc(loaded, 16)
                sp.dma_start(mem.b1c[:, :], b1c).then_inc(loaded, 16)
                sp.dma_start(mem.w[WB][:, :, :, :], wb).then_inc(loaded, 16)
                sp.dma_start(mem.gate[:, :, 0:E], gate0).then_inc(loaded, 16)
                sp.wait_ge(loaded, 16 * (B + 6))

            @block.gpsimd
            def _(pool):
                pool.memset(mem.ident[:, :], 0.0).then_inc(setup, 1)
                pool.memset(mem.identb[:, :], 0.0).then_inc(setup, 1)
                pool.memset(mem.ones[:, :], 1.0).then_inc(setup, 1)
                pool.memset(mem.tri[:, :], 1.0).then_inc(setup, 1)
                pool.memset(mem.neghalf[:, :], -0.5).then_inc(setup, 1)
                pool.memset(mem.zero[:, :], 0).then_inc(setup, 1)
                pool.iota(mem.count_i[:, :], [[1, SLOTS + T]], base=0, channel_multiplier=0).then_inc(setup, 1)
                pool.iota(mem.token[:, :], [[P, NT]], base=0, channel_multiplier=1).then_inc(setup, 1)
                pool.wait_ge(setup, 8)
                for eye in (mem.ident, mem.identb):
                    pool.affine_select(out=eye[:, :], in_=eye[:, :], compare_op=ALU.not_equal, fill=1.0, base=0,
                                       pattern=[[-1, P]], channel_multiplier=1).then_inc(setup, 1)
                pool.affine_select(out=mem.tri[:, :], in_=mem.tri[:, :], compare_op=ALU.is_gt, fill=0.0, base=0,
                                   pattern=[[1, P]], channel_multiplier=-1).then_inc(setup, 1)
                pool.tensor_copy(mem.count[:, :], mem.count_i[:, :]).then_inc(setup, 1)
                pool.wait_ge(setup, 12)

        def cleared(stage):
            with nc.Block() as block:
                @block.gpsimd
                def _(pool):
                    for sem in (*stage.used, *stage.passed.values()):
                        pool.sem_clear(sem)

        def attention(*what):
            with ExitStack() as stage:
                a = Attention(nc, ctx, stage, mem, dram, *what)
                attention_blocks(a)
                cleared(a)

        def mixture(*what, loads, result=None):
            with ExitStack() as stage:
                m = Mixture(nc, ctx, stage, mem, dram, *what)
                mixture_blocks(m, loads, result)
                if result is None:
                    cleared(m)

        def attention_blocks(a):
            with nc.Block() as block:
                block.sync(lambda sp: project_sync(sp, a))
                block.gpsimd(lambda pool: project_gpsimd(pool, a))
                block.scalar(lambda act: project_scalar(act, a))
                block.vector(lambda dve: project_vector(dve, a))
                block.tensor(lambda pe: project_tensor(pe, a))
            with nc.Block() as block:
                block.sync(lambda sp: attend_sync(sp, a))
                block.gpsimd(lambda pool: attend_gpsimd(pool, a))
                block.scalar(lambda act: attend_scalar(act, a))
                block.vector(lambda dve: attend_vector(dve, a))
                block.tensor(lambda pe: attend_tensor(pe, a))

        def mixture_blocks(m, loads, result):
            with nc.Block() as block:
                @block.sync
                def _(sp):
                    for dst, src in loads:
                        sp.dma_start(dst, src).then_inc(m.weights.sem, 16)
                    gate_sync(sp, m)
                block.gpsimd(lambda pool: gate_gpsimd(pool, m))
                block.scalar(lambda act: gate_scalar(act, m))
                block.vector(lambda dve: gate_vector(dve, m))
                block.tensor(lambda pe: gate_tensor(pe, m))
            with nc.Block() as block:
                block.sync(lambda sp: route_sync(sp, m, nc))
                block.gpsimd(lambda pool: route_gpsimd(pool, m))
                block.vector(lambda dve: route_vector(dve, m))
                block.tensor(lambda pe: route_tensor(pe, m))
            with nc.Block() as block:
                block.sync(lambda sp: expert_sync(sp, m))
                block.gpsimd(lambda pool: expert_gpsimd(pool, m))
                block.scalar(lambda act: expert_scalar(act, m))
                block.vector(lambda dve: expert_vector(dve, m))
                block.tensor(lambda pe: expert_tensor(pe, m))
            with nc.Block() as block:
                block.sync(lambda sp: combine_sync(sp, m, result))
                block.gpsimd(lambda pool: combine_gpsimd(pool, m))
                block.vector(lambda dve: combine_vector(dve, m))

        attention("a", WA, True, 1, None, {"qk": 0}, None, True, False)
        attention("b", WB, False, 2, 12, {"qk": 4}, 0, False, True)
        mixture("e", 16, E, 4, F, loads=[(mem.w1, w1), (mem.w2, w2), (mem.b2, b2)])
        with nc.Block() as block:
            @block.sync
            def _(sp):
                sp.dma_start(mem.w[WC][:, :, :, :], wc).then_inc(loaded, 16)
                sp.dma_start(mem.gate[:, :, :], gate1).then_inc(loaded, 16)
                sp.dma_start(mem.rows[:, :, :], rows[1]).then_inc(loaded, 16)
                sp.wait_ge(loaded, 16 * (B + 9))
        attention("c", WC, True, 1, None, {"qk": 8}, 2, False, False)
        mixture("f", None, D, 4, None, loads=[(mem.we, we), (mem.b2, be)], result=out)


def kernel(**inputs):
    import concourse.bacc as bacc
    from concourse.bass_utils import run_bass_kernel_spmd

    a = {k: np.asarray(v) for k, v in inputs.items()}

    def weight(w):
        return w.reshape(C, P, -1).transpose(1, 0, 2)

    def weights(names, turned):
        return np.ascontiguousarray(np.stack([weight(a[n].T if turned else a[n]) for n in names], 1))

    def col(v):
        return v.reshape(C, P).T

    def row(v):
        return np.broadcast_to(np.pad(v, (0, D - v.size)), (P, D))

    zero = np.zeros(D, np.float32)
    f0, x1, f1 = "L0_ffn_", "L1_xattn_", "L1_ffn_"
    arrays = {
        "x": a["x"], "ctx": a["ctx_1024"], "mask": a["mask_Bx1xSxS2_ik0"],
        "wa": weights(["L0_xattn_W_Q", "L0_xattn_W_K", "L0_xattn_W_V", "L0_xattn_W_O"], True),
        "wb": weights([f0 + "wq", f0 + "wk", f0 + "wv", f0 + "wo"], False),
        "wc": weights([x1 + "Wq", x1 + "Wk", x1 + "Wv", x1 + "Wo"], True),
        "cols": np.concatenate([col(v) for v in (
            zero, zero, a[f0 + "bq"], a[f0 + "bk"], a[x1 + "bq"], a[x1 + "bk"],
            a[f0 + "ln1_g"], a[f0 + "ln1_b"], a[f0 + "ln2_g"], a[f0 + "ln2_b"])], 1),
        "rows": np.stack([
            np.stack([row(v) for v in (a[f0 + "bv"], a[f0 + "bo"], zero, zero, a[f0 + "gate_b"])], 1),
            np.stack([row(v) for v in (zero, zero, a[x1 + "bv"], a[x1 + "bo"], a[f1 + "bg"])], 1)]),
        "b1c": a[f0 + "b1"].reshape(E * FT, P).T,
        "b2": np.broadcast_to(a[f0 + "b2"], (P, E, D)),
        "gate0": weight(a[f0 + "gate_w"]),
        "w1": a[f0 + "w1"].reshape(E, C, P, F).transpose(2, 1, 0, 3),
        "w2": a[f0 + "w2"].reshape(E, FT, P, D).transpose(2, 1, 0, 3),
        "gate1": weight(a[f1 + "Wg"]),
        "we": a[f1 + "We"].reshape(E, C, P, D).transpose(2, 1, 0, 3),
        "be": np.broadcast_to(a[f1 + "be"], (P, E, D)),
    }
    arrays = {f"in_{k}": np.ascontiguousarray(v) for k, v in arrays.items()}
    nc = bacc.Bacc("TRN2", target_bir_lowering=False, num_devices=1)
    ins = [nc.dram_tensor(k, v.shape, mybir.dt.from_np(v.dtype), kind="ExternalInput").ap() for k, v in arrays.items()]
    out = nc.dram_tensor("out", (B, S, D), F32, kind="ExternalOutput").ap()
    program(nc, *ins, out)
    r = run_bass_kernel_spmd(nc, [arrays], core_ids=[0])
    return r.results[0]["out"]
```

```python
from contextlib import ExitStack

import numpy as np

import concourse.bass as bass
from concourse import mybir

F32 = mybir.dt.float32
BF16 = mybir.dt.bfloat16
I32 = mybir.dt.int32
U32 = mybir.dt.uint32
ALU = mybir.AluOpType
ACT = mybir.ActivationFunctionType
AX = mybir.AxisListType

P = 128
B, S, D, H = 4, 512, 256, 16
DK = D // H
T = S // P
C = D // P
HG = 4
NG = H // HG
GW = HG * DK
TERMS = 6
ROWS = TERMS * DK
PARTS = 3
KROWS = ROWS + PARTS
VW = 32
E = 8
F = 1024
FT = F // P
NT = B * T
SLOTS = NT + E - 1
EPS = 1e-5
MASKED = -(2.0 ** 100)
FLOOR = -1e29
SCALE = float(DK) ** -0.5


class Signal:

    def __init__(self, sem, per, lead=0):
        self.sem, self.per, self.lead = sem, per, lead

    def at(self, i, k=0):
        return i * self.per + (self.lead + k)


def wait_alone(eng, sem, value, passed):
    eng.wait_ge(sem, value)
    eng.sem_inc(passed, 1)


class Memory:

    def __init__(self, nc, ctx):
        def sb(name, shape, dt=F32):
            return ctx.enter_context(nc.sbuf_tensor(name, shape, dt))

        self.x = sb("x", [P, B, T, D])
        self.w = [sb(f"w{i}", [P, 4, C, D]) for i in range(2)]
        self.r1 = sb("r1", [P, C * E * F])
        self.r2 = sb("r2", [P, 24576])
        self.cols = sb("cols", [P, 20])
        self.rows = sb("rows", [P, 5, D])
        self.gate = sb("gate", [P, C, D])
        self.ident = sb("ident", [P, P])
        self.identb = sb("identb", [P, P], BF16)
        self.neghalf = sb("neghalf", [P, T])
        self.stats = sb("stats", [P, T, 6])
        self.mv = sb("mv", [P, T, 2])
        self.var = sb("var", [P, T])
        self.rstd = sb("rstd", [P, T])
        self.mv_in = sb("mv_in", [P, B, T, 2])
        self.rstd_in = sb("rstd_in", [P, B, T])
        self.m = sb("m", [P, 2, T, HG])
        self.mres = sb("mres", [P, T, HG])
        self.mparts = sb("mparts", [P, T, PARTS, HG], BF16)
        self.mT = sb("mT", [PARTS * HG, S], BF16)
        self.den = sb("den", [P, T, HG])
        self.rden = sb("rden", [P, T, HG])
        self.tri = sb("tri", [P, P])
        self.ones = sb("ones", [P, P])
        self.zero = sb("zero", [SLOTS, P], I32)
        self.count_i = sb("count_i", [P, SLOTS + T], I32)
        self.count = sb("count", [P, SLOTS + T])
        self.token = sb("token", [P, NT], I32)
        self.b1c = sb("b1c", [P, E * FT])
        self.top8 = sb("top8", [P, T, 8])
        self.idx8 = sb("idx8", [P, T, 8], U32)
        self.expert_u = sb("expert_u", [P, T], U32)
        self.ntop = sb("ntop", [P, T])
        self.sum = sb("sum", [P, T])
        self.expert = sb("expert", [P, B, T])
        self.prob = sb("prob", [P, B, T])
        self.onehot = sb("onehot", [P, NT, E])
        self.tiles = sb("tiles", [P, NT, E])
        self.place = sb("place", [P, NT, E])
        self.more = sb("more", [P, SLOTS, E])
        self.total = sb("total", [P, E])
        self.need = sb("need", [P, E])
        self.end = sb("end", [P, E])
        self.start = sb("start", [P, E])
        self.pos = sb("pos", [P, NT])
        self.pos_u = sb("pos_u", [P, NT], U32)
        self.slot_f = sb("slot_f", [P, SLOTS])
        self.slot_e = sb("slot_e", [P, SLOTS], I32)
        self.inv = sb("inv", [P, SLOTS], U32)
        self.ps = ctx.enter_context(nc.psum_tensor("ps", [P, 8, 512], F32))
        self._r1 = self._r2 = 0

        self.total_x, self.block_in = (self.w[0][:, 2 * i:2 * i + 2, :, :].rearrange("p i c d -> p (i c) d")
                                       for i in range(2))

        at = [0]

        def take(region, words, shape, dt=F32):
            n = at[0]
            at[0] += words
            assert at[0] <= region.shape[1], (at[0], region.shape)
            v = region[:, n:n + words]
            if dt is not F32:
                v = v.bitcast(dt)
            if len(shape) == 1:
                return v
            names = "abcd"[:len(shape)]
            kw = dict(zip(names[1:], shape[1:]))
            return v.rearrange(f"p ({' '.join(names)}) -> p {' '.join(names)}", **kw)

        self.hn = take(self.r1, T * D, [T, D])
        self.hT = take(self.r1, C * S, [C, S])
        self.cin = take(self.r1, T * D, [T, D])
        self.cT = take(self.r1, C * S, [C, S])
        self.parts = [take(self.r1, PARTS * S // 2, [PARTS, S], BF16) for _ in range(2 * C)]
        self.res = [take(self.r1, S, [S]) for _ in range(2)]
        self.mb_all = take(self.r1, B * T * S // 2, [B, T, S], BF16)
        self.mint = take(self.r1, T * S, [T, S], I32)
        self.junk = [self.mint[:, t, 0:S // 2].bitcast(BF16) for t in range(DEEP)]
        self.mbS = take(self.r1, T * S // 2, [T, S], BF16)
        self.mbT = take(self.r1, T * S // 2, [T, S], BF16)
        self.w1 = self.r1[:, :].rearrange("p (c e f) -> p c e f", c=C, e=E)
        self.we = self.r1[:, 0:C * E * D].rearrange("p (c e f) -> p c e f", c=C, e=E)

        at[0] = 0
        self.probs = take(self.r2, T * HG * S, [T, HG, S])
        self.qst = [take(self.r2, HG * S // 2, [HG, S], BF16) for _ in range(NG)]
        self.kst = [take(self.r2, HG * S // 2, [HG, S], BF16) for _ in range(NG)]
        self.v = take(self.r2, B * NG * T * GW, [B, NG, T, GW])
        self.vg = [take(self.r2, T * HG * VW, [T, HG, VW]) for _ in range(2)]
        self.ot = take(self.r2, S, [S])
        self.o = take(self.r2, T * D, [T, D])
        self.oT = take(self.r2, C * S, [C, S])
        at[0] = 0
        self.w2 = take(self.r2, FT * E * D, [FT, E, D])
        self.xg = [take(self.r2, D, [D]) for _ in range(2)]
        self.xT = [take(self.r2, C * P, [C, P]) for _ in range(2)]
        self.mid = take(self.r2, F, [F])
        self.midT = take(self.r2, FT * P, [FT, P])
        self.y = [take(self.r2, D, [D]) for _ in range(2)]
        self.rn = take(self.r2, T * D, [T, D])
        self.rnT = take(self.r2, C * S, [C, S])
        self.logits = self.mid.rearrange("p (t d) -> p t d", t=T)
        self.exps = self.midT.rearrange("p f n -> p (f n)").rearrange("p (t d) -> p t d", t=T)
        self.b2 = take(self.r2, E * D, [E, D])
        self.yg = self.r2[:, 0:NT * D].rearrange("p (t d) -> p t d", t=NT)


class Attention:

    def __init__(self, nc, ctx, stage, mem, dram, name, w, cross, norms, affine, cols, rows, masked, self_block,
                 x_first=None, x_rest=None):
        self.x_first, self.x_rest = x_first, x_rest
        self.mem, self.dram, self.name = mem, dram, name
        self.w, self.cross, self.norms, self.affine = mem.w[w], cross, norms, affine
        self.cols, self.rows, self.masked, self.self_block = cols, rows, masked, self_block

        self.used = []

        def sig(what, per, lead=0, kept=stage):
            self.used.append(kept.enter_context(nc.semaphore(f"{name}_{what}")))
            return Signal(self.used[-1], per, lead)

        self.passed = {eng: stage.enter_context(nc.semaphore(f"{name}_{eng}_passed")) for eng in ("dve", "pool")}
        self.stat = [sig(f"stat{n}", T) for n in range(norms)]
        self.aggr = [sig(f"aggr{n}", T) for n in range(norms)]
        self.vare = [sig(f"vare{n}", 1) for n in range(norms)]
        self.rs = [sig(f"rs{n}", 1) for n in range(norms)]
        self.first_norm = sig("first_norm", T)
        self.hn_ready = sig("hn_ready", T)
        self.hT_ps = sig("hT_ps", C, C)
        self.hT_ready = sig("hT_ready", C, C)
        self.c_loaded = sig("c_loaded", 16)
        self.cT_ps = sig("cT_ps", C, C)
        self.cT_ready = sig("cT_ready", C, C)
        self.qk_ps = sig("qk_ps", 2 * C, 2 * C)
        self.hi = sig("hi", 2 * C)
        self.r1 = sig("r1", 2 * C)
        self.midp = sig("midp", 2 * C)
        self.lo = sig("lo", 2 * C, 2 * C)
        self.stored = [sig(f"stored{n}", 16 * PARTS, 16 * PARTS) for n in range(2 * C)]
        self.v_ps = sig("v_ps", 2)
        self.v_ready = sig("v_ready", 2, 2)
        self.mask_loaded = sig("mask_loaded", 16)
        self.mask_bias = sig("mask_bias", 1, 1)
        self.preset = sig("preset", 1)
        self.stacks = [sig(f"stacks{s}", 32) for s in range(NG)]
        self.shift = [sig(f"shift{s}", 16) for s in range(NG)]
        self.s_ps = sig("s_ps", UNITS)
        self.s_max = sig("s_max", UNITS)
        self.m_hi = sig("m_hi", 1)
        self.m_res = sig("m_res", 1)
        self.m_mid = sig("m_mid", 1)
        self.m_lo = sig("m_lo", 1)
        self.m_ps = sig("m_ps", 1)
        self.m_sb = sig("m_sb", 1)
        self.st_ps = sig("st_ps", UNITS)
        self.p_exp = sig("p_exp", UNITS)
        self.vg_ready = sig("vg_ready", 1)
        self.pv = sig("pv", T, T)
        self.ot_sb = sig("ot_sb", 1, 1)
        self.ot_ps = sig("ot_ps", 1, 1)
        self.den = sig("den", 1)
        self.rden = sig("rden", 1)
        self.o_ready = sig("o_ready", 1)
        self.oT_ps = sig("oT_ps", C)
        self.oT_sb = sig("oT_sb", C)
        self.op_ps = sig("op_ps", 2)
        self.op_used = sig("op_used", 2)
        self.step = [sig(f"step{n}", 2) for n in range(4)] if self_block else []
        self.acc_ready = sig("acc_ready", 2)
        self.acc_stored = sig("acc_stored", 32, 32)
        self.mbS_ready = sig("mbS_ready", 1)
        self.mbT_ready = sig("mbT_ready", 1)




def each_batch(eng, body):
    with eng.Fori(0, B - 1) as b:
        body(b, b + 1)
    body(B - 1, None)


def project_vector(dve, a):
    mem = a.mem
    ps = mem.ps
    for s in range(NG):
        dve.memset(mem.kst[s][ROWS:P, :, :], 1.0)
    for g in range(2):
        dve.memset(mem.vg[g][:, :, :, DK:VW], 0.0)
    dve.sem_inc(a.v_ready.sem, a.v_ready.lead)
    dve.sem_inc(a.lo.sem, a.lo.lead)

    def statistics(b, n):
        for t in range(T):
            src = mem.x[:, b, t, :] if n == 0 else mem.hn[:, t, :]
            if n == 1:
                dve.wait_ge(a.first_norm.sem, a.first_norm.at(b, t + 1))
            dve.bn_stats(mem.stats[:, t, :], src).then_inc(a.stat[n].sem, 1)
        for t in range(T):
            wait_alone(dve, a.stat[n].sem, a.stat[n].at(b, t + 1), a.passed["dve"])
            dve.bn_aggr(mem.mv[:, t, :], mem.stats[:, t, :]).then_inc(a.aggr[n].sem, 1)

    def normalise(b, n):
        last = n == a.norms - 1
        wait_alone(dve, a.rs[n].sem, a.rs[n].at(b, 1), a.passed["dve"])
        if not last:
            dve.tensor_copy(mem.mv_in[:, b, :, :], mem.mv[:, :, :])
            dve.tensor_copy(mem.rstd_in[:, b, :], mem.rstd[:, :])
        for t in range(T):
            if n == 0 and t == 0:
                dve.wait_ge(a.hT_ps.sem, a.hT_ps.at(b))
            src = mem.x[:, b, t, :] if n == 0 else mem.hn[:, t, :]
            out = dve.tensor_scalar(mem.hn[:, t, :], src, mem.mv[:, t, 0:1], mem.rstd[:, t:t + 1],
                                    ALU.subtract, ALU.mult)
            sig = a.hn_ready if last else a.first_norm
            out.then_inc(sig.sem, 1)

    def values(b, k):
        dve.wait_ge(a.v_ps.sem, a.v_ps.at(b, k + 1))
        for t in range(2):
            out = mem.v[:, b, :, 2 * k + t, :]
            got = ps[:, 6 + k, t * D:(t + 1) * D].rearrange("p (g d) -> p g d", g=NG)
            if a.rows is None:
                ins = dve.tensor_copy(out, got)
            else:
                row = mem.rows[:, a.rows, :].rearrange("p (g d) -> p g d", g=NG)
                ins = dve.tensor_tensor(out, got, row, ALU.add)
        ins.then_inc(a.v_ready.sem, 1)

    def rest(b, n):
        bias = mem.cols[:, a.cols["qk"] + n:a.cols["qk"] + n + 1]
        dve.wait_ge(a.hi.sem, a.hi.at(b, n + 1))
        dve.wait_ge(a.lo.sem, a.lo.at(b, n - 1))
        dve.scalar_tensor_tensor(mem.res[n % 2], ps[:, 2 + n, :], bias, mem.parts[n][:, 0, :],
                                 ALU.add, ALU.subtract).then_inc(a.r1.sem, 1)

    def third(b, n):
        dve.wait_ge(a.midp.sem, a.midp.at(b, n + 1))
        dve.tensor_tensor(mem.parts[n][:, 2, :], mem.res[n % 2], mem.parts[n][:, 1, :],
                          ALU.subtract).then_inc(a.lo.sem, 1)

    def body(b, ahead):
        for n in range(a.norms):
            if ahead is not None:
                statistics(ahead, n)
            if n == 0:
                values(b, 0)
            if ahead is not None:
                normalise(ahead, n)
        values(b, 1)
        for n in range(2 * C + 1):
            if n < 2 * C:
                rest(b, n)
            if n >= 1:
                third(b, n - 1)
        if a.masked:
            dve.wait_ge(a.mask_loaded.sem, a.mask_loaded.at(b, 16))
            dve.tensor_scalar(mem.mb_all[:, b, :, :], mem.mint[:, :, :], 0.0, MASKED, ALU.is_equal,
                              ALU.mult).then_inc(a.mask_bias.sem, 1)

    if a.masked:
        dve.sem_inc(a.mask_bias.sem, a.mask_bias.lead)
    if a.x_first is not None:
        dve.wait_ge(a.x_first, 16)
    for n in range(a.norms):
        statistics(0, n)
        normalise(0, n)
    if a.x_first is not None:
        dve.wait_ge(a.x_rest, 16 * (B - 1))
    each_batch(dve, body)


def project_gpsimd(pool, a):
    mem = a.mem

    def scale(b):
        for n in range(a.norms):
            wait_alone(pool, a.aggr[n].sem, a.aggr[n].at(b, T), a.passed["pool"])
            pool.tensor_scalar(mem.var[:, :], mem.mv[:, :, 1], EPS, None, ALU.add).then_inc(a.vare[n].sem, 1)
            pool.wait_ge(a.vare[n].sem, a.vare[n].at(b, 1))
            pool.tensor_tensor(mem.rstd[:, :], mem.var[:, :], mem.neghalf[:, :], ALU.pow).then_inc(a.rs[n].sem, 1)

    def body(b, ahead):
        if ahead is not None:
            scale(ahead)
        for n in range(2 * C):
            wait_alone(pool, a.r1.sem, a.r1.at(b, n + 1), a.passed["pool"])
            pool.tensor_copy(mem.parts[n][:, 1, :], mem.res[n % 2]).then_inc(a.midp.sem, 1)

    scale(0)
    each_batch(pool, body)


def project_scalar(act, a):
    mem = a.mem
    ps = mem.ps

    def turned(b):
        for c in range(C):
            act.wait_ge(a.hT_ps.sem, a.hT_ps.at(b, c + 1))
            if c == 0:
                act.wait_ge(a.qk_ps.sem, a.qk_ps.at(b))
            if a.affine is None:
                ins = act.activation(mem.hT[:, c, :], ps[:, c, :], ACT.Copy)
            else:
                g, s = a.affine + c, a.affine + C + c
                ins = act.activation(mem.hT[:, c, :], ps[:, c, :], ACT.Identity, bias=mem.cols[:, s:s + 1],
                                     scale=mem.cols[:, g:g + 1])
            ins.then_inc(a.hT_ready.sem, 1)
        if a.cross:
            for c in range(C):
                act.wait_ge(a.cT_ps.sem, a.cT_ps.at(b, c + 1))
                act.activation(mem.cT[:, c, :], ps[:, 6 + c, :], ACT.Copy).then_inc(a.cT_ready.sem, 1)

    def body(b, ahead):
        for n in range(2 * C):
            act.wait_ge(a.qk_ps.sem, a.qk_ps.at(b, n + 1))
            act.wait_ge(a.stored[n].sem, a.stored[n].at(b))
            bias = mem.cols[:, a.cols["qk"] + n:a.cols["qk"] + n + 1]
            act.activation(mem.parts[n][:, 0, :], ps[:, 2 + n, :], ACT.Identity, bias=bias).then_inc(a.hi.sem, 1)
        if ahead is not None:
            turned(ahead)

    act.sem_inc(a.hT_ready.sem, a.hT_ready.lead)
    act.sem_inc(a.cT_ready.sem, a.cT_ready.lead)
    turned(0)
    each_batch(act, body)


def project_tensor(pe, a):
    mem = a.mem
    ps = mem.ps
    kv = mem.cT if a.cross else mem.hT

    def turn(b):
        pe.wait_ge(a.hT_ready.sem, a.hT_ready.at(b))
        pe.wait_ge(a.hn_ready.sem, a.hn_ready.at(b, T))
        for c in range(C):
            for t in range(T):
                ins = pe.transpose(ps[:, c, t * P:(t + 1) * P], mem.hn[:, t, c * P:(c + 1) * P], mem.ident[:, :])
            ins.then_inc(a.hT_ps.sem, 1)
        if a.cross:
            pe.wait_ge(a.v_ready.sem, a.v_ready.at(b))
            pe.wait_ge(a.c_loaded.sem, a.c_loaded.at(b, 16))
            for c in range(C):
                for t in range(T):
                    ins = pe.transpose(ps[:, 6 + c, t * P:(t + 1) * P], mem.cin[:, t, c * P:(c + 1) * P],
                                       mem.ident[:, :])
                ins.then_inc(a.cT_ps.sem, 1)

    def body(b, ahead):
        pe.wait_ge(a.hT_ready.sem, a.hT_ready.at(b, C))
        if a.cross:
            pe.wait_ge(a.cT_ready.sem, a.cT_ready.at(b, C))
        pe.wait_ge(a.v_ready.sem, a.v_ready.at(b))
        for k in range(2):
            for t in range(2):
                for c in range(C):
                    ins = pe.matmul(ps[:, 6 + k, t * D:(t + 1) * D], kv[:, c, (2 * k + t) * P:(2 * k + t + 1) * P],
                                    a.w[:, 2, c, :], start=(c == 0), stop=(c == C - 1))
            ins.then_inc(a.v_ps.sem, 1)
        for n in range(2 * C):
            src = mem.hT if n < C else kv
            pe.wait_ge(a.lo.sem, a.lo.at(b - 1, n + 1))
            for c in range(C):
                ins = pe.matmul(ps[:, 2 + n, :], a.w[:, n // C, c, (n % C) * P:(n % C + 1) * P], src[:, c, :],
                                start=(c == 0), stop=(c == C - 1))
            ins.then_inc(a.qk_ps.sem, 1)
        if ahead is not None:
            turn(ahead)

    pe.sem_inc(a.hT_ps.sem, a.hT_ps.lead)
    pe.sem_inc(a.cT_ps.sem, a.cT_ps.lead)
    pe.sem_inc(a.qk_ps.sem, a.qk_ps.lead)
    turn(0)
    each_batch(pe, body)


def project_sync(sp, a):
    mem = a.mem

    def context(b):
        if a.cross:
            sp.wait_ge(a.cT_ps.sem, a.cT_ps.at(b))
            sp.dma_start(mem.cin[:, :, :], a.dram["ctx"][b]).then_inc(a.c_loaded.sem, 16)

    def mask(b):
        if a.masked:
            sp.wait_ge(a.mask_bias.sem, a.mask_bias.at(b))
            sp.dma_start(mem.mint[:, :, :], a.dram["mask"][b]).then_inc(a.mask_loaded.sem, 16)

    def body(b, ahead):
        if ahead is not None:
            context(ahead)
        for n in range(2 * C):
            half = slice((n % C) * P, (n % C + 1) * P)
            out = a.dram["q" if n < C else "k"][b, half, :, :]
            sp.wait_ge(a.lo.sem, a.lo.at(b, n + 1))
            runs = ((0, 3), (3, 5), (5, 6))
            for i, (r0, r1) in enumerate(runs):
                if n < C:
                    src = mem.parts[n][:, 0:r1 - r0, :]
                else:
                    src = mem.parts[n][:, i:i + 1, :].to_broadcast([P, r1 - r0, S])
                sp.dma_start(out[:, r0:r1, :], src).then_inc(a.stored[n].sem, 16)
        if ahead is not None:
            mask(ahead)

    for n in range(2 * C):
        sp.sem_inc(a.stored[n].sem, a.stored[n].lead)
    context(0)
    mask(0)
    each_batch(sp, body)



UNITS = T * HG
ROUND = NG * UNITS
DEEP = 3
ST, SB = 0, DEEP
OB = 2 * DEEP
MISC = OB + 1
LATE = 2
M_STEP, TURN_STEP = 5, 8
OUT_TURNS = (0, 3)
OUT_TILES = ((1, 11), (1, 12), (2, 0), (2, 1))


def before(b, n):
    n -= DEEP
    if n < 0:
        b = b - 1
        n = max(m for m in range(ROUND) if m % DEEP == (n + DEEP) % DEEP)
    return NG * b + n // UNITS, n % UNITS


def attend_sync(sp, a, meanwhile):
    mem = a.mem

    def load(b, g):
        for dst, src in ((mem.qst[g], a.dram["q"]), (mem.kst[g], a.dram["k"])):
            rows = src[b, g * GW:(g + 1) * GW, :, :].rearrange("(h r) t n -> (r t) h n", h=HG)
            sp.dma_start(dst[0:ROWS, :, :], rows).then_inc(a.stacks[g].sem, 16)

    def shift(b, g):
        G = NG * b + g
        sp.wait_ge(a.m_sb.sem, a.m_sb.at(G, 1))
        sp.dma_start(mem.qst[g][ROWS:KROWS, :, :], mem.mT[:, :]).then_inc(a.shift[g].sem, 16)

    def body(b, first, last):
        for g in range(NG):
            G = NG * b + g
            ahead = (b, g + 2) if g < 2 else (b + 1, g - 2)
            if not (last and g >= 2):
                if not (first and g < 2):
                    sp.wait_ge(a.st_ps.sem, a.st_ps.at(G - 1))
                load(*ahead)
            if a.self_block and g == 2 and not first:
                store(b - 1)
            if not (last and g == NG - 1):
                shift(*((b, g + 1) if g < NG - 1 else (b + 1, 0)))
            if meanwhile is not None:
                meanwhile(sp, b, g)

    def store(b):
        for k in range(2):
            sp.wait_ge(a.acc_ready.sem, a.acc_ready.at(b, k + 1))
            sp.dma_start(a.dram["acc"][b, :, 2 * k:2 * k + 2, :], mem.total_x[:, 2 * k:2 * k + 2, :])\
              .then_inc(a.acc_stored.sem, 16)

    if a.self_block:
        sp.sem_inc(a.acc_stored.sem, a.acc_stored.lead)
    for n in range(2 * C):
        sp.wait_ge(a.stored[n].sem, a.stored[n].at(B))
    load(0, 0)
    load(0, 1)
    shift(0, 0)
    body(0, True, False)
    with sp.Fori(1, B - 1) as b:
        body(b, False, False)
    body(B - 1, False, True)
    if a.self_block:
        store(B - 1)
        sp.wait_ge(a.acc_stored.sem, a.acc_stored.at(B))


def attend_gpsimd(pool, a):
    mem = a.mem

    def gather(b, g):
        G = NG * b + g
        if not (type(b) is int and G < 2):
            wait_alone(pool, a.pv.sem, a.pv.at(G - 1), a.passed["pool"])
        pool.tensor_copy(mem.vg[g % 2][:, :, :, 0:DK],
                         mem.v[:, b, g, :, :].rearrange("p t (h d) -> p t h d", h=HG)).then_inc(a.vg_ready.sem, 1)

    pool.wait_ge(a.v_ready.sem, a.v_ready.at(B))
    for g in range(2):
        pool.memset(mem.vg[g][:, :, :, DK:DK + 1], 1.0).then_inc(a.preset.sem, 1)
    pool.wait_ge(a.preset.sem, 2)
    for g in range(NG):
        gather(0, g)
    with pool.Fori(1, B) as b:
        for g in range(NG):
            gather(b, g)


def attend_scalar(act, a):
    mem = a.mem
    ps = mem.ps

    def exps(b, g, u):
        G = NG * b + g
        act.wait_ge(a.st_ps.sem, a.st_ps.at(G, u + 1))
        if u % HG == 0:
            act.wait_ge(a.pv.sem, a.pv.at(G - 1, u // HG + 1))
        act.activation(mem.probs[:, u // HG, u % HG, :], ps[:, ST + (UNITS * g + u) % DEEP, :], ACT.Exp,
                       scale=SCALE).then_inc(a.p_exp.sem, 1)

    def out_copy(G):
        act.wait_ge(a.pv.sem, a.pv.at(G, T))
        act.wait_ge(a.ot_ps.sem, a.ot_ps.at(G))
        act.activation(mem.ot, ps[:, OB, :], ACT.Copy).then_inc(a.ot_sb.sem, 1)

    def maxima(G, used=None):
        act.wait_ge(a.m_ps.sem, a.m_ps.at(G, 1))
        if used is not None:
            b, g = used
            act.wait_ge(a.shift[g].sem, a.shift[g].at(b, 16))
        act.activation(mem.mT[:, :], ps[0:PARTS * HG, MISC, 0:S // 2].bitcast(BF16), ACT.Copy)\
           .then_inc(a.m_sb.sem, 1)

    def oT_copy(b, c):
        act.wait_ge(a.oT_ps.sem, a.oT_ps.at(b, c + 1))
        act.activation(mem.oT[:, c, :], ps[:, MISC, :], ACT.Copy).then_inc(a.oT_sb.sem, 1)

    def body(b, first, last):
        for g in range(NG):
            G = NG * b + g
            for u in range(UNITS):
                exps(b, g, u)
                if g == 1 and not first and u in OUT_TURNS:
                    oT_copy(b - 1, OUT_TURNS.index(u))
                if u == LATE and not (first and g == 0):
                    out_copy(G - 1)
                if u == M_STEP and not (last and g == NG - 1):
                    maxima(G + 1, (b, g))

    act.sem_inc(a.ot_sb.sem, a.ot_sb.lead)
    maxima(0)
    body(0, True, False)
    with act.Fori(1, B - 1) as b:
        body(b, False, False)
    body(B - 1, False, True)
    out_copy(B * NG - 1)
    oT_copy(B - 1, 0)
    oT_copy(B - 1, 1)


def attend_tensor(pe, a):
    mem = a.mem
    ps = mem.ps
    misc = [None]

    def take_misc():
        if misc[0] is not None:
            pe.wait_ge(*misc[0])

    def scores(G, g, v, used):
        h, t = v // T, v % T
        if used is not None:
            pe.wait_ge(a.s_max.sem, a.s_max.at(used[0], used[1] + 1))
        pe.matmul(ps[:, SB + (UNITS * (g + 2) + v) % ROUND % DEEP, :], mem.qst[g][0:ROWS, h, t * P:(t + 1) * P],
                  mem.kst[g][0:ROWS, h, :], start=True, stop=True).then_inc(a.s_ps.sem, 1)

    def transposed_scores(b, g, u, first):
        G, kt, h = NG * b + g, u // HG, u % HG
        if not (first and UNITS * g + u < DEEP):
            used = before(b, UNITS * g + u)
            pe.wait_ge(a.p_exp.sem, a.p_exp.at(used[0], used[1] + 1))
        if u == 0:
            pe.wait_ge(a.shift[g].sem, a.shift[g].at(b, 16))
            if a.masked and g == 0:
                pe.wait_ge(a.mbT_ready.sem, a.mbT_ready.at(b, 1))
        out = ps[:, ST + (UNITS * g + u) % DEEP, :]
        ins = pe.matmul(out, mem.kst[g][0:KROWS, h, kt * P:(kt + 1) * P], mem.qst[g][0:KROWS, h, :],
                        start=True, stop=not a.masked)
        if a.masked:
            for t in range(T):
                ins = pe.matmul(out[:, t * P:(t + 1) * P], mem.mbT[:, t, kt * P:(kt + 1) * P], mem.identb[:, :],
                                start=False, stop=(t == T - 1))
        ins.then_inc(a.st_ps.sem, 1)

    def products(G, g, kt):
        pe.wait_ge(a.p_exp.sem, a.p_exp.at(G, HG * (kt + 1)))
        if kt == 0:
            pe.wait_ge(a.vg_ready.sem, a.vg_ready.at(G, 1))
            pe.wait_ge(a.ot_sb.sem, a.ot_sb.at(G))
        for h in range(HG):
            ins = pe.matmul(ps[h * VW:(h + 1) * VW, OB, :], mem.vg[g % 2][:, kt, h, :], mem.probs[:, kt, h, :],
                            start=(kt == 0), stop=(kt == T - 1))
        ins.then_inc(a.pv.sem, 1)

    def maxima(G):
        pe.wait_ge(a.m_lo.sem, a.m_lo.at(G, 1))
        take_misc()
        for t in range(T):
            ins = pe.transpose(ps[0:PARTS * HG, MISC, t * P // 2:(t + 1) * P // 2].bitcast(BF16),
                               mem.mparts[:, t, :, :].rearrange("p a h -> p (a h)"), mem.identb[:, :])
        ins.then_inc(a.m_ps.sem, 1)
        misc[0] = (a.m_sb.sem, a.m_sb.at(G, 1))

    def turn(G):
        pe.wait_ge(a.ot_sb.sem, a.ot_sb.at(G, 1))
        take_misc()
        for t in range(T):
            ins = pe.transpose(ps[:, MISC, t * P:(t + 1) * P], mem.ot[:, t * P:(t + 1) * P], mem.ident[:, :])
        ins.then_inc(a.ot_ps.sem, 1)
        misc[0] = (a.o_ready.sem, a.o_ready.at(G, 1))

    def turn_out(b, c):
        pe.wait_ge(a.o_ready.sem, a.o_ready.at(NG * b + NG - 1, 1))
        take_misc()
        for t in range(T):
            ins = pe.transpose(ps[:, MISC, t * P:(t + 1) * P], mem.o[:, t, c * P:(c + 1) * P], mem.ident[:, :])
        ins.then_inc(a.oT_ps.sem, 1)
        misc[0] = (a.oT_sb.sem, a.oT_sb.at(b, c + 1))

    def project_out(b, t):
        pe.wait_ge(a.oT_sb.sem, a.oT_sb.at(b, C))
        if t % 2 == 0:
            take_misc()
        for c in range(C):
            ins = pe.matmul(ps[:, MISC, t % 2 * D:(t % 2 + 1) * D], mem.oT[:, c, t * P:(t + 1) * P],
                            a.w[:, 3, c, :], start=(c == 0), stop=(c == C - 1))
        if t % 2:
            ins.then_inc(a.op_ps.sem, 1)
        misc[0] = (a.op_used.sem, a.op_used.at(b, t // 2 + 1))

    def body(b, first, last):
        if not first:
            misc[0] = (a.o_ready.sem, a.o_ready.at(NG * b - 2, 1))
        for g in range(NG):
            G = NG * b + g
            for u in range(UNITS):
                transposed_scores(b, g, u, first)
                if not (last and g >= 2):
                    s = (g + 2) % NG
                    if u == 0:
                        pe.wait_ge(a.stacks[s].sem, a.stacks[s].at(b if g < 2 else b + 1, 32))
                    used = before(b, UNITS * g + u)
                    scores(G + 2, s, u, (used[0] + 2, used[1]))
                at = u - HG - LATE + 1
                if at < 0 and u == LATE - 1 and not (first and g == 0):
                    products(G - 1, (g - 1) % NG, T - 1)
                if at >= 0 and at % HG == 0:
                    products(G, g, at // HG)
                if g == 1 and not first and u in OUT_TURNS:
                    turn_out(b - 1, OUT_TURNS.index(u))
                if u == M_STEP and not (last and g == NG - 1):
                    maxima(G + 1)
                if u == TURN_STEP and not (first and g == 0):
                    turn(G - 1)
                if (g, u) in OUT_TILES and not first:
                    project_out(b - 1, OUT_TILES.index((g, u)))

    pe.sem_inc(a.pv.sem, a.pv.lead)
    pe.sem_inc(a.ot_ps.sem, a.ot_ps.lead)
    pe.wait_ge(a.lo.sem, a.lo.at(B))
    pe.wait_ge(a.v_ready.sem, a.v_ready.at(B))
    for G in range(2):
        pe.wait_ge(a.stacks[G].sem, a.stacks[G].at(0, 32))
        for v in range(UNITS):
            n = UNITS * G + v
            scores(G, G, v, divmod(n - DEEP, UNITS) if n >= DEEP else None)
    maxima(0)
    body(0, True, False)
    with pe.Fori(1, B - 1) as b:
        body(b, False, False)
    body(B - 1, False, True)
    G = B * NG - 1
    products(G, NG - 1, T - 1)
    turn(G)
    for c in range(C):
        turn_out(B - 1, c)
    for t in range(T):
        project_out(B - 1, t)


def attend_vector(dve, a):
    mem = a.mem
    ps = mem.ps

    def top(G, g, v):
        h, t = v // T, v % T
        bank = SB + (UNITS * (g + 2) + v) % ROUND % DEEP
        out = mem.m[:, 0, t, h:h + 1]
        if a.masked:
            wait_alone(dve, a.s_ps.sem, a.s_ps.at(G, v + 1), a.passed["dve"])
            ins = dve.tensor_tensor_reduce(mem.junk[bank - SB], ps[:, bank, :], mem.mbS[:, t, :], 1.0, FLOOR, ALU.add,
                                           ALU.max, out)
        else:
            dve.wait_ge(a.s_ps.sem, a.s_ps.at(G, v + 1))
            ins = dve.tensor_reduce(out, ps[:, bank, :], AX.X, ALU.max)
        ins.then_inc(a.s_max.sem, 1)

    def split(G):
        dve.wait_ge(a.s_max.sem, a.s_max.at(G, HG * T))
        if not (type(G) is int and G < 1):
            dve.wait_ge(a.m_ps.sem, a.m_ps.at(G))
        m = mem.m[:, 0, :, :]
        hi, mid, lo = (mem.mparts[:, :, i, :] for i in range(PARTS))
        dve.tensor_scalar(hi, m, -1.0, None, ALU.mult).then_inc(a.m_hi.sem, 1)
        dve.wait_ge(a.m_hi.sem, a.m_hi.at(G, 1))
        dve.scalar_tensor_tensor(mem.mres[:, :, :], m, -1.0, hi, ALU.mult, ALU.subtract).then_inc(a.m_res.sem, 1)
        dve.wait_ge(a.m_res.sem, a.m_res.at(G, 1))
        dve.tensor_copy(mid, mem.mres[:, :, :]).then_inc(a.m_mid.sem, 1)
        dve.wait_ge(a.m_mid.sem, a.m_mid.at(G, 1))
        dve.tensor_tensor(lo, mem.mres[:, :, :], mid, ALU.subtract).then_inc(a.m_lo.sem, 1)

    def normalise(G, b, g, first):
        dve.wait_ge(a.ot_ps.sem, a.ot_ps.at(G, 1))
        if g == 0 and not first:
            dve.wait_ge(a.oT_ps.sem, a.oT_ps.at(b - 1, C))
        got = ps[:, MISC, :].rearrange("p (t h d) -> p t h d", t=T, h=HG)
        dve.tensor_scalar(mem.den[:, :, :], got[:, :, :, DK], 1e-30, None, ALU.max).then_inc(a.den.sem, 1)
        dve.wait_ge(a.den.sem, a.den.at(G, 1))
        dve.reciprocal(mem.rden[:, :, :], mem.den[:, :, :]).then_inc(a.rden.sem, 1)
        dve.wait_ge(a.rden.sem, a.rden.at(G, 1))
        out = mem.o[:, :, g * GW:(g + 1) * GW].rearrange("p t (h d) -> p t h d", h=HG)
        dve.tensor_tensor(out, got[:, :, :, 0:DK], mem.rden[:, :, :].unsqueeze(3).to_broadcast([P, T, HG, DK]),
                          ALU.mult).then_inc(a.o_ready.sem, 1)

    def residual(b, k):
        two = slice(2 * k, 2 * k + 2)
        x = mem.x[:, b, two, :]
        got = ps[:, MISC, :].rearrange("p (t d) -> p t d", t=2)
        row = None if a.rows is None else mem.rows[:, a.rows + 1:a.rows + 2, :].to_broadcast([P, 2, D])
        if not a.self_block:
            dve.wait_ge(a.op_ps.sem, a.op_ps.at(b, k + 1))
            ins = dve.tensor_tensor(x, got, x, ALU.add)
            ins.then_inc(a.op_used.sem, 1)
            if row is not None:
                dve.wait_ge(a.op_used.sem, a.op_used.at(b, k + 1))
                dve.tensor_tensor(x, x, row, ALU.add)
            return
        y, u = mem.total_x[:, two, :], mem.block_in[:, two, :]
        for t in range(2 * k, 2 * k + 2):
            ins = dve.tensor_scalar(mem.block_in[:, t, :], mem.x[:, b, t, :], mem.mv_in[:, b, t, 0:1],
                                    mem.rstd_in[:, b, t:t + 1], ALU.subtract, ALU.mult)
        ins.then_inc(a.step[0].sem, 1)
        dve.wait_ge(a.step[0].sem, a.step[0].at(b, k + 1))
        dve.tensor_tensor(u, u, row, ALU.add).then_inc(a.step[1].sem, 1)
        dve.wait_ge(a.step[1].sem, a.step[1].at(b, k + 1))
        dve.wait_ge(a.op_ps.sem, a.op_ps.at(b, k + 1))
        dve.tensor_tensor(u, got, u, ALU.add).then_inc(a.op_used.sem, 1)
        dve.wait_ge(a.op_used.sem, a.op_used.at(b, k + 1))
        dve.wait_ge(a.acc_stored.sem, a.acc_stored.at(b))
        dve.tensor_tensor(y, x, u, ALU.add).then_inc(a.acc_ready.sem, 1)
        wait_alone(dve, a.acc_ready.sem, a.acc_ready.at(b, k + 1), a.passed["dve"])
        dve.tensor_copy(x, u).then_inc(a.step[2].sem, 1)

    def mask_of(b, which):
        if which == "S":
            dve.tensor_copy(mem.mbS[:, :, :], mem.mb_all[:, b, :, :]).then_inc(a.mbS_ready.sem, 1)
            dve.wait_ge(a.mbS_ready.sem, a.mbS_ready.at(b, 1))
        else:
            if type(b) is not int or b:
                wait_alone(dve, a.st_ps.sem, a.st_ps.at(NG * b), a.passed["dve"])
            dve.tensor_copy(mem.mbT[:, :, :], mem.mb_all[:, b, :, :]).then_inc(a.mbT_ready.sem, 1)

    def body(b, first, last):
        for g in range(NG):
            G = NG * b + g
            if a.masked and g == 0 and not first:
                mask_of(b, "T")
            if a.masked and g == 2 and not last:
                mask_of(b + 1, "S")
            for u in range(UNITS):
                if not (last and g >= 2):
                    top(G + 2, (g + 2) % NG, u)
                if u == TURN_STEP + 1 and not (first and g == 0):
                    normalise(G - 1, b if g else b - 1, (g - 1) % NG, first)
                if not first and (g, u - 1) in OUT_TILES[1::2]:
                    residual(b - 1, OUT_TILES[1::2].index((g, u - 1)))
            if not (last and g >= 2):
                split(G + 2)

    if a.masked:
        dve.wait_ge(a.mask_bias.sem, a.mask_bias.at(B))
        mask_of(0, "S")
        mask_of(0, "T")
    for G in range(2):
        for v in range(UNITS):
            top(G, G, v)
        split(G)
    body(0, True, False)
    with dve.Fori(1, B - 1) as b:
        body(b, False, False)
    body(B - 1, False, True)
    normalise(B * NG - 1, B - 1, NG - 1, False)
    residual(B - 1, 0)
    residual(B - 1, 1)




class Mixture:

    def __init__(self, nc, ctx, stage, mem, dram, name, affine, gate_width, row, hidden):
        self.mem, self.dram, self.name, self.affine = mem, dram, name, affine
        self.width, self.row, self.hidden = gate_width, row, hidden

        self.used = []

        def sig(what, per, lead=0, kept=stage):
            self.used.append(kept.enter_context(nc.semaphore(f"{name}_{what}")))
            return Signal(self.used[-1], per, lead)

        self.passed = {eng: stage.enter_context(nc.semaphore(f"{name}_{eng}_passed")) for eng in ("dve", "pool")}
        self.stat = sig("stat", T)
        self.aggr = sig("aggr", T)
        self.vare = sig("vare", 1)
        self.rs = sig("rs", 1)
        self.rn_ready = sig("rn_ready", T)
        self.rn_stored = sig("rn_stored", 16, 16)
        self.rnT_ps = sig("rnT_ps", C, C)
        self.rnT_ready = sig("rnT_ready", C, C)
        self.g_ps = sig("g_ps", 2, 2)
        self.logit = sig("logit", 2, 2)
        self.top = sig("top", T)
        self.index = sig("index", T)
        self.chosen = sig("chosen", 1)
        self.ntop = sig("ntop", 1)
        self.exps = sig("exps", T, T)
        self.prob = sig("prob", 1)
        self.route = sig("route", 1)
        self.onehot = sig("onehot", 1)
        self.counts = sig("counts", 1)
        self.routed = sig("routed", 1)
        self.cleared = sig("cleared", 16)
        self.scattered = sig("scattered", 16, kept=ctx)
        self.inv_loaded = sig("inv_loaded", 16)
        self.weights = sig("weights", 16)
        self.gathered = [sig(f"gathered{j}", 16, kept=ctx) for j in range(2)]
        self.tx_ps = sig("tx_ps", 1, 2)
        self.xT_ready = sig("xT_ready", 1, 1)
        self.h_ps = sig("h_ps", 2)
        self.mid_ready = sig("mid_ready", 2, 2)
        self.tm_ps = sig("tm_ps", 2, 2)
        self.midT_ready = sig("midT_ready", 2, 2)
        self.y_ps = sig("y_ps", 1, 1)
        self.y_sum = sig("y_sum", 1, 1)
        self.y_ready = sig("y_ready", 1)
        self.y_stored = [sig(f"y_stored{j}", 16, 16) for j in range(2)]
        self.fetched = sig("fetched", 16, kept=ctx)
        self.acc_loaded = sig("acc_loaded", 16)
        self.x_ready = sig("x_ready", 1)
        self.out_stored = sig("out_stored", 16)


def gate_vector(dve, m):
    mem = m.mem
    ps = mem.ps
    dve.sem_inc(m.logit.sem, m.logit.lead)
    with dve.Fori(0, B) as b:
        for t in range(T):
            dve.bn_stats(mem.stats[:, t, :], mem.x[:, b, t, :]).then_inc(m.stat.sem, 1)
        for t in range(T):
            wait_alone(dve, m.stat.sem, m.stat.at(b, t + 1), m.passed["dve"])
            dve.bn_aggr(mem.mv[:, t, :], mem.stats[:, t, :]).then_inc(m.aggr.sem, 1)
        dve.wait_ge(m.rs.sem, m.rs.at(b, 1))
        dve.wait_ge(m.rnT_ps.sem, m.rnT_ps.at(b))
        dve.wait_ge(m.rn_stored.sem, m.rn_stored.at(b))
        for t in range(T):
            dve.tensor_scalar(mem.rn[:, t, :], mem.x[:, b, t, :], mem.mv[:, t, 0:1], mem.rstd[:, t:t + 1],
                              ALU.subtract, ALU.mult).then_inc(m.rn_ready.sem, 1)
        if m.hidden is None:
            dve.wait_ge(m.exps.sem, m.exps.at(b))
        for k in range(2):
            dve.wait_ge(m.g_ps.sem, m.g_ps.at(b, k + 1))
            got = ps[:, 2 + k, 0:2 * m.width].rearrange("p (t d) -> p t d", t=2)
            row = mem.rows[:, m.row:m.row + 1, 0:m.width].to_broadcast([P, 2, m.width])
            dve.tensor_tensor(mem.logits[:, 2 * k:2 * k + 2, 0:m.width], got, row, ALU.add).then_inc(m.logit.sem, 1)
        for t in range(T):
            wait_alone(dve, m.logit.sem, m.logit.at(b, t // 2 + 1), m.passed["dve"])
            dve.max(mem.top8[:, t, :], mem.logits[:, t, 0:m.width]).then_inc(m.top.sem, 1)
        for t in range(T):
            wait_alone(dve, m.top.sem, m.top.at(b, t + 1), m.passed["dve"])
            dve.max_index(mem.idx8[:, t, :], mem.top8[:, t, :], mem.logits[:, t, 0:m.width]).then_inc(m.index.sem, 1)
        dve.wait_ge(m.index.sem, m.index.at(b, T))
        dve.tensor_scalar(mem.expert_u[:, :], mem.idx8[:, :, 0], E - 1, None, ALU.bitwise_and).then_inc(m.chosen.sem, 1)
        wait_alone(dve, m.chosen.sem, m.chosen.at(b, 1), m.passed["dve"])
        dve.tensor_copy(mem.expert[:, b, :], mem.expert_u[:, :])
        if m.hidden is None:
            dve.tensor_scalar(mem.ntop[:, :], mem.top8[:, :, 0], -1.0, None, ALU.mult).then_inc(m.ntop.sem, 1)
            dve.wait_ge(m.exps.sem, m.exps.at(b, T))
            dve.reciprocal(mem.prob[:, b, :], mem.sum[:, :]).then_inc(m.prob.sem, 1)


def gate_gpsimd(pool, m):
    mem = m.mem
    with pool.Fori(0, B) as b:
        wait_alone(pool, m.aggr.sem, m.aggr.at(b, T), m.passed["pool"])
        pool.tensor_scalar(mem.var[:, :], mem.mv[:, :, 1], EPS, None, ALU.add).then_inc(m.vare.sem, 1)
        pool.wait_ge(m.vare.sem, m.vare.at(b, 1))
        pool.tensor_tensor(mem.rstd[:, :], mem.var[:, :], mem.neghalf[:, :], ALU.pow).then_inc(m.rs.sem, 1)


def gate_scalar(act, m):
    mem = m.mem
    ps = mem.ps
    act.sem_inc(m.rnT_ready.sem, m.rnT_ready.lead)
    act.sem_inc(m.exps.sem, m.exps.lead)
    with act.Fori(0, B) as b:
        for c in range(C):
            act.wait_ge(m.rnT_ps.sem, m.rnT_ps.at(b, c + 1))
            act.wait_ge(m.g_ps.sem, m.g_ps.at(b))
            if m.affine is None:
                ins = act.activation(mem.rnT[:, c, :], ps[:, c, :], ACT.Copy)
            else:
                g, s = m.affine + c, m.affine + C + c
                ins = act.activation(mem.rnT[:, c, :], ps[:, c, :], ACT.Identity, bias=mem.cols[:, s:s + 1],
                                     scale=mem.cols[:, g:g + 1])
            ins.then_inc(m.rnT_ready.sem, 1)
        if m.hidden is None:
            act.wait_ge(m.ntop.sem, m.ntop.at(b, 1))
            for t in range(T):
                act.activation(mem.exps[:, t, :], mem.logits[:, t, :], ACT.Exp, bias=mem.ntop[:, t:t + 1],
                               accum_out=mem.sum[:, t:t + 1]).then_inc(m.exps.sem, 1)


def gate_tensor(pe, m):
    mem = m.mem
    ps = mem.ps
    pe.sem_inc(m.rnT_ps.sem, m.rnT_ps.lead)
    pe.sem_inc(m.g_ps.sem, m.g_ps.lead)
    with pe.Fori(0, B) as b:
        pe.wait_ge(m.rnT_ready.sem, m.rnT_ready.at(b))
        pe.wait_ge(m.rn_ready.sem, m.rn_ready.at(b, T))
        for c in range(C):
            for t in range(T):
                ins = pe.transpose(ps[:, c, t * P:(t + 1) * P], mem.rn[:, t, c * P:(c + 1) * P], mem.ident[:, :])
            ins.then_inc(m.rnT_ps.sem, 1)
        pe.wait_ge(m.rnT_ready.sem, m.rnT_ready.at(b, C))
        pe.wait_ge(m.logit.sem, m.logit.at(b))
        for k in range(2):
            for t in range(2):
                for c in range(C):
                    ins = pe.matmul(ps[:, 2 + k, t * m.width:(t + 1) * m.width],
                                    mem.rnT[:, c, (2 * k + t) * P:(2 * k + t + 1) * P], mem.gate[:, c, 0:m.width],
                                    start=(c == 0), stop=(c == C - 1))
            ins.then_inc(m.g_ps.sem, 1)


def gate_sync(sp, m):
    mem = m.mem
    sp.sem_inc(m.rn_stored.sem, m.rn_stored.lead)
    with sp.Fori(0, B) as b:
        sp.wait_ge(m.rn_ready.sem, m.rn_ready.at(b, T))
        sp.dma_start(m.dram["rows"].rearrange("(b t p) d -> b p t d", b=B, t=T)[b], mem.rn[:, :, :])\
          .then_inc(m.rn_stored.sem, 16)
    sp.wait_ge(m.rn_stored.sem, m.rn_stored.at(B))


def route_vector(dve, m):
    mem = m.mem
    ps = mem.ps
    done = [0]

    def then(ins):
        done[0] += 1
        ins.then_inc(m.route.sem, 1)
        dve.wait_ge(m.route.sem, done[0])

    expert = mem.expert[:, :, :].rearrange("p b t -> p (b t)")
    dve.tensor_tensor(mem.onehot[:, :, :], expert.unsqueeze(2).to_broadcast([P, NT, E]),
                      mem.count[:, 0:E].unsqueeze(1).to_broadcast([P, NT, E]), ALU.is_equal).then_inc(m.onehot.sem, 1)
    dve.wait_ge(m.counts.sem, 1)
    then(dve.tensor_copy(mem.tiles[:, :, :], ps[:, 1, 0:NT * E].rearrange("p (t e) -> p t e", t=NT)))
    then(dve.memset(mem.place[:, 0, :], 0.0))
    for t in range(1, NT):
        then(dve.tensor_tensor(mem.place[:, t, :], mem.place[:, t - 1, :], mem.tiles[:, t - 1, :], ALU.add))
    then(dve.tensor_tensor(mem.total[:, :], mem.place[:, NT - 1, :], mem.tiles[:, NT - 1, :], ALU.add))
    under = mem.tiles[:, :, :].rearrange("p t e -> p (t e)").rearrange("p (e t) -> p e t", e=E)
    then(dve.tensor_scalar(mem.total[:, :], mem.total[:, :], 1.0 / P, None, ALU.mult))
    then(dve.tensor_tensor(under, mem.total[:, :].unsqueeze(2).to_broadcast([P, E, NT]),
                           mem.count[:, 0:NT].unsqueeze(1).to_broadcast([P, E, NT]), ALU.is_gt))
    then(dve.tensor_reduce(mem.need[:, :], under, AX.X, ALU.add))
    then(dve.tensor_copy(mem.end[:, 0:1], mem.need[:, 0:1]))
    for e in range(1, E):
        then(dve.tensor_tensor(mem.end[:, e:e + 1], mem.end[:, e - 1:e], mem.need[:, e:e + 1], ALU.add))
    then(dve.tensor_tensor(mem.start[:, :], mem.end[:, :], mem.need[:, :], ALU.subtract))
    then(dve.tensor_scalar(mem.start[:, :], mem.start[:, :], float(P), None, ALU.mult))
    then(dve.tensor_tensor(mem.place[:, :, :], mem.place[:, :, :],
                           mem.start[:, :].unsqueeze(1).to_broadcast([P, NT, E]), ALU.add))
    then(dve.tensor_tensor(mem.place[:, :, :], ps[:, 0, 0:NT * E].rearrange("p (t e) -> p t e", t=NT),
                           mem.place[:, :, :], ALU.add))
    then(dve.tensor_tensor(mem.place[:, :, :], mem.place[:, :, :], mem.onehot[:, :, :], ALU.mult))
    then(dve.tensor_reduce(mem.pos[:, :], mem.place[:, :, :], AX.X, ALU.add))
    dve.tensor_copy(mem.pos_u[:, :], mem.pos[:, :]).then_inc(m.routed.sem, 1)
    then(dve.tensor_tensor(mem.more[:, :, :], mem.count[:, 0:SLOTS].unsqueeze(2).to_broadcast([P, SLOTS, E]),
                           mem.end[:, :].unsqueeze(1).to_broadcast([P, SLOTS, E]), ALU.is_ge))
    then(dve.tensor_reduce(mem.slot_f[:, :], mem.more[:, :, :], AX.X, ALU.add))
    dve.tensor_scalar(mem.slot_e[:, :], mem.slot_f[:, :], float(E - 1), None, ALU.min).then_inc(m.routed.sem, 1)


def route_tensor(pe, m):
    mem = m.mem
    pe.wait_ge(m.onehot.sem, 1)
    onehot = mem.onehot[:, :, :].rearrange("p t e -> p (t e)")
    pe.matmul(mem.ps[:, 0, 0:NT * E], mem.tri[:, :], onehot, start=True, stop=True)
    pe.matmul(mem.ps[:, 1, 0:NT * E], mem.ones[:, :], onehot, start=True, stop=True).then_inc(m.counts.sem, 1)


def route_sync(sp, m, nc):
    mem = m.mem
    sp.dma_start(m.dram["inv"].rearrange("(s p) o -> s (p o)", p=P), mem.zero[:, :].bitcast(U32)).then_inc(m.cleared.sem, 16)
    sp.wait_ge(m.scattered.sem, 16 * NT)
    with nc.allow_non_contiguous_dma(reason="a table of four-byte indices, turned"):
        sp.dma_start(mem.inv[:, :], m.dram["inv"].rearrange("(s p) o -> p (s o)", p=P)).then_inc(m.inv_loaded.sem, 16)
    sp.wait_ge(m.inv_loaded.sem, 16)


def route_gpsimd(pool, m):
    mem = m.mem
    pool.wait_ge(m.cleared.sem, 16)
    pool.wait_ge(m.routed.sem, 1)
    for t in range(NT):
        pool.indirect_dma_start(m.dram["inv"], bass.IndirectOffsetOnAxis(ap=mem.pos_u[:, t:t + 1], axis=0),
                                mem.token[:, t:t + 1].bitcast(U32), None).then_inc(m.scattered.sem, 16)


def expert_of(eng, m, s):
    return eng.value_load(m.mem.slot_e[0:1, bass.ds(s, 1)], min_val=0, max_val=E - 1)


def each_slot(eng, body):
    pairs = (SLOTS - 3) // 2
    with eng.Fori(0, pairs) as i:
        for j in range(2):
            body(i * 2 + j, j, i)
    for s in range(2 * pairs, SLOTS):
        body(s, s % 2, s // 2)


def expert_sync(sp, m):
    mem = m.mem
    for j in range(2):
        sp.sem_inc(m.y_stored[j].sem, m.y_stored[j].lead)
    out = m.dram["y"].rearrange("(s p) d -> s p d", p=P)

    def body(s, j, i):
        ready = m.y_sum if m.hidden is not None else m.y_ready
        sp.wait_ge(ready.sem, ready.at(s, 1))
        sp.dma_start(out[s], mem.y[j]).then_inc(m.y_stored[j].sem, 16)

    each_slot(sp, body)
    for j in range(2):
        sp.wait_ge(m.y_stored[j].sem, m.y_stored[j].at((SLOTS + 1 - j) // 2))


def expert_gpsimd(pool, m):
    mem = m.mem
    for s in range(SLOTS):
        if s >= 2:
            pool.wait_ge(m.tx_ps.sem, m.tx_ps.at(s - 1))
        pool.indirect_dma_start(mem.xg[s % 2], None, m.dram["rows"],
                                bass.IndirectOffsetOnAxis(ap=mem.inv[:, s:s + 1], axis=0))\
            .then_inc(m.gathered[s % 2].sem, 16)


def expert_scalar(act, m):
    mem = m.mem
    ps = mem.ps
    act.sem_inc(m.xT_ready.sem, m.xT_ready.lead)
    act.sem_inc(m.midT_ready.sem, m.midT_ready.lead)

    def turned(s, j):
        act.wait_ge(m.tx_ps.sem, m.tx_ps.at(s, 1))
        if m.hidden is None:
            act.wait_ge(m.y_ps.sem, m.y_ps.at(s - 1))
            act.activation(mem.xT[j].rearrange("p c n -> p (c n)"), ps[:, 0, 0:C * P], ACT.Copy)\
               .then_inc(m.xT_ready.sem, 1)
            return
        for c in range(C):
            g, sh = m.affine + c, m.affine + C + c
            ins = act.activation(mem.xT[j][:, c, :], ps[:, 0, c * P:(c + 1) * P], ACT.Identity,
                                 bias=mem.cols[:, sh:sh + 1], scale=mem.cols[:, g:g + 1])
        ins.then_inc(m.xT_ready.sem, 1)

    def hidden(s):
        e = expert_of(act, m, s)
        act.wait_ge(m.y_ps.sem, m.y_ps.at(s))
        for f in range(FT):
            if f % 4 == 0:
                act.wait_ge(m.tm_ps.sem, m.tm_ps.at(s, f // 4 + 1))
            ins = act.activation(mem.midT[:, f, :], ps[:, 3 + f // 4, (f % 4) * P:(f % 4 + 1) * P], ACT.Relu,
                                 bias=mem.b1c[:, bass.ds(e * FT + f, 1)])
            if f % 4 == 3:
                ins.then_inc(m.midT_ready.sem, 1)

    def body(s, j, i):
        if m.hidden is not None:
            hidden(s)
        if type(s) is not int or s + 2 < SLOTS:
            turned(s + 2, j)

    turned(0, 0)
    turned(1, 1)
    each_slot(act, body)


def expert_vector(dve, m):
    mem = m.mem
    ps = mem.ps
    dve.sem_inc(m.mid_ready.sem, m.mid_ready.lead)
    dve.sem_inc(m.y_sum.sem, m.y_sum.lead)

    def hidden(s):
        for k in range(2):
            dve.wait_ge(m.h_ps.sem, m.h_ps.at(s, k + 1))
            if k == 0:
                dve.wait_ge(m.tm_ps.sem, m.tm_ps.at(s))
            dve.tensor_copy(mem.mid[:, k * 512:(k + 1) * 512], ps[:, 1 + k, :]).then_inc(m.mid_ready.sem, 1)

    def out(s, j, i):
        e = expert_of(dve, m, s)
        dve.wait_ge(m.y_ps.sem, m.y_ps.at(s, 1))
        dve.wait_ge(m.y_stored[j].sem, m.y_stored[j].at(i))
        bias = mem.b2[:, bass.ds(e, 1), :].rearrange("p e d -> p (e d)")
        dve.tensor_tensor(mem.y[j], ps[:, 5, 0:D], bias, ALU.add).then_inc(m.y_sum.sem, 1)
        if m.hidden is None:
            dve.wait_ge(m.y_sum.sem, m.y_sum.at(s, 1))
            dve.tensor_scalar(mem.y[j], mem.y[j], 0.0, None, ALU.max).then_inc(m.y_ready.sem, 1)

    def body(s, j, i):
        if m.hidden is not None and (type(s) is not int or s + 1 < SLOTS):
            hidden(s + 1)
        out(s, j, i)

    if m.hidden is not None:
        hidden(0)
    each_slot(dve, body)


def expert_tensor(pe, m):
    mem = m.mem
    ps = mem.ps
    pe.sem_inc(m.tx_ps.sem, m.tx_ps.lead)
    pe.sem_inc(m.tm_ps.sem, m.tm_ps.lead)
    pe.sem_inc(m.y_ps.sem, m.y_ps.lead)
    pe.wait_ge(m.weights.sem, m.weights.at(0, 48 if m.hidden is not None else 32))

    def turn_in(s, j, i):
        pe.wait_ge(m.gathered[j].sem, m.gathered[j].at(i, 16))
        pe.wait_ge(m.xT_ready.sem, m.xT_ready.at(s))
        for c in range(C):
            ins = pe.transpose(ps[:, 0, c * P:(c + 1) * P], mem.xg[j][:, c * P:(c + 1) * P], mem.ident[:, :])
        ins.then_inc(m.tx_ps.sem, 1)

    def up(s, j):
        e = expert_of(pe, m, s)
        pe.wait_ge(m.xT_ready.sem, m.xT_ready.at(s, 1))
        pe.wait_ge(m.mid_ready.sem, m.mid_ready.at(s))
        for k in range(2):
            for c in range(C):
                w = mem.w1[:, c, bass.ds(e, 1), k * 512:(k + 1) * 512].rearrange("p e f -> p (e f)")
                ins = pe.matmul(ps[:, 1 + k, :], mem.xT[j][:, c, :], w, start=(c == 0), stop=(c == C - 1))
            ins.then_inc(m.h_ps.sem, 1)

    def turn_mid(s):
        pe.wait_ge(m.midT_ready.sem, m.midT_ready.at(s))
        for f in range(FT):
            if f % 4 == 0:
                pe.wait_ge(m.mid_ready.sem, m.mid_ready.at(s, f // 4 + 1))
            ins = pe.transpose(ps[:, 3 + f // 4, (f % 4) * P:(f % 4 + 1) * P], mem.mid[:, f * P:(f + 1) * P],
                               mem.ident[:, :])
            if f % 4 == 3:
                ins.then_inc(m.tm_ps.sem, 1)

    def down(s, j):
        e = expert_of(pe, m, s)
        pe.wait_ge(m.y_sum.sem, m.y_sum.at(s))
        if m.hidden is None:
            pe.wait_ge(m.xT_ready.sem, m.xT_ready.at(s, 1))
            for c in range(C):
                w = mem.we[:, c, bass.ds(e, 1), :].rearrange("p e d -> p (e d)")
                ins = pe.matmul(ps[:, 5, 0:D], mem.xT[j][:, c, :], w, start=(c == 0), stop=(c == C - 1))
        else:
            for f in range(FT):
                if f % 4 == 0:
                    pe.wait_ge(m.midT_ready.sem, m.midT_ready.at(s, f // 4 + 1))
                w = mem.w2[:, f, bass.ds(e, 1), :].rearrange("p e d -> p (e d)")
                ins = pe.matmul(ps[:, 5, 0:D], mem.midT[:, f, :], w, start=(f == 0), stop=(f == FT - 1))
        ins.then_inc(m.y_ps.sem, 1)

    def body(s, j, i):
        if m.hidden is not None:
            turn_mid(s)
            if type(s) is not int or s + 1 < SLOTS:
                up(s + 1, 1 - j)
        down(s, j)
        if type(s) is not int or s + 2 < SLOTS:
            turn_in(s + 2, j, i + 1)

    turn_in(0, 0, 0)
    if m.hidden is not None:
        up(0, 0)
    turn_in(1, 1, 0)
    each_slot(pe, body)


def combine_gpsimd(pool, m):
    mem = m.mem
    for t in range(NT):
        pool.indirect_dma_start(mem.yg[:, t, :], None, m.dram["y"],
                                bass.IndirectOffsetOnAxis(ap=mem.pos_u[:, t:t + 1], axis=0)).then_inc(m.fetched.sem, 16)


def combine_sync(sp, m, out):
    mem = m.mem
    if m.hidden is not None:
        for b in range(B):
            sp.dma_start(mem.x[:, b, :, :], m.dram["acc"][b]).then_inc(m.acc_loaded.sem, 16)
    if out is not None:
        for b in range(B):
            sp.wait_ge(m.x_ready.sem, b + 1)
            sp.dma_start(out[b].rearrange("(t p) d -> p t d", p=P), mem.x[:, b, :, :]).then_inc(m.out_stored.sem, 16)
        sp.wait_ge(m.out_stored.sem, 16 * B)


def combine_vector(dve, m):
    mem = m.mem
    dve.wait_ge(m.fetched.sem, 16 * NT)
    if m.hidden is not None:
        dve.wait_ge(m.acc_loaded.sem, 16 * B)
    for b in range(B):
        if m.hidden is not None:
            ins = dve.tensor_tensor(mem.x[:, b, :, :], mem.x[:, b, :, :], mem.yg[:, b * T:(b + 1) * T, :], ALU.add)
        else:
            for t in range(T):
                ins = dve.scalar_tensor_tensor(mem.x[:, b, t, :], mem.yg[:, b * T + t, :], mem.prob[:, b, t:t + 1],
                                               mem.x[:, b, t, :], ALU.mult, ALU.add)
        ins.then_inc(m.x_ready.sem, 1)



WA, WB, WC = 0, 1, 0


def program(nc, x, ctx_in, mask, wa, wb, wc, cols, rows, b1c, b2, gate0, w1, w2, gate1, we, be, out):
    dram = {
        "ctx": ctx_in.rearrange("b (t p) d -> b p t d", p=P),
        "mask": mask.rearrange("b o (t p) k -> b p (o t) k", p=P),
        "q": nc.dram_tensor("q_parts", (B, D, TERMS, S), BF16, kind="Internal").ap(),
        "k": nc.dram_tensor("k_parts", (B, D, TERMS, S), BF16, kind="Internal").ap(),
        "acc": nc.dram_tensor("residual", (B, P, T, D), F32, kind="Internal").ap(),
        "rows": nc.dram_tensor("token_rows", (NT * P, D), F32, kind="Internal").ap(),
        "inv": nc.dram_tensor("slot_tokens", (SLOTS * P, 1), U32, kind="Internal").ap(),
        "y": nc.dram_tensor("slot_out", (SLOTS * P, D), F32, kind="Internal").ap(),
    }
    with ExitStack() as ctx:
        mem = Memory(nc, ctx)
        loaded = ctx.enter_context(nc.semaphore("loaded"))
        setup = ctx.enter_context(nc.semaphore("setup"))

        with nc.Block() as block:

            @block.sync
            def _(sp):
                for b in range(B):
                    sp.dma_start(mem.x[:, b, :, :], x[b].rearrange("(t p) d -> p t d", p=P)).then_inc(loaded, 16)
                sp.dma_start(mem.w[WA][:, :, :, :], wa).then_inc(loaded, 16)
                sp.dma_start(mem.cols[:, :], cols).then_inc(loaded, 16)
                sp.dma_start(mem.rows[:, :, :], rows[0]).then_inc(loaded, 16)
                sp.dma_start(mem.b1c[:, :], b1c).then_inc(loaded, 16)
                sp.dma_start(mem.w[WB][:, :, :, :], wb).then_inc(loaded, 16)
                sp.dma_start(mem.gate[:, :, 0:E], gate0).then_inc(loaded, 16)
                sp.wait_ge(loaded, 16 * (B + 6))

            @block.gpsimd
            def _(pool):
                pool.memset(mem.ident[:, :], 0.0).then_inc(setup, 1)
                pool.memset(mem.identb[:, :], 0.0).then_inc(setup, 1)
                pool.memset(mem.ones[:, :], 1.0).then_inc(setup, 1)
                pool.memset(mem.tri[:, :], 1.0).then_inc(setup, 1)
                pool.memset(mem.neghalf[:, :], -0.5).then_inc(setup, 1)
                pool.memset(mem.zero[:, :], 0).then_inc(setup, 1)
                pool.iota(mem.count_i[:, :], [[1, SLOTS + T]], base=0, channel_multiplier=0).then_inc(setup, 1)
                pool.iota(mem.token[:, :], [[P, NT]], base=0, channel_multiplier=1).then_inc(setup, 1)
                pool.wait_ge(setup, 8)
                for eye in (mem.ident, mem.identb):
                    pool.affine_select(out=eye[:, :], in_=eye[:, :], compare_op=ALU.not_equal, fill=1.0, base=0,
                                       pattern=[[-1, P]], channel_multiplier=1).then_inc(setup, 1)
                pool.affine_select(out=mem.tri[:, :], in_=mem.tri[:, :], compare_op=ALU.is_gt, fill=0.0, base=0,
                                   pattern=[[1, P]], channel_multiplier=-1).then_inc(setup, 1)
                pool.tensor_copy(mem.count[:, :], mem.count_i[:, :]).then_inc(setup, 1)
                pool.wait_ge(setup, 12)

        def cleared(stage):
            with nc.Block() as block:
                @block.gpsimd
                def _(pool):
                    for sem in (*stage.used, *stage.passed.values()):
                        pool.sem_clear(sem)

        def attention(*what):
            with ExitStack() as stage:
                a = Attention(nc, ctx, stage, mem, dram, *what)
                attention_blocks(a)
                cleared(a)

        def mixture(*what, loads, result=None):
            with ExitStack() as stage:
                m = Mixture(nc, ctx, stage, mem, dram, *what)
                mixture_blocks(m, loads, result)
                if result is None:
                    cleared(m)

        def attention_blocks(a, meanwhile=None):
            with nc.Block() as block:
                @block.sync
                def _(sp):
                    project_sync(sp, a)
                    attend_sync(sp, a, meanwhile)

                @block.gpsimd
                def _(pool):
                    project_gpsimd(pool, a)
                    attend_gpsimd(pool, a)

                @block.scalar
                def _(act):
                    project_scalar(act, a)
                    attend_scalar(act, a)

                @block.vector
                def _(dve):
                    project_vector(dve, a)
                    attend_vector(dve, a)

                @block.tensor
                def _(pe):
                    project_tensor(pe, a)
                    attend_tensor(pe, a)

        def mixture_blocks(m, loads, result):
            with nc.Block() as block:
                @block.sync
                def _(sp):
                    for dst, src in loads:
                        sp.dma_start(dst, src).then_inc(m.weights.sem, 16)
                    gate_sync(sp, m)
                block.gpsimd(lambda pool: gate_gpsimd(pool, m))
                block.scalar(lambda act: gate_scalar(act, m))
                block.vector(lambda dve: gate_vector(dve, m))
                block.tensor(lambda pe: gate_tensor(pe, m))
            with nc.Block() as block:
                block.sync(lambda sp: route_sync(sp, m, nc))
                block.gpsimd(lambda pool: route_gpsimd(pool, m))
                block.vector(lambda dve: route_vector(dve, m))
                block.tensor(lambda pe: route_tensor(pe, m))
            with nc.Block() as block:
                block.sync(lambda sp: expert_sync(sp, m))
                block.gpsimd(lambda pool: expert_gpsimd(pool, m))
                block.scalar(lambda act: expert_scalar(act, m))
                block.vector(lambda dve: expert_vector(dve, m))
                block.tensor(lambda pe: expert_tensor(pe, m))
            with nc.Block() as block:
                block.sync(lambda sp: combine_sync(sp, m, result))
                block.gpsimd(lambda pool: combine_gpsimd(pool, m))
                block.vector(lambda dve: combine_vector(dve, m))

        attention("a", WA, True, 1, None, {"qk": 0}, None, True, False)
        attention("b", WB, False, 2, 12, {"qk": 4}, 0, False, True)
        mixture("e", 16, E, 4, F, loads=[(mem.w1, w1), (mem.w2, w2), (mem.b2, b2)])
        with nc.Block() as block:
            @block.sync
            def _(sp):
                sp.dma_start(mem.w[WC][:, :, :, :], wc).then_inc(loaded, 16)
                sp.dma_start(mem.gate[:, :, :], gate1).then_inc(loaded, 16)
                sp.dma_start(mem.rows[:, :, :], rows[1]).then_inc(loaded, 16)
                sp.wait_ge(loaded, 16 * (B + 9))
        attention("c", WC, True, 1, None, {"qk": 8}, 2, False, False)
        mixture("f", None, D, 4, None, loads=[(mem.we, we), (mem.b2, be)], result=out)


def kernel(**inputs):
    import concourse.bacc as bacc
    from concourse.bass_utils import run_bass_kernel_spmd

    a = {k: np.asarray(v) for k, v in inputs.items()}

    def weight(w):
        return w.reshape(C, P, -1).transpose(1, 0, 2)

    def weights(names, turned):
        return np.ascontiguousarray(np.stack([weight(a[n].T if turned else a[n]) for n in names], 1))

    def col(v):
        return v.reshape(C, P).T

    def row(v):
        return np.broadcast_to(np.pad(v, (0, D - v.size)), (P, D))

    zero = np.zeros(D, np.float32)
    f0, x1, f1 = "L0_ffn_", "L1_xattn_", "L1_ffn_"
    arrays = {
        "x": a["x"], "ctx": a["ctx_1024"], "mask": a["mask_Bx1xSxS2_ik0"],
        "wa": weights(["L0_xattn_W_Q", "L0_xattn_W_K", "L0_xattn_W_V", "L0_xattn_W_O"], True),
        "wb": weights([f0 + "wq", f0 + "wk", f0 + "wv", f0 + "wo"], False),
        "wc": weights([x1 + "Wq", x1 + "Wk", x1 + "Wv", x1 + "Wo"], True),
        "cols": np.concatenate([col(v) for v in (
            zero, zero, a[f0 + "bq"], a[f0 + "bk"], a[x1 + "bq"], a[x1 + "bk"],
            a[f0 + "ln1_g"], a[f0 + "ln1_b"], a[f0 + "ln2_g"], a[f0 + "ln2_b"])], 1),
        "rows": np.stack([
            np.stack([row(v) for v in (a[f0 + "bv"], a[f0 + "bo"], zero, zero, a[f0 + "gate_b"])], 1),
            np.stack([row(v) for v in (zero, zero, a[x1 + "bv"], a[x1 + "bo"], a[f1 + "bg"])], 1)]),
        "b1c": a[f0 + "b1"].reshape(E * FT, P).T,
        "b2": np.broadcast_to(a[f0 + "b2"], (P, E, D)),
        "gate0": weight(a[f0 + "gate_w"]),
        "w1": a[f0 + "w1"].reshape(E, C, P, F).transpose(2, 1, 0, 3),
        "w2": a[f0 + "w2"].reshape(E, FT, P, D).transpose(2, 1, 0, 3),
        "gate1": weight(a[f1 + "Wg"]),
        "we": a[f1 + "We"].reshape(E, C, P, D).transpose(2, 1, 0, 3),
        "be": np.broadcast_to(a[f1 + "be"], (P, E, D)),
    }
    arrays = {f"in_{k}": np.ascontiguousarray(v) for k, v in arrays.items()}
    nc = bacc.Bacc("TRN2", target_bir_lowering=False, num_devices=1)
    ins = [nc.dram_tensor(k, v.shape, mybir.dt.from_np(v.dtype), kind="ExternalInput").ap() for k, v in arrays.items()]
    out = nc.dram_tensor("out", (B, S, D), F32, kind="ExternalOutput").ap()
    program(nc, *ins, out)
    r = run_bass_kernel_spmd(nc, [arrays], core_ids=[0])
    return r.results[0]["out"]
```

```python
from contextlib import ExitStack

import numpy as np

import concourse.bass as bass
from concourse import mybir

F32 = mybir.dt.float32
BF16 = mybir.dt.bfloat16
I32 = mybir.dt.int32
U32 = mybir.dt.uint32
ALU = mybir.AluOpType
ACT = mybir.ActivationFunctionType
AX = mybir.AxisListType

P = 128
B, S, D, H = 4, 512, 256, 16
DK = D // H
T = S // P
C = D // P
HG = 4
NG = H // HG
GW = HG * DK
TERMS = 6
ROWS = TERMS * DK
PARTS = 3
KROWS = ROWS + PARTS
VW = 32
E = 8
F = 1024
FT = F // P
NT = B * T
SLOTS = NT + E - 1
EPS = 1e-5
MASKED = -(2.0 ** 100)
FLOOR = -1e29
SCALE = float(DK) ** -0.5


class Signal:

    def __init__(self, sem, per, lead=0):
        self.sem, self.per, self.lead = sem, per, lead

    def at(self, i, k=0):
        return i * self.per + (self.lead + k)


def wait_alone(eng, sem, value, passed):
    eng.wait_ge(sem, value)
    eng.sem_inc(passed, 1)


class Memory:

    def __init__(self, nc, ctx):
        def sb(name, shape, dt=F32):
            return ctx.enter_context(nc.sbuf_tensor(name, shape, dt))

        self.x = sb("x", [P, B, T, D])
        self.w = [sb(f"w{i}", [P, 4, C, D]) for i in range(2)]
        self.r1 = sb("r1", [P, C * E * F])
        self.r2 = sb("r2", [P, 24576])
        self.cols = sb("cols", [P, 20])
        self.rows = sb("rows", [P, 5, D])
        self.gate = sb("gate", [P, C, D])
        self.ident = sb("ident", [P, P])
        self.identb = sb("identb", [P, P], BF16)
        self.neghalf = sb("neghalf", [P, T])
        self.stats = sb("stats", [P, T, 6])
        self.mv = sb("mv", [P, T, 2])
        self.var = sb("var", [P, T])
        self.rstd = sb("rstd", [P, T])
        self.mv_in = sb("mv_in", [P, B, T, 2])
        self.var_in = sb("var_in", [P, B, T])
        self.rstd_in = sb("rstd_in", [P, B, T])
        self.mv_g = sb("mv_g", [P, B, T, 2])
        self.var_g = sb("var_g", [P, B, T])
        self.rstd_g = sb("rstd_g", [P, B, T])
        self.m = sb("m", [P, T, HG])
        self.mres = sb("mres", [P, T, HG])
        self.mparts = sb("mparts", [P, T, PARTS, HG], BF16)
        self.mT = sb("mT", [PARTS * HG, S], BF16)
        self.den = sb("den", [P, T, HG])
        self.rden = sb("rden", [P, T, HG])
        self.tri = sb("tri", [P, P], BF16)
        self.ones = sb("ones", [P, P], BF16)
        self.count_i = sb("count_i", [P, P], I32)
        self.count = sb("count", [P, P])
        self.number_i = sb("number_i", [P, 1], I32)
        self.number = sb("number", [P, 1])
        self.b1c = sb("b1c", [P, E * FT])
        self.top8 = sb("top8", [P, T, 8])
        self.idx8 = sb("idx8", [P, T, 8], U32)
        self.expert_u = sb("expert_u", [P, T], U32)
        self.ntop = sb("ntop", [P, T])
        self.sum = sb("sum", [P, B, T])
        self.expert = sb("expert", [P, B, T])
        self.prob = sb("prob", [P, B, T])
        self.onehot = sb("onehot", [P, NT + 1, E], BF16)
        self.under = sb("under", [P, E, NT])
        self.upto = sb("upto", [P, E, E])
        self.needs = sb("needs", [P, E, E])
        self.first_row = sb("first_row", [P, SLOTS])
        self.place = self.under[:, :, :].rearrange("p e t -> p (e t)").rearrange("p (t e) -> p t e", t=NT)
        self.more = sb("more", [P, SLOTS, E])
        self.need = sb("need", [P, E])
        self.end = sb("end", [P, E])
        self.start = sb("start", [P, E])
        self.pos = sb("pos", [P, NT])
        self.pos_u = sb("pos_u", [P, NT], U32)
        self.row_u = sb("row_u", [P, NT], U32)
        self.row_f = sb("row_f", [P, NT])
        self.slot_f = sb("slot_f", [P, SLOTS])
        self.token_f = sb("token_f", [P, SLOTS])
        self.filled = sb("filled", [P, SLOTS])
        self.slot_e = sb("slot_e", [P, SLOTS], I32)
        self.source = sb("source", [P, SLOTS], U32)
        self.target = sb("target", [P, SLOTS], U32)
        self.ps = ctx.enter_context(nc.psum_tensor("ps", [P, 8, 512], F32))

        self.total_x, self.block_in = (self.w[0][:, 2 * i:2 * i + 2, :, :].rearrange("p i c d -> p (i c) d")
                                       for i in range(2))

        at = [0]

        def take(region, words, shape, dt=F32):
            n = at[0]
            at[0] += words
            assert at[0] <= region.shape[1], (at[0], region.shape)
            v = region[:, n:n + words]
            if dt is not F32:
                v = v.bitcast(dt)
            if len(shape) == 1:
                return v
            names = "abcd"[:len(shape)]
            kw = dict(zip(names[1:], shape[1:]))
            return v.rearrange(f"p ({' '.join(names)}) -> p {' '.join(names)}", **kw)

        self.mbT = take(self.r1, B * T * S // 2, [B, T, S], BF16)
        at[0] = 0
        self.hn = take(self.r1, T * D, [T, D])
        self.hT = take(self.r1, C * S, [C, S])
        self.cin = take(self.r1, T * D, [T, D])
        self.cT = take(self.r1, C * S, [C, S])
        self.parts = [take(self.r1, PARTS * S // 2, [PARTS, S], BF16) for _ in range(2 * C)]
        self.res = [take(self.r1, S, [S]) for _ in range(2)]
        self.junk = [take(self.r1, S // 2, [S], BF16) for _ in range(8)]
        self.mint = take(self.r1, T * S, [T, S], I32)
        self.mbS = take(self.r1, T * S // 2, [T, S], BF16)
        self.w1 = self.r1[:, :].rearrange("p (c e f) -> p c e f", c=C, e=E)
        at[0] = 0
        self.we = take(self.r1, C * E * D, [C, E, D])
        self.be = take(self.r1, E * D, [E, D])

        at[0] = 0
        self.probs = take(self.r2, T * HG * S, [T, HG, S])
        self.qst = [take(self.r2, HG * S // 2, [HG, S], BF16) for _ in range(NG)]
        self.kst = [take(self.r2, HG * S // 2, [HG, S], BF16) for _ in range(NG)]
        self.v = take(self.r2, B * NG * T * GW, [B, NG, T, GW])
        self.vg = [take(self.r2, T * HG * VW, [T, HG, VW]) for _ in range(2)]
        self.ot = take(self.r2, S, [S])
        self.o = take(self.r2, T * D, [T, D])
        self.oT = take(self.r2, C * S, [C, S])
        at[0] = 0
        self.w2 = take(self.r2, FT * E * D, [FT, E, D])
        self.b2 = take(self.r2, E * D, [E, D])
        gate_from = at[0]
        self.rnT = [take(self.r2, C * S, [C, S]), self.w[0][:, 2:4, :, :].rearrange("p i c d -> p i (c d)")]
        self.rn = take(self.r2, NT * D, [B, T, D])
        logits_from = at[0]
        self.logits = take(self.r2, T * D, [T, D])
        at[0] = gate_from
        self.at_row = take(self.r2, NT * P // 2, [NT, P], BF16)
        at[0] = logits_from
        self.at_slot = take(self.r2, NT * 3 * SLOTS // 2, [NT, 3, SLOTS], BF16)
        at[0] = 0
        self.exps = take(self.r2, T * D, [T, D])
        at[0] = gate_from
        self.xg = [take(self.r2, D, [D]) for _ in range(DEPTH)]
        self.xT = [take(self.r2, C * P, [C, P]) for _ in range(2)]
        self.mid = take(self.r2, F, [F])
        self.midT = take(self.r2, FT * P, [FT, P])
        self.y = [take(self.r2, D, [D]) for _ in range(DEPTH)]
        self.yg = self.r2[:, 0:NT * D].rearrange("p (t d) -> p t d", t=NT)


class Attention:

    def __init__(self, nc, stage, mem, dram, name, w, cross, norms, affine, cols, rows, masked, self_block,
                 fresh, rest, x_first=None, q_loaded=None, acc_stored=None):
        self.fresh, self.rest, self.x_first, self.q_loaded = fresh, rest, x_first, q_loaded
        self.mem, self.dram, self.name = mem, dram, name
        self.w, self.cross, self.norms, self.affine = mem.w[w], cross, norms, affine
        self.cols, self.rows, self.masked, self.self_block = cols, rows, masked, self_block

        self.used = []

        def sig(what, per, lead=0):
            self.used.append(stage.enter_context(nc.semaphore(f"{name}_{what}")))
            return Signal(self.used[-1], per, lead)

        self.passed = {eng: stage.enter_context(nc.semaphore(f"{name}_{eng}_passed")) for eng in ("dve", "pool")}
        self.stat = [sig(f"stat{n}", T) for n in range(norms)]
        self.aggr = [sig(f"aggr{n}", T) for n in range(norms)]
        self.scale = [sig(f"scale{n}", 2) for n in range(norms)]
        if norms == 2:
            self.first_norm = sig("first_norm", T)
        self.hn_ready = sig("hn_ready", T)
        self.hT_ps = sig("hT_ps", C)
        self.hT_ready = sig("hT_ready", C, C)
        if cross:
            self.c_loaded = sig("c_loaded", 16)
            self.cT_ps = sig("cT_ps", C, C)
            self.cT_ready = sig("cT_ready", C, C)
        self.qk_ps = sig("qk_ps", 2 * C, 2 * C)
        self.hi = sig("hi", 2 * C)
        self.r1 = sig("r1", 2 * C, 2 * C)
        self.midp = sig("midp", 2 * C)
        self.lo = sig("lo", 2 * C, 2 * C)
        self.stored = [sig(f"stored{n}", 16 * PARTS, 16 * PARTS) for n in range(2 * C)]
        self.v_ps = sig("v_ps", 2)
        self.v_ready = sig("v_ready", 2, 2)
        if masked:
            self.mask_loaded = sig("mask_loaded", 16)
            self.mbS_ready = sig("mbS_ready", T)
            self.mbT_ps = sig("mbT_ps", MASK_ROUNDS)
            self.mbT_ready = sig("mbT_ready", MASK_ROUNDS)
        if fresh:
            self.preset = sig("preset", 1)
        self.stacks = [sig(f"stacks{s}", 32) for s in range(NG)]
        self.shift = [sig(f"shift{s}", 16) for s in range(NG)]
        self.s_ps = sig("s_ps", UNITS)
        self.s_max = sig("s_max", UNITS)
        self.cut = sig("cut", CUTS)
        self.m_ps = sig("m_ps", 1)
        self.m_sb = sig("m_sb", 1)
        self.st_ps = sig("st_ps", UNITS)
        self.p_exp = sig("p_exp", UNITS)
        self.vg_ready = sig("vg_ready", 1)
        self.pv = sig("pv", T, T)
        self.ot_sb = sig("ot_sb", 1, 1)
        self.ot_ps = sig("ot_ps", 1, 1)
        self.quotient = sig("quotient", QUOTIENT)
        self.oT_ps = sig("oT_ps", C)
        self.oT_sb = sig("oT_sb", C)
        self.op_ps = sig("op_ps", 2)
        self.op_used = sig("op_used", 2)
        if self_block:
            self.step = sig("step", 2 * STEPS)
            self.acc_ready = sig("acc_ready", 2)
            self.acc_stored = Signal(acc_stored, 32, 32)
        self.x_done = self.op_used if rows is None else sig("x_done", 2, 2)




def each_batch(eng, body):
    with eng.Fori(0, B - 1) as b:
        body(b, b + 1)
    body(B - 1, None)


def each_pair(eng, body):
    with eng.Fori(0, B // 2 - 1) as i:
        for odd in range(2):
            body(2 * i + odd, 2 * i + (odd + 1), odd)
    for odd in range(2):
        b = B - 2 + odd
        body(b, b + 1 if b + 1 < B else None, odd)


def tokens_of(a, odd):
    return a.mem.cT if odd and not a.cross else a.mem.hT


QK = 2 * C
QK_BANK = 2


def of_query(n):
    return n >= C


def bias_of(a, n):
    at = a.cols + (C if not of_query(n) else 0) + n % C
    return a.mem.cols[:, at:at + 1]


def load_stacks(sp, a, b, g):
    for dst, src in ((a.mem.qst[g], a.dram["q"]), (a.mem.kst[g], a.dram["k"])):
        rows = src[b, g * GW:(g + 1) * GW, :, :].rearrange("(h r) t n -> (r t) h n", h=HG)
        sp.dma_start(dst[0:ROWS, :, :], rows).then_inc(a.stacks[g].sem, 16)


EARLY = (0, 1, 6, 7)
EACH = 4


def early_scores(pe, a, i):
    mem = a.mem
    for v in range(EACH * i, EACH * (i + 1)):
        if v == 0:
            pe.wait_ge(a.hT_ready.sem, a.hT_ready.at(B))
            pe.wait_ge(a.stacks[0].sem, 32)
            if a.fresh:
                pe.wait_ge(a.preset.sem, NG + 4)
        if v == 2:
            pe.wait_ge(a.v_ready.sem, a.v_ready.at(B))
        if v >= len(EARLY):
            pe.wait_ge(a.s_max.sem, v - len(EARLY) + 1)
        h, t = v // T, v % T
        pe.matmul(mem.ps[:, EARLY[v % len(EARLY)], :], mem.qst[0][0:ROWS, h, t * P:(t + 1) * P],
                  mem.kst[0][0:ROWS, h, :], start=True, stop=True).then_inc(a.s_ps.sem, 1)


def early_maxima(dve, a, i):
    for v in range(EACH * i, EACH * (i + 1)):
        maximum(dve, a, 0, v, EARLY[v % len(EARLY)])


def maximum(dve, a, G, v, bank):
    mem = a.mem
    h, t = v // T, v % T
    out = mem.m[:, t, h:h + 1]
    if a.masked:
        wait_alone(dve, a.s_ps.sem, a.s_ps.at(G, v + 1), a.passed["dve"])
        ins = dve.tensor_tensor_reduce(mem.junk[bank], mem.ps[:, bank, :], mem.mbS[:, t, :], 1.0, FLOOR,
                                       ALU.add, ALU.max, out)
    else:
        dve.wait_ge(a.s_ps.sem, a.s_ps.at(G, v + 1))
        ins = dve.tensor_reduce(out, mem.ps[:, bank, :], AX.X, ALU.max)
    ins.then_inc(a.s_max.sem, 1)


def load_mask(sp, a, b):
    sp.dma_start(a.mem.mint[:, :, :], a.dram["mask"][b]).then_inc(a.mask_loaded.sem, 16)


def mask_for_maxima(dve, a, b, t):
    if t == 0:
        dve.wait_ge(a.mask_loaded.sem, a.mask_loaded.at(b, 16))
    dve.tensor_scalar(a.mem.mbS[:, t, :], a.mem.mint[:, t, :], 0.0, MASKED, ALU.is_equal,
                      ALU.mult).then_inc(a.mbS_ready.sem, 1)
    dve.wait_ge(a.mbS_ready.sem, a.mbS_ready.at(b, t + 1))


def project_vector(dve, a):
    mem = a.mem
    ps = mem.ps

    last = a.norms - 1

    def statistics_first(b):
        if b:
            dve.wait_ge(a.aggr[0].sem, a.aggr[0].at(b - 1, T))
        for t in range(T):
            dve.bn_stats(mem.stats[:, t, :], mem.x[:, b, t, :]).then_inc(a.stat[0].sem, 1)
        for t in range(T):
            dve.wait_ge(a.stat[0].sem, a.stat[0].at(b, t + 1))
            dve.bn_aggr(mem.mv_in[:, b, t, :], mem.stats[:, t, :]).then_inc(a.aggr[0].sem, 1)

    def normalise_first(b):
        wait_alone(dve, a.scale[0].sem, a.scale[0].at(b, 2), a.passed["dve"])
        if type(b) is not int or b:
            dve.wait_ge(a.hT_ps.sem, a.hT_ps.at(b))
        for t in range(T):
            dve.tensor_scalar(mem.hn[:, t, :], mem.x[:, b, t, :], mem.mv_in[:, b, t, 0:1], mem.rstd_in[:, b, t:t + 1],
                              ALU.subtract, ALU.mult).then_inc(a.first_norm.sem, 1)

    def statistics(b):
        for t in range(T):
            if a.norms == 2:
                dve.wait_ge(a.first_norm.sem, a.first_norm.at(b, t + 1))
            src = mem.x[:, b, t, :] if a.norms == 1 else mem.hn[:, t, :]
            dve.bn_stats(mem.stats[:, t, :], src).then_inc(a.stat[last].sem, 1)
        for t in range(T):
            wait_alone(dve, a.stat[last].sem, a.stat[last].at(b, t + 1), a.passed["dve"])
            dve.bn_aggr(mem.mv[:, t, :], mem.stats[:, t, :]).then_inc(a.aggr[last].sem, 1)

    def normalise(b):
        wait_alone(dve, a.scale[last].sem, a.scale[last].at(b, 2), a.passed["dve"])
        if a.norms == 1 and (type(b) is not int or b):
            dve.wait_ge(a.hT_ps.sem, a.hT_ps.at(b))
        for t in range(T):
            src = mem.x[:, b, t, :] if a.norms == 1 else mem.hn[:, t, :]
            dve.tensor_scalar(mem.hn[:, t, :], src, mem.mv[:, t, 0:1], mem.rstd[:, t:t + 1],
                              ALU.subtract, ALU.mult).then_inc(a.hn_ready.sem, 1)

    def values(b, k):
        dve.wait_ge(a.v_ps.sem, a.v_ps.at(b, k + 1))
        for t in range(2):
            out = mem.v[:, b, :, 2 * k + t, :]
            got = ps[:, 6 + k, t * D:(t + 1) * D].rearrange("p (g d) -> p g d", g=NG)
            if a.rows is None:
                ins = dve.tensor_copy(out, got)
            else:
                row = mem.rows[:, a.rows, :].rearrange("p (g d) -> p g d", g=NG)
                ins = dve.tensor_tensor(out, got, row, ALU.add)
        ins.then_inc(a.v_ready.sem, 1)

    def rest(b, n):
        dve.wait_ge(a.hi.sem, a.hi.at(b, n + 1))
        dve.wait_ge(a.lo.sem, a.lo.at(b, n - 1))
        dve.scalar_tensor_tensor(mem.res[n % 2], ps[:, QK_BANK + n, :], bias_of(a, n), mem.parts[n][:, 0, :],
                                 ALU.add, ALU.subtract).then_inc(a.r1.sem, 1)

    def body(b, ahead):
        if not a.cross:
            if ahead is not None:
                normalise_first(ahead)
                statistics(ahead)
            values(b, 0)
            if ahead is not None:
                normalise(ahead)
            values(b, 1)
        else:
            values(b, 0)
            values(b, 1)
        if ahead is None:
            if a.masked:
                for t in range(T):
                    mask_for_maxima(dve, a, 0, t)
            early_maxima(dve, a, 0)
        for n in range(QK):
            rest(b, n)
            if a.cross and ahead is not None:
                if n == 0:
                    statistics(ahead)
                if n == 1:
                    normalise(ahead)
            if ahead is None and n + 1 < UNITS // EACH:
                early_maxima(dve, a, n + 1)

    early = B - 1

    def start(before=None):
        if a.x_first is not None:
            dve.wait_ge(*a.x_first)
        if a.norms == 2:
            for b in range(early):
                if b == early - 1:
                    dve.wait_ge(before.x_done.sem, before.x_done.at(early))
                statistics_first(b)
            dve.wait_ge(a.aggr[0].sem, a.aggr[0].at(early))
            normalise_first(0)
        statistics(0)

    def begin():
        normalise(0)

    def rest_of_batches():
        for sem, value in a.rest:
            dve.wait_ge(sem, value)
        if a.norms == 2:
            dve.wait_ge(a.aggr[1].sem, a.aggr[1].at(1))
            for b in range(early, B):
                statistics_first(b)
            dve.wait_ge(a.aggr[0].sem, a.aggr[0].at(B))
        each_batch(dve, body)

    return start, begin, rest_of_batches


def project_gpsimd(pool, a):
    mem = a.mem

    last = a.norms - 1

    def scale_first(b):
        pool.wait_ge(a.aggr[0].sem, a.aggr[0].at(b, T))
        pool.tensor_scalar(mem.var_in[:, b, :], mem.mv_in[:, b, :, 1], EPS, None, ALU.add).then_inc(a.scale[0].sem, 1)
        pool.wait_ge(a.scale[0].sem, a.scale[0].at(b, 1))
        pool.tensor_tensor(mem.rstd_in[:, b, :], mem.var_in[:, b, :], mem.neghalf[:, :], ALU.pow)\
            .then_inc(a.scale[0].sem, 1)

    def scale(b):
        wait_alone(pool, a.aggr[last].sem, a.aggr[last].at(b, T), a.passed["pool"])
        pool.tensor_scalar(mem.var[:, :], mem.mv[:, :, 1], EPS, None, ALU.add).then_inc(a.scale[last].sem, 1)
        pool.wait_ge(a.scale[last].sem, a.scale[last].at(b, 1))
        pool.tensor_tensor(mem.rstd[:, :], mem.var[:, :], mem.neghalf[:, :], ALU.pow).then_inc(a.scale[last].sem, 1)

    def third(b, n):
        pool.wait_ge(a.midp.sem, a.midp.at(b, n + 1))
        pool.tensor_tensor(mem.parts[n][:, 2, :], mem.res[n % 2], mem.parts[n][:, 1, :],
                           ALU.subtract).then_inc(a.lo.sem, 1)

    def body(b, ahead):
        for n in range(QK):
            if n == 0 and ahead is not None:
                scale(ahead)
            third(b, n)

    if a.norms == 2:
        for b in range(B - 1):
            scale_first(b)
    scale(0)
    if a.norms == 2:
        scale_first(B - 1)
    if a.fresh:
        ones_beside(pool, a)
    each_batch(pool, body)


def ones_beside(pool, a):
    mem = a.mem
    pool.wait_ge(a.scale[-1].sem, 2)
    for s in range(NG):
        pool.memset(mem.kst[s][ROWS:P, :, :], 1.0).then_inc(a.preset.sem, 1)
    pool.wait_ge(a.preset.sem, NG)
    for g in range(2):
        pool.memset(mem.vg[g][:, :, :, DK + 1:VW], 0.0).then_inc(a.preset.sem, 1)
        pool.memset(mem.vg[g][:, :, :, DK:DK + 1], 1.0).then_inc(a.preset.sem, 1)


def project_scalar(act, a):
    mem = a.mem
    ps = mem.ps

    def tokens(b, odd):
        hT = tokens_of(a, odd)
        for c in range(C):
            act.wait_ge(a.hT_ps.sem, a.hT_ps.at(b, c + 1))
            if c == 0 and (type(b) is not int or b):
                act.wait_ge(a.qk_ps.sem, a.qk_ps.at(b if a.cross else b - 1))
            if a.affine is None:
                ins = act.activation(hT[:, c, :], ps[:, c, :], ACT.Copy)
            else:
                g, s = a.affine + c, a.affine + C + c
                ins = act.activation(hT[:, c, :], ps[:, c, :], ACT.Identity, bias=mem.cols[:, s:s + 1],
                                     scale=mem.cols[:, g:g + 1])
            ins.then_inc(a.hT_ready.sem, 1)

    def context(b):
        for c in range(C):
            act.wait_ge(a.cT_ps.sem, a.cT_ps.at(b, c + 1))
            if c == 0:
                act.wait_ge(a.qk_ps.sem, a.qk_ps.at(b - 1, C))
            act.activation(mem.cT[:, c, :], ps[:, 6 + c, :], ACT.Copy).then_inc(a.cT_ready.sem, 1)

    def first_part(b, n):
        act.wait_ge(a.qk_ps.sem, a.qk_ps.at(b, n + 1))
        act.wait_ge(a.stored[n].sem, a.stored[n].at(b))
        act.activation(mem.parts[n][:, 0, :], ps[:, QK_BANK + n, :], ACT.Identity, bias=bias_of(a, n))\
           .then_inc(a.hi.sem, 1)

    def second_part(b, n):
        act.wait_ge(a.r1.sem, a.r1.at(b, n + 1))
        act.activation(mem.parts[n][:, 1, :], mem.res[n % 2], ACT.Copy).then_inc(a.midp.sem, 1)

    def body(b, ahead, odd):
        if a.cross and ahead is None:
            tokens(b, odd)
        for n in range(QK + 1):
            if n == QK - 1 and not a.cross and ahead is not None:
                tokens(ahead, 1 - odd)
            if n < QK:
                first_part(b, n)
            if n >= 1:
                second_part(b, n - 1)
            if a.cross and ahead is not None:
                if n == 0:
                    tokens(b, odd)
                if n == QK - 2:
                    context(ahead)

    def begin():
        act.sem_inc(a.hT_ready.sem, a.hT_ready.lead)
        if a.cross:
            act.sem_inc(a.cT_ready.sem, a.cT_ready.lead)
        if a.cross:
            context(0)
        else:
            tokens(0, 0)

    return begin, lambda: each_pair(act, body)


def project_tensor(pe, a):
    mem = a.mem
    ps = mem.ps

    def turn_tokens(b):
        pe.wait_ge(a.hT_ready.sem, a.hT_ready.at(b))
        pe.wait_ge(a.hn_ready.sem, a.hn_ready.at(b, T))
        for c in range(C):
            for t in range(T):
                ins = pe.transpose(ps[:, c, t * P:(t + 1) * P], mem.hn[:, t, c * P:(c + 1) * P], mem.ident[:, :])
            ins.then_inc(a.hT_ps.sem, 1)

    def turn_context(b):
        pe.wait_ge(a.v_ready.sem, a.v_ready.at(b))
        pe.wait_ge(a.c_loaded.sem, a.c_loaded.at(b, 16))
        for c in range(C):
            for t in range(T):
                ins = pe.transpose(ps[:, 6 + c, t * P:(t + 1) * P], mem.cin[:, t, c * P:(c + 1) * P],
                                   mem.ident[:, :])
            ins.then_inc(a.cT_ps.sem, 1)

    def body(b, ahead, odd):
        hT = tokens_of(a, odd)
        kv = mem.cT if a.cross else hT
        if a.cross:
            if ahead is None:
                turn_tokens(b)
            pe.wait_ge(a.cT_ready.sem, a.cT_ready.at(b, C))
        else:
            pe.wait_ge(a.hT_ready.sem, a.hT_ready.at(b, C))
        pe.wait_ge(a.v_ready.sem, a.v_ready.at(b))
        for k in range(2):
            for t in range(2):
                for c in range(C):
                    ins = pe.matmul(ps[:, 6 + k, t * D:(t + 1) * D], kv[:, c, (2 * k + t) * P:(2 * k + t + 1) * P],
                                    a.w[:, 2, c, :], start=(c == 0), stop=(c == C - 1))
            ins.then_inc(a.v_ps.sem, 1)
        for n in range(QK):
            if ahead is None and n < UNITS // EACH:
                early_scores(pe, a, n)
            if n == C:
                if a.q_loaded is not None:
                    pe.wait_ge(*a.q_loaded)
                pe.wait_ge(a.hT_ready.sem, a.hT_ready.at(b, C))
            src = hT if of_query(n) else kv
            pe.wait_ge(a.r1.sem, a.r1.at(b - 1, n + 1))
            for c in range(C):
                ins = pe.matmul(ps[:, QK_BANK + n, :], a.w[:, 0 if of_query(n) else 1, c, (n % C) * P:(n % C + 1) * P],
                                src[:, c, :], start=(c == 0), stop=(c == C - 1))
            ins.then_inc(a.qk_ps.sem, 1)
            if a.cross and ahead is not None:
                if n == 0:
                    turn_tokens(b)
                if n == QK - 2:
                    turn_context(ahead)
            if n == QK - 2 and not a.cross and ahead is not None:
                turn_tokens(ahead)

    def begin():
        if a.cross:
            pe.sem_inc(a.cT_ps.sem, a.cT_ps.lead)
        pe.sem_inc(a.qk_ps.sem, a.qk_ps.lead)
        pe.sem_inc(a.v_ready.sem, a.v_ready.lead)
        pe.sem_inc(a.r1.sem, a.r1.lead)
        pe.sem_inc(a.lo.sem, a.lo.lead)
        if a.cross:
            turn_context(0)
        else:
            turn_tokens(0)

    return begin, lambda: each_pair(pe, body)


def project_sync(sp, a):
    mem = a.mem

    def context(b):
        if a.cross:
            if type(b) is not int or b:
                sp.wait_ge(a.cT_ps.sem, a.cT_ps.at(b))
            sp.dma_start(mem.cin[:, :, :], a.dram["ctx"][b]).then_inc(a.c_loaded.sem, 16)

    def parts(b, n):
        half = slice((n % C) * P, (n % C + 1) * P)
        out = a.dram["q" if of_query(n) else "k"][b, half, :, :]
        sp.wait_ge(a.lo.sem, a.lo.at(b, n + 1))
        runs = ((0, 3), (3, 5), (5, 6))
        for i, (r0, r1) in enumerate(runs):
            if of_query(n):
                src = mem.parts[n][:, 0:r1 - r0, :]
            else:
                src = mem.parts[n][:, i:i + 1, :].to_broadcast([P, r1 - r0, S])
            sp.dma_start(out[:, r0:r1, :], src).then_inc(a.stored[n].sem, 16)

    def body(b, second):
        for n in range(QK):
            if n == QK - 1 and second is not None:
                context(second)
            parts(b, n)

    def begin():
        for n in range(QK):
            sp.sem_inc(a.stored[n].sem, a.stored[n].lead)
        context(0)

    def rest_of_batches():
        context(1)
        if a.masked:
            load_mask(sp, a, 0)
        with sp.Fori(0, B - 2) as b:
            body(b, b + 2)
        for n in range(QK):
            sp.wait_ge(a.stored[n].sem, a.stored[n].at(1))
        load_stacks(sp, a, 0, 0)
        load_stacks(sp, a, 0, 1)
        body(B - 2, None)
        body(B - 1, None)

    return begin, rest_of_batches



UNITS = T * HG
ROUND = NG * UNITS
LEAD = UNITS + 12
CUTS = 4
QUOTIENT, STEPS = 3, 2
DEEP = 3
ST, SB = 0, DEEP
OB = 2 * DEEP
MISC = OB + 1
MASK_STEPS = ((2, 9), (3, 9))
KEY_TILES = 2
MASK_ROUNDS = T // KEY_TILES
NEXT_STAGE = ((3, 5), (3, 14))
HALF_TURN = (3, 13)
LAST_TURN, LAST_OUT = (5, 2), (3, 4)
LATE = 2
M_STEP, TURN_STEP = 8, 12
OUT_TURNS = (3, 5)
OUT_TILES = ((2, 3), (2, 4), (3, 3), (3, 4))


def before(b, n):
    n -= DEEP
    if n < 0:
        b = b - 1
        n = max(m for m in range(ROUND) if m % DEEP == (n + DEEP) % DEEP)
    return NG * b + n // UNITS, n % UNITS


def led(G, g, u):
    n = LEAD + u
    more = n // UNITS
    return (G + more, (g + more) % NG, n % UNITS) if type(G) is not int or G + more < B * NG else None


def led_bank(n):
    return SB + n % ROUND % DEEP


def attend_sync(sp, a, meanwhile, then=None):
    mem = a.mem

    def shift(b, g):
        G = NG * b + g
        sp.wait_ge(a.m_sb.sem, a.m_sb.at(G, 1))
        sp.dma_start(mem.qst[g][ROWS:KROWS, :, :], mem.mT[:, :]).then_inc(a.shift[g].sem, 16)

    def body(b, first, last):
        for g in range(NG):
            G = NG * b + g
            ahead = (b, g + 2) if g < 2 else (b + 1, g - 2)
            if not (last and g >= 2):
                if first and g == 2:
                    for n in range(QK):
                        sp.wait_ge(a.stored[n].sem, a.stored[n].at(B))
                if not (first and g < 2):
                    sp.wait_ge(a.st_ps.sem, a.st_ps.at(G - 1))
                load_stacks(sp, a, *ahead)
            if a.self_block and g == OUT_TILES[-1][0] and not first:
                store(b - 1)
            if not (last and g == NG - 1):
                shift(*((b, g + 1) if g < NG - 1 else (b + 1, 0)))
            if a.masked and g == 0 and not last:
                sp.wait_ge(a.mbS_ready.sem, a.mbS_ready.at(b, T))
                load_mask(sp, a, b + 1)
            if meanwhile is not None:
                meanwhile(sp, b, g)

    def store(b):
        for k in range(2):
            sp.wait_ge(a.acc_ready.sem, a.acc_ready.at(b, k + 1))
            sp.dma_start(a.dram["acc"][b, :, 2 * k:2 * k + 2, :], mem.total_x[:, 2 * k:2 * k + 2, :])\
              .then_inc(a.acc_stored.sem, 16)

    if a.self_block:
        sp.sem_inc(a.acc_stored.sem, a.acc_stored.lead)
    shift(0, 0)
    body(0, True, False)
    with sp.Fori(1, B - 1) as b:
        body(b, False, False)
    body(B - 1, False, True)
    if then is not None:
        then()
    if a.self_block:
        store(B - 1)


def last_sums(eng, a, name, b, k):
    if a.rows is None:
        return
    mem = a.mem
    two = slice(2 * k, 2 * k + 2)
    x = mem.x[:, b, two, :]
    eng.wait_ge(a.op_used.sem, a.op_used.at(b, k + 1))
    if not a.self_block:
        row = mem.rows[:, a.rows + 1:a.rows + 2, :].to_broadcast([P, 2, D])
        eng.tensor_tensor(x, x, row, ALU.add).then_inc(a.x_done.sem, 1)
        return
    u = mem.block_in[:, two, :]
    eng.wait_ge(a.acc_stored.sem, a.acc_stored.at(b))
    eng.tensor_tensor(mem.total_x[:, two, :], x, u, ALU.add).then_inc(a.acc_ready.sem, 1)
    wait_alone(eng, a.acc_ready.sem, a.acc_ready.at(b, k + 1), a.passed[name])
    eng.tensor_copy(x, u).then_inc(a.x_done.sem, 1)


def attend_gpsimd(pool, a):
    mem = a.mem

    def gather(b, g):
        G = NG * b + g
        if not (type(b) is int and G < 2):
            wait_alone(pool, a.pv.sem, a.pv.at(G - 1), a.passed["pool"])
        pool.tensor_copy(mem.vg[g % 2][:, :, :, 0:DK],
                         mem.v[:, b, g, :, :].rearrange("p t (h d) -> p t h d", h=HG)).then_inc(a.vg_ready.sem, 1)

    if a.x_done is not a.op_used:
        pool.sem_inc(a.x_done.sem, a.x_done.lead)
    pool.wait_ge(a.v_ready.sem, a.v_ready.at(B))
    for g in range(NG):
        gather(0, g)
    with pool.Fori(1, B) as b:
        for g in range(NG):
            gather(b, g)
        for k in range(2):
            last_sums(pool, a, "pool", b - 1, k)


def attend_scalar(act, a, meanwhile):
    mem = a.mem
    ps = mem.ps

    def exps(b, g, u):
        G = NG * b + g
        act.wait_ge(a.st_ps.sem, a.st_ps.at(G, u + 1))
        if u % HG == 0:
            act.wait_ge(a.pv.sem, a.pv.at(G - 1, u // HG + 1))
        act.activation(mem.probs[:, u // HG, u % HG, :], ps[:, ST + (UNITS * g + u) % DEEP, :], ACT.Exp,
                       scale=SCALE).then_inc(a.p_exp.sem, 1)

    def out_copy(G):
        act.wait_ge(a.pv.sem, a.pv.at(G, T))
        act.wait_ge(a.ot_ps.sem, a.ot_ps.at(G))
        act.activation(mem.ot, ps[:, OB, :], ACT.Copy).then_inc(a.ot_sb.sem, 1)

    def maxima(G, used=None):
        act.wait_ge(a.m_ps.sem, a.m_ps.at(G, 1))
        if used is not None:
            b, g = used
            act.wait_ge(a.shift[g].sem, a.shift[g].at(b, 16))
        act.activation(mem.mT[:, :], ps[0:PARTS * HG, MISC, 0:S // 2].bitcast(BF16), ACT.Copy)\
           .then_inc(a.m_sb.sem, 1)

    def mask_copy(b, i, bank=MISC):
        act.wait_ge(a.mbT_ps.sem, a.mbT_ps.at(b, i + 1))
        batch = slice(b, b + 1) if type(b) is int else bass.ds(b, 1)
        act.activation(mem.mbT[:, batch, KEY_TILES * i:KEY_TILES * (i + 1), :].rearrange("p b k n -> p (b k n)"),
                       ps[:, bank, :].bitcast(BF16), ACT.Copy).then_inc(a.mbT_ready.sem, 1)

    def oT_copy(b, c, bank=MISC):
        act.wait_ge(a.oT_ps.sem, a.oT_ps.at(b, c + 1))
        act.activation(mem.oT[:, c, :], ps[:, bank, :], ACT.Copy).then_inc(a.oT_sb.sem, 1)

    def body(b, first, last):
        for g in range(NG):
            G = NG * b + g
            for u in range(UNITS):
                exps(b, g, u)
                if g == 1 and not first and u in OUT_TURNS:
                    oT_copy(b - 1, OUT_TURNS.index(u))
                if u == LATE and not (first and g == 0):
                    out_copy(G - 1)
                if u == M_STEP and not (last and g == NG - 1):
                    maxima(G + 1, (b, g))
                if last and (g, u) == HALF_TURN:
                    oT_copy(b, 0, LAST_TURN[0])
                if a.masked and not last and (g, u) in MASK_STEPS:
                    mask_copy(b + 1, MASK_STEPS.index((g, u)))

    act.sem_inc(a.ot_sb.sem, a.ot_sb.lead)
    if a.masked:
        mask_copy(0, 0, ST + DEEP - 1)
    maxima(0)
    if a.masked:
        mask_copy(0, 1, ST + DEEP - 1)
    body(0, True, False)
    with act.Fori(1, B - 1) as b:
        body(b, False, False)
    body(B - 1, False, True)
    out_copy(B * NG - 1)
    meanwhile()
    for c in range(1, C):
        oT_copy(B - 1, c, LAST_TURN[c])


def attend_tensor(pe, a, meanwhile):
    mem = a.mem
    ps = mem.ps
    misc = [None]

    def take_misc():
        if misc[0] is not None:
            pe.wait_ge(*misc[0])

    def scores(g, v, n, used):
        h, t = v // T, v % T
        if used is not None:
            pe.wait_ge(a.s_max.sem, a.s_max.at(used[0], used[1] + 1))
        pe.matmul(ps[:, led_bank(n), :], mem.qst[g][0:ROWS, h, t * P:(t + 1) * P],
                  mem.kst[g][0:ROWS, h, :], start=True, stop=True).then_inc(a.s_ps.sem, 1)

    def transposed_scores(b, g, u, first):
        G, kt, h = NG * b + g, u // HG, u % HG
        if not (first and UNITS * g + u < DEEP):
            used = before(b, UNITS * g + u)
            pe.wait_ge(a.p_exp.sem, a.p_exp.at(used[0], used[1] + 1))
        if u == 0:
            pe.wait_ge(a.shift[g].sem, a.shift[g].at(b, 16))
            if a.masked and g == 0:
                pe.wait_ge(a.mbT_ready.sem, a.mbT_ready.at(b, MASK_ROUNDS))
        out = ps[:, ST + (UNITS * g + u) % DEEP, :]
        ins = pe.matmul(out, mem.kst[g][0:KROWS, h, kt * P:(kt + 1) * P], mem.qst[g][0:KROWS, h, :],
                        start=True, stop=not a.masked)
        if a.masked:
            batch = slice(b, b + 1) if type(b) is int else bass.ds(b, 1)
            ins = pe.matmul(out, mem.identb[:, :], mem.mbT[:, batch, kt, :].rearrange("p b n -> p (b n)"),
                            start=False, stop=True)
        ins.then_inc(a.st_ps.sem, 1)

    def products(G, g, kt):
        pe.wait_ge(a.p_exp.sem, a.p_exp.at(G, HG * (kt + 1)))
        if kt == 0:
            pe.wait_ge(a.vg_ready.sem, a.vg_ready.at(G, 1))
            pe.wait_ge(a.ot_sb.sem, a.ot_sb.at(G))
        for h in range(HG):
            ins = pe.matmul(ps[h * VW:(h + 1) * VW, OB, :], mem.vg[g % 2][:, kt, h, :], mem.probs[:, kt, h, :],
                            start=(kt == 0), stop=(kt == T - 1))
        ins.then_inc(a.pv.sem, 1)

    def maxima(G):
        pe.wait_ge(a.cut.sem, a.cut.at(G, CUTS))
        take_misc()
        for t in range(T):
            ins = pe.transpose(ps[0:PARTS * HG, MISC, t * P // 2:(t + 1) * P // 2].bitcast(BF16),
                               mem.mparts[:, t, :, :].rearrange("p a h -> p (a h)"), mem.identb[:, :])
        ins.then_inc(a.m_ps.sem, 1)
        misc[0] = (a.m_sb.sem, a.m_sb.at(G, 1))

    def turn_mask(b, i, bank=MISC):
        if bank == MISC:
            take_misc()
        for k in range(KEY_TILES):
            for t in range(T):
                kt = KEY_TILES * i + k
                ins = pe.transpose(ps[:, bank, (T * k + t) * P // 2:(T * k + t + 1) * P // 2].bitcast(BF16),
                                   mem.mbS[:, t, kt * P:(kt + 1) * P], mem.identb[:, :])
        ins.then_inc(a.mbT_ps.sem, 1)
        if bank == MISC:
            misc[0] = (a.mbT_ready.sem, a.mbT_ready.at(b, i + 1))

    def turn(G):
        pe.wait_ge(a.ot_sb.sem, a.ot_sb.at(G, 1))
        take_misc()
        for t in range(T):
            ins = pe.transpose(ps[:, MISC, t * P:(t + 1) * P], mem.ot[:, t * P:(t + 1) * P], mem.ident[:, :])
        ins.then_inc(a.ot_ps.sem, 1)
        misc[0] = (a.quotient.sem, a.quotient.at(G, QUOTIENT))

    def turn_out(b, c, bank=MISC):
        pe.wait_ge(a.quotient.sem, a.quotient.at(NG * b + (c + 1) * NG // C - 1, QUOTIENT))
        if bank == MISC:
            take_misc()
        for t in range(T):
            ins = pe.transpose(ps[:, bank, t * P:(t + 1) * P], mem.o[:, t, c * P:(c + 1) * P], mem.ident[:, :])
        ins.then_inc(a.oT_ps.sem, 1)
        if bank == MISC:
            misc[0] = (a.oT_sb.sem, a.oT_sb.at(b, c + 1))

    def project_out(b, t, bank=MISC):
        pe.wait_ge(a.oT_sb.sem, a.oT_sb.at(b, C))
        if t % 2 == 0 and bank == MISC:
            take_misc()
        for c in range(C):
            ins = pe.matmul(ps[:, bank, t % 2 * D:(t % 2 + 1) * D], mem.oT[:, c, t * P:(t + 1) * P],
                            a.w[:, 3, c, :], start=(c == 0), stop=(c == C - 1))
        if t % 2:
            ins.then_inc(a.op_ps.sem, 1)
        misc[0] = (a.op_used.sem, a.op_used.at(b, t // 2 + 1))

    def body(b, first, last):
        if not first:
            misc[0] = (a.quotient.sem, a.quotient.at(NG * b - 2, QUOTIENT)) if not a.masked else \
                (a.mbT_ready.sem, a.mbT_ready.at(b, MASK_ROUNDS))
        for g in range(NG):
            G = NG * b + g
            for u in range(UNITS):
                transposed_scores(b, g, u, first)
                unit = led(G, g, u)
                if unit is not None:
                    _, s, v = unit
                    if v == 0:
                        pe.wait_ge(a.stacks[s].sem, a.stacks[s].at(b if s > g else b + 1, 32))
                    used = before(b, UNITS * g + u)
                    scores(s, v, UNITS * g + u, (used[0], used[1] + LEAD))
                at = u - HG - LATE + 1
                if at < 0 and u == LATE - 1 and not (first and g == 0):
                    products(G - 1, (g - 1) % NG, T - 1)
                if at >= 0 and at % HG == 0:
                    products(G, g, at // HG)
                if g == 1 and not first and u in OUT_TURNS:
                    turn_out(b - 1, OUT_TURNS.index(u))
                if u == M_STEP and not (last and g == NG - 1):
                    maxima(G + 1)
                if u == TURN_STEP and not (first and g == 0):
                    turn(G - 1)
                if (g, u) in OUT_TILES and not first:
                    project_out(b - 1, OUT_TILES.index((g, u)))
                if last and (g, u) == HALF_TURN:
                    turn_out(b, 0, LAST_TURN[0])
                if a.masked and not last and (g, u) in MASK_STEPS:
                    i = MASK_STEPS.index((g, u))
                    if i == 0:
                        pe.wait_ge(a.mbS_ready.sem, a.mbS_ready.at(b + 1, T))
                    turn_mask(b + 1, i)

    pe.sem_inc(a.pv.sem, a.pv.lead)
    pe.sem_inc(a.ot_ps.sem, a.ot_ps.lead)
    pe.wait_ge(a.r1.sem, a.r1.at(B - 1, 1))
    pe.wait_ge(a.v_ready.sem, a.v_ready.at(B))
    pe.wait_ge(a.stacks[1].sem, 32)
    if a.masked:
        pe.wait_ge(a.mbS_ready.sem, a.mbS_ready.at(0, T))
        turn_mask(0, 0, ST + DEEP - 1)
    for v in range(LEAD - UNITS):
        if a.masked and v == DEEP + 1:
            pe.wait_ge(a.mbT_ready.sem, a.mbT_ready.at(0, 1))
            turn_mask(0, 1, ST + DEEP - 1)
        if v < DEEP:
            bank = led_bank(UNITS - LEAD + v)
            pe.wait_ge(a.r1.sem, a.r1.at(B - 1, bank - QK_BANK + 1))
        scores(1, v, UNITS - LEAD + v, (1, v - DEEP) if v >= DEEP else None)
        if v == DEEP:
            maxima(0)
    body(0, True, False)
    with pe.Fori(1, B - 1) as b:
        body(b, False, False)
    body(B - 1, False, True)
    G = B * NG - 1
    products(G, NG - 1, T - 1)
    turn(G)
    meanwhile()
    for c in range(1, C):
        turn_out(B - 1, c, LAST_TURN[c])
    for t in range(T):
        project_out(B - 1, t, LAST_OUT[t // 2])
    pe.wait_ge(a.op_used.sem, a.op_used.at(B))


def attend_vector(dve, a, meanwhile, beside=None):
    mem = a.mem
    ps = mem.ps

    def split(G):
        dve.wait_ge(a.s_max.sem, a.s_max.at(G, HG * T))
        if not (type(G) is int and G < 1):
            dve.wait_ge(a.m_ps.sem, a.m_ps.at(G))
        m = mem.m[:, :, :]
        hi, mid, lo = (mem.mparts[:, :, i, :] for i in range(PARTS))
        dve.tensor_scalar(hi, m, -1.0, None, ALU.mult).then_inc(a.cut.sem, 1)
        dve.wait_ge(a.cut.sem, a.cut.at(G, 1))
        dve.scalar_tensor_tensor(mem.mres[:, :, :], m, -1.0, hi, ALU.mult, ALU.subtract).then_inc(a.cut.sem, 1)
        dve.wait_ge(a.cut.sem, a.cut.at(G, 2))
        dve.tensor_copy(mid, mem.mres[:, :, :]).then_inc(a.cut.sem, 1)
        dve.wait_ge(a.cut.sem, a.cut.at(G, 3))
        dve.tensor_tensor(lo, mem.mres[:, :, :], mid, ALU.subtract).then_inc(a.cut.sem, 1)

    def normalise(G, b, g, first):
        dve.wait_ge(a.ot_ps.sem, a.ot_ps.at(G, 1))
        if g == 0 and not first:
            dve.wait_ge(a.oT_ps.sem, a.oT_ps.at(b - 1, C))
        got = ps[:, MISC, :].rearrange("p (t h d) -> p t h d", t=T, h=HG)
        dve.tensor_scalar(mem.den[:, :, :], got[:, :, :, DK], 1e-30, None, ALU.max).then_inc(a.quotient.sem, 1)
        dve.wait_ge(a.quotient.sem, a.quotient.at(G, 1))
        dve.reciprocal(mem.rden[:, :, :], mem.den[:, :, :]).then_inc(a.quotient.sem, 1)
        dve.wait_ge(a.quotient.sem, a.quotient.at(G, 2))
        out = mem.o[:, :, g * GW:(g + 1) * GW].rearrange("p t (h d) -> p t h d", h=HG)
        dve.tensor_tensor(out, got[:, :, :, 0:DK], mem.rden[:, :, :].unsqueeze(3).to_broadcast([P, T, HG, DK]),
                          ALU.mult).then_inc(a.quotient.sem, 1)

    def block_input(b, k):
        u, row = mem.block_in[:, 2 * k:2 * k + 2, :], mem.rows[:, a.rows + 1:a.rows + 2, :].to_broadcast([P, 2, D])
        if type(b) is not int or b:
            wait_alone(dve, a.x_done.sem, a.x_done.at(b - 1, k + 1), a.passed["dve"])
        for t in range(2 * k, 2 * k + 2):
            ins = dve.tensor_scalar(mem.block_in[:, t, :], mem.x[:, b, t, :], mem.mv_in[:, b, t, 0:1],
                                    mem.rstd_in[:, b, t:t + 1], ALU.subtract, ALU.mult)
        ins.then_inc(a.step.sem, 1)
        dve.wait_ge(a.step.sem, a.step.at(b, STEPS * k + 1))
        dve.tensor_tensor(u, u, row, ALU.add).then_inc(a.step.sem, 1)

    def residual(b, k, bank=MISC):
        two = slice(2 * k, 2 * k + 2)
        x = mem.x[:, b, two, :]
        got = ps[:, bank, :].rearrange("p (t d) -> p t d", t=2)
        if not a.self_block:
            dve.wait_ge(a.op_ps.sem, a.op_ps.at(b, k + 1))
            ins = dve.tensor_tensor(x, got, x, ALU.add)
            ins.then_inc(a.op_used.sem, 1)
            return
        u = mem.block_in[:, two, :]
        dve.wait_ge(a.step.sem, a.step.at(b, STEPS * k + 2))
        dve.wait_ge(a.op_ps.sem, a.op_ps.at(b, k + 1))
        dve.tensor_tensor(u, got, u, ALU.add).then_inc(a.op_used.sem, 1)

    def body(b, first, last):
        for g in range(NG):
            G = NG * b + g
            for u in range(UNITS):
                unit = led(G, g, u)
                if unit is not None:
                    led_group, s, v = unit
                    if a.masked and s == 0 and v < T:
                        mask_for_maxima(dve, a, b + 1, v)
                    maximum(dve, a, led_group, v, led_bank(UNITS * g + u))
                    if v == UNITS - 1:
                        split(led_group)
                if u == TURN_STEP + 1 and not (first and g == 0):
                    normalise(G - 1, b if g else b - 1, (g - 1) % NG, first)
                if not first and (g, u - 1) in OUT_TILES[1::2]:
                    k = OUT_TILES[1::2].index((g, u - 1))
                    if a.self_block:
                        block_input(b - 1, k)
                    residual(b - 1, k)
                if last and (g, u) in NEXT_STAGE:
                    meanwhile[NEXT_STAGE.index((g, u))]()

    split(0)
    for v in range(LEAD - UNITS):
        maximum(dve, a, 1, v, led_bank(UNITS - LEAD + v))
    body(0, True, False)
    with dve.Fori(1, B - 1) as b:
        body(b, False, False)
    body(B - 1, False, True)
    if a.self_block:
        for k in range(2):
            block_input(B - 1, k)
    normalise(B * NG - 1, B - 1, NG - 1, False)
    if beside is not None:
        dve.wait_ge(a.oT_ps.sem, a.oT_ps.at(B))
        beside()
    for k in range(2):
        residual(B - 1, k, LAST_OUT[k])
        last_sums(dve, a, "dve", B - 1, k)
    dve.wait_ge(a.x_done.sem, a.x_done.at(B))



CHOICE = 2 * T + 2
DEPTH = 6
ABSENT = 2 * NT * P


class Mixture:

    def __init__(self, nc, stage, mem, dram, name, affine, gate_width, row, hidden, b2, weights, loads,
                 x_done, space, acc_stored, gathered, earlier, scattered=None, fetched=None):
        self.mem, self.dram, self.name, self.affine = mem, dram, name, affine
        self.width, self.row, self.hidden, self.b2 = gate_width, row, hidden, b2
        self.weights, self.loads = weights, loads
        self.space, self.x_done, self.acc_stored = space, x_done, acc_stored
        self.used = []

        def sig(what, per, lead=0):
            self.used.append(stage.enter_context(nc.semaphore(f"{name}_{what}")))
            return Signal(self.used[-1], per, lead)

        self.passed = {eng: stage.enter_context(nc.semaphore(f"{name}_{eng}_passed")) for eng in ("dve",)}
        self.stat = sig("stat", T)
        self.aggr = sig("aggr", T)
        self.scale = sig("scale", 2)
        self.rn_ready = sig("rn_ready", 1)
        self.rn_stored = sig("rn_stored", 16)
        self.rnT_ps = sig("rnT_ps", C, C)
        self.rnT_ready = sig("rnT_ready", C, C)
        self.g_ps = sig("g_ps", 2)
        self.logit = sig("logit", 2, 2)
        self.choice = sig("choice", CHOICE)
        if hidden is None:
            self.ntop = sig("ntop", 1)
            self.exps = sig("exps", T, T)
        self.route = sig("route", 1)
        self.operands = sig("operands", 1)
        self.products = sig("products", 1)
        self.experts = sig("experts", 1)
        self.routed = sig("routed", 1)
        leads = [16 * earlier * len(range(j, SLOTS, DEPTH)) for j in range(DEPTH)]
        self.gathered = [Signal(gathered[j], 16, leads[j]) for j in range(DEPTH)]
        self.stored = [Signal(scattered[j], 16) for j in range(DEPTH)] if hidden is not None else \
            [sig(f"stored{j}", 16) for j in range(DEPTH)]
        self.tx_ps = sig("tx_ps", 1)
        self.xT_ready = sig("xT_ready", 1, 2)
        self.h_ps = sig("h_ps", 2)
        self.mid_ready = sig("mid_ready", 2, 2)
        self.tm_ps = sig("tm_ps", 2, 2)
        self.midT_ready = sig("midT_ready", 2, 2)
        self.y_ps = sig("y_ps", 1, 2)
        self.y_sum = sig("y_sum", 1, 2)
        if hidden is None:
            self.y_ready = sig("y_ready", 1)
        if hidden is not None:
            self.acc_loaded = sig("acc_loaded", 16)
        self.fetched = [Signal(sem, 16 * T) for sem in fetched] if fetched else \
            [sig(f"fetched{b}", 16) for b in range(B)]
        self.x_ready = sig("x_ready", 1)
        if hidden is None:
            self.out_stored = sig("out_stored", 16)


def gate_vector(dve, m):
    mem = m.mem
    ps = mem.ps

    def statistics(b):
        if b:
            dve.wait_ge(m.aggr.sem, m.aggr.at(b - 1, T))
        for t in range(T):
            dve.bn_stats(mem.stats[:, t, :], mem.x[:, b, t, :]).then_inc(m.stat.sem, 1)
        for t in range(T):
            dve.wait_ge(m.stat.sem, m.stat.at(b, t + 1))
            dve.bn_aggr(mem.mv_g[:, b, t, :], mem.stats[:, t, :]).then_inc(m.aggr.sem, 1)

    def normalise(b):
        dve.wait_ge(m.scale.sem, m.scale.at(b, 2))
        for t in range(T):
            ins = dve.tensor_scalar(mem.rn[:, b, t, :], mem.x[:, b, t, :], mem.mv_g[:, b, t, 0:1],
                                    mem.rstd_g[:, b, t:t + 1], ALU.subtract, ALU.mult)
        ins.then_inc(m.rn_ready.sem, 1)

    def body(b):
        if m.hidden is None:
            dve.wait_ge(m.exps.sem, m.exps.at(b))
        for k in range(2):
            dve.wait_ge(m.g_ps.sem, m.g_ps.at(b, k + 1))
            got = ps[:, 2 + k, 0:2 * m.width].rearrange("p (t d) -> p t d", t=2)
            row = mem.rows[:, m.row:m.row + 1, 0:m.width].to_broadcast([P, 2, m.width])
            dve.tensor_tensor(mem.logits[:, 2 * k:2 * k + 2, 0:m.width], got, row, ALU.add).then_inc(m.logit.sem, 1)
        for t in range(T):
            wait_alone(dve, m.logit.sem, m.logit.at(b, t // 2 + 1), m.passed["dve"])
            dve.max(mem.top8[:, t, :], mem.logits[:, t, 0:m.width]).then_inc(m.choice.sem, 1)
        if m.hidden is None:
            dve.wait_ge(m.choice.sem, m.choice.at(b, T))
            dve.tensor_scalar(mem.ntop[:, :], mem.top8[:, :, 0], -1.0, None, ALU.mult).then_inc(m.ntop.sem, 1)
        for t in range(T):
            wait_alone(dve, m.choice.sem, m.choice.at(b, t + 1), m.passed["dve"])
            dve.max_index(mem.idx8[:, t, :], mem.top8[:, t, :], mem.logits[:, t, 0:m.width]).then_inc(m.choice.sem, 1)
        dve.wait_ge(m.choice.sem, m.choice.at(b, 2 * T))
        dve.tensor_scalar(mem.expert_u[:, :], mem.idx8[:, :, 0], E - 1, None, ALU.bitwise_and).then_inc(m.choice.sem, 1)
        wait_alone(dve, m.choice.sem, m.choice.at(b, CHOICE - 1), m.passed["dve"])
        dve.tensor_copy(mem.expert[:, b, :], mem.expert_u[:, :]).then_inc(m.choice.sem, 1)

    early = B - 1

    def start(before):
        dve.sem_inc(m.logit.sem, m.logit.lead)
        for b in range(early):
            if b == early - 1:
                dve.wait_ge(before.x_done.sem, before.x_done.at(early))
            statistics(b)

    def begin():
        normalise(0)

    def between():
        for b in range(1, early):
            normalise(b)

    def rest_of_batches():
        for b in range(early, B):
            statistics(b)
        body(0)
        for b in range(early, B):
            normalise(b)
        with dve.Fori(1, B) as b:
            body(b)

    return start, begin, between, rest_of_batches


def gate_gpsimd(pool, m):
    mem = m.mem
    for b in range(B):
        pool.wait_ge(m.aggr.sem, m.aggr.at(b, T))
        pool.tensor_scalar(mem.var_g[:, b, :], mem.mv_g[:, b, :, 1], EPS, None, ALU.add).then_inc(m.scale.sem, 1)
        pool.wait_ge(m.scale.sem, m.scale.at(b, 1))
        pool.tensor_tensor(mem.rstd_g[:, b, :], mem.var_g[:, b, :], mem.neghalf[:, :], ALU.pow).then_inc(m.scale.sem, 1)


def gate_scalar(act, m):
    mem = m.mem
    ps = mem.ps

    def turned(b):
        for c in range(C):
            act.wait_ge(m.rnT_ps.sem, m.rnT_ps.at(b, c + 1))
            if b == 1 and c == 0:
                act.wait_ge(m.x_done.sem, m.x_done.at(B))
            if b >= 2:
                act.wait_ge(m.g_ps.sem, m.g_ps.at(b - 1))
            if m.affine is None:
                ins = act.activation(mem.rnT[b % 2][:, c, :], ps[:, c, :], ACT.Copy)
            else:
                g, s = m.affine + c, m.affine + C + c
                ins = act.activation(mem.rnT[b % 2][:, c, :], ps[:, c, :], ACT.Identity, bias=mem.cols[:, s:s + 1],
                                     scale=mem.cols[:, g:g + 1])
            ins.then_inc(m.rnT_ready.sem, 1)

    def body(b):
        if b + 1 < B:
            turned(b + 1)
        if m.hidden is None:
            act.wait_ge(m.ntop.sem, m.ntop.at(b, 1))
            for t in range(T):
                act.activation(mem.exps[:, t, :], mem.logits[:, t, :], ACT.Exp, bias=mem.ntop[:, t:t + 1],
                               accum_out=mem.sum[:, b, t:t + 1]).then_inc(m.exps.sem, 1)

    def begin():
        act.sem_inc(m.rnT_ready.sem, m.rnT_ready.lead)
        if m.hidden is None:
            act.sem_inc(m.exps.sem, m.exps.lead)
        turned(0)

    def rest_of_batches():
        for b in range(B):
            body(b)

    return begin, rest_of_batches


def gate_tensor(pe, m):
    mem = m.mem
    ps = mem.ps

    def turn(b):
        pe.wait_ge(m.rnT_ready.sem, m.rnT_ready.at(b))
        pe.wait_ge(m.rn_ready.sem, m.rn_ready.at(b, 1))
        for c in range(C):
            for t in range(T):
                ins = pe.transpose(ps[:, c, t * P:(t + 1) * P], mem.rn[:, b, t, c * P:(c + 1) * P], mem.ident[:, :])
            ins.then_inc(m.rnT_ps.sem, 1)

    def body(b):
        if b + 1 < B:
            turn(b + 1)
        pe.wait_ge(m.rnT_ready.sem, m.rnT_ready.at(b, C))
        pe.wait_ge(m.logit.sem, m.logit.at(b))
        for k in range(2):
            for t in range(2):
                for c in range(C):
                    ins = pe.matmul(ps[:, 2 + k, t * m.width:(t + 1) * m.width],
                                    mem.rnT[b % 2][:, c, (2 * k + t) * P:(2 * k + t + 1) * P], mem.gate[:, c, 0:m.width],
                                    start=(c == 0), stop=(c == C - 1))
            ins.then_inc(m.g_ps.sem, 1)

    def begin():
        pe.sem_inc(m.rnT_ps.sem, m.rnT_ps.lead)
        turn(0)

    def rest_of_batches():
        for b in range(B):
            body(b)

    return begin, rest_of_batches


COUNTS, TOKENS = 6, 7


def route_vector(dve, m):
    mem = m.mem
    ps = mem.ps
    done = [0]

    def then(ins):
        done[0] += 1
        ins.then_inc(m.route.sem, 1)
        dve.wait_ge(m.route.sem, done[0])

    def along(v, n):
        return v.unsqueeze(2).to_broadcast([P, v.shape[1], n])

    def across(v, n):
        return v.unsqueeze(1).to_broadcast([P, n, v.shape[1]])

    rank = ps[:, COUNTS, 0:NT * E].rearrange("p (t e) -> p t e", t=NT)
    total = ps[:, COUNTS, NT * E:NT * E + E]
    expert = mem.expert[:, :, :].rearrange("p b t -> p (b t)")
    dve.wait_ge(m.choice.sem, m.choice.at(B))
    dve.tensor_tensor(mem.onehot[:, 0:NT, :], along(expert, E), across(mem.count[:, 0:E], NT), ALU.is_equal)\
       .then_inc(m.operands.sem, 1)
    dve.tensor_tensor(mem.upto[:, :, :], along(mem.count[:, 0:E], E), across(mem.count[:, 0:E], E), ALU.is_ge)
    then(dve.tensor_scalar(mem.first_row[:, :], mem.count[:, 0:SLOTS], float(P), None, ALU.mult))
    if m.hidden is None:
        dve.wait_ge(m.exps.sem, m.exps.at(B))
        dve.reciprocal(mem.prob[:, :, :], mem.sum[:, :, :])
    dve.wait_ge(m.products.sem, 1)
    then(dve.tensor_tensor(mem.under[:, :, :], along(total, NT), across(mem.first_row[:, 0:NT], E), ALU.is_gt))
    then(dve.tensor_reduce(mem.need[:, :], mem.under[:, :, :], AX.X, ALU.add))
    then(dve.tensor_tensor(mem.needs[:, :, :], mem.upto[:, :, :], across(mem.need[:, :], E), ALU.mult))
    then(dve.tensor_reduce(mem.end[:, :], mem.needs[:, :, :], AX.X, ALU.add))
    then(dve.tensor_tensor(mem.start[:, :], mem.end[:, :], mem.need[:, :], ALU.subtract))
    then(dve.scalar_tensor_tensor(mem.place[:, :, :], across(mem.start[:, :], NT), float(P), rank, ALU.mult, ALU.add))
    then(dve.tensor_tensor(mem.place[:, :, :], mem.place[:, :, :], mem.onehot[:, 0:NT, :], ALU.mult))
    then(dve.tensor_reduce(mem.pos[:, :], mem.place[:, :, :], AX.X, ALU.add))
    then(dve.tensor_copy(mem.pos_u[:, :], mem.pos[:, :]))
    then(dve.tensor_scalar(mem.row_u[:, :], mem.pos_u[:, :], P - 1, None, ALU.bitwise_and))
    then(dve.tensor_copy(mem.row_f[:, :], mem.row_u[:, :]))
    then(dve.tensor_tensor(mem.pos[:, :], mem.pos[:, :], mem.row_f[:, :], ALU.subtract))
    dve.tensor_tensor(mem.at_row[:, :, :], along(mem.row_f[:, :], P), across(mem.count[:, :], NT), ALU.is_equal)
    then(dve.tensor_tensor(mem.at_slot[:, :, 2, :], along(mem.pos[:, :], SLOTS), across(mem.first_row[:, :], NT),
                           ALU.is_equal))
    dve.tensor_scalar(mem.at_slot[:, :, 0, :], mem.at_slot[:, :, 2, :], mem.number[:, 0:1], None, ALU.mult)
    dve.tensor_tensor(mem.at_slot[:, :, 1, :], mem.at_slot[:, :, 2, :], along(mem.count[:, 0:NT], SLOTS),
                      ALU.mult).then_inc(m.operands.sem, 1)
    then(dve.tensor_tensor(mem.more[:, :, :], along(mem.count[:, 0:SLOTS], E), across(mem.end[:, :], SLOTS),
                           ALU.is_ge))
    then(dve.tensor_reduce(mem.slot_f[:, :], mem.more[:, :, :], AX.X, ALU.add))
    dve.tensor_scalar(mem.slot_e[:, :], mem.slot_f[:, :], float(E - 1), None, ALU.min).then_inc(m.experts.sem, 1)
    dve.wait_ge(m.products.sem, 2)
    number, tile, filled = (ps[:, TOKENS, i * SLOTS:(i + 1) * SLOTS] for i in range(3))
    then(dve.tensor_scalar(mem.token_f[:, :], tile, float(P), None, ALU.mult))
    then(dve.tensor_tensor(mem.token_f[:, :], number, mem.token_f[:, :], ALU.add))
    dve.tensor_copy(mem.source[:, :], mem.token_f[:, :]).then_inc(m.routed.sem, 1)
    if m.hidden is None:
        return
    then(dve.tensor_scalar(mem.filled[:, :], filled, -float(ABSENT), float(ABSENT), ALU.mult, ALU.add))
    then(dve.tensor_tensor(mem.filled[:, :], mem.filled[:, :], mem.token_f[:, :], ALU.add))
    dve.tensor_copy(mem.target[:, :], mem.filled[:, :]).then_inc(m.routed.sem, 1)


def route_tensor(pe, m):
    mem = m.mem
    ps = mem.ps
    pe.wait_ge(m.operands.sem, 1)
    onehot = mem.onehot[:, :, :].rearrange("p t e -> p (t e)")
    pe.matmul(ps[:, COUNTS, 0:(NT + 1) * E], mem.tri[:, :], onehot, start=True, stop=False)
    for t in range(NT):
        ins = pe.matmul(ps[:, COUNTS, (t + 1) * E:(NT + 1) * E], mem.ones[:, :],
                        mem.onehot[:, t:t + 1, :].to_broadcast([P, NT - t, E]), start=False, stop=(t == NT - 1))
    ins.then_inc(m.products.sem, 1)
    pe.wait_ge(m.operands.sem, 2)
    for t in range(NT):
        ins = pe.matmul(ps[:, TOKENS, 0:3 * SLOTS], mem.at_row[:, t, :],
                        mem.at_slot[:, t, :, :].rearrange("p a s -> p (a s)"), start=(t == 0), stop=(t == NT - 1))
    ins.then_inc(m.products.sem, 1)


def expert_of(eng, m, s):
    return eng.value_load(m.mem.slot_e[0:1, bass.ds(s, 1)], min_val=0, max_val=E - 1)


def each_slot(eng, body):
    rounds = SLOTS // DEPTH
    for s in range(DEPTH):
        body(s, s, 0)
    with eng.Fori(1, rounds) as i:
        for j in range(DEPTH):
            body(i * DEPTH + j, j, i)
    for s in range(rounds * DEPTH, SLOTS):
        body(s, s % DEPTH, s // DEPTH)


def follows(s, n):
    return type(s) is not int or s + n < SLOTS


def all_stored(eng, m):
    for j in range(DEPTH):
        eng.wait_ge(m.stored[j].sem, m.stored[j].at(len(range(j, SLOTS, DEPTH))))


def expert_gpsimd(pool, m, done=()):
    mem = m.mem

    def gather(s):
        if s >= DEPTH:
            pool.wait_ge(m.tx_ps.sem, m.tx_ps.at(s - DEPTH, 1))
        pool.indirect_dma_start(mem.xg[s % DEPTH], None, m.dram["rows"],
                                bass.IndirectOffsetOnAxis(ap=mem.source[:, s:s + 1], axis=0))\
            .then_inc(m.gathered[s % DEPTH].sem, 16)

    pool.wait_ge(m.rn_stored.sem, m.rn_stored.at(B))
    pool.wait_ge(m.routed.sem, 1)
    for s in range(DEPTH):
        gather(s)
    for stage in done:
        for sem in (*stage.used, *stage.passed.values()):
            pool.sem_clear(sem)
    if m.hidden is None:
        for s in range(DEPTH, SLOTS):
            gather(s)
        all_stored(pool, m)
        for t in range(NT):
            pool.indirect_dma_start(mem.yg[:, t, :], None, m.dram["slots"],
                                    bass.IndirectOffsetOnAxis(ap=mem.pos_u[:, t:t + 1], axis=0))\
                .then_inc(m.fetched[t // T].sem, 16)
        return
    pool.wait_ge(m.routed.sem, 2)
    for s in range(SLOTS):
        if s >= 1 and s - 1 + DEPTH < SLOTS:
            gather(s - 1 + DEPTH)
        pool.wait_ge(m.y_sum.sem, m.y_sum.at(s, 1))
        pool.indirect_dma_start(m.dram["y"], bass.IndirectOffsetOnAxis(ap=mem.target[:, s:s + 1], axis=0),
                                mem.y[s % DEPTH], None, bounds_check=NT * P - 1, oob_is_err=False)\
            .then_inc(m.stored[s % DEPTH].sem, 16)


def expert_scalar(act, m):
    mem = m.mem
    ps = mem.ps
    act.sem_inc(m.xT_ready.sem, m.xT_ready.lead)
    act.sem_inc(m.midT_ready.sem, m.midT_ready.lead)
    act.wait_ge(m.experts.sem, 1)

    def turned(s, j):
        act.wait_ge(m.tx_ps.sem, m.tx_ps.at(s, 1))
        act.wait_ge(m.y_ps.sem, m.y_ps.at(s - 1))
        if m.hidden is None:
            act.activation(mem.xT[j % 2].rearrange("p c n -> p (c n)"), ps[:, TX[j % 2], 0:C * P], ACT.Copy)\
               .then_inc(m.xT_ready.sem, 1)
            return
        for c in range(C):
            g, sh = m.affine + c, m.affine + C + c
            ins = act.activation(mem.xT[j % 2][:, c, :], ps[:, TX[j % 2], c * P:(c + 1) * P], ACT.Identity,
                                 bias=mem.cols[:, sh:sh + 1], scale=mem.cols[:, g:g + 1])
        ins.then_inc(m.xT_ready.sem, 1)

    def hidden(s):
        e = expert_of(act, m, s)
        act.wait_ge(m.y_ps.sem, m.y_ps.at(s))
        for f in range(FT):
            if f % 4 == 0:
                act.wait_ge(m.tm_ps.sem, m.tm_ps.at(s, f // 4 + 1))
            ins = act.activation(mem.midT[:, f, :], ps[:, TM[f // 4], (f % 4) * P:(f % 4 + 1) * P], ACT.Relu,
                                 bias=mem.b1c[:, bass.ds(e * FT + f, 1)])
            if f % 4 == 3:
                ins.then_inc(m.midT_ready.sem, 1)

    def body(s, j, i):
        if m.hidden is not None:
            hidden(s)
        if follows(s, 2):
            turned(s + 2, j + 2)
        if m.hidden is None:
            act.wait_ge(m.y_sum.sem, m.y_sum.at(s, 1))
            act.activation(mem.y[j], mem.y[j], ACT.Relu).then_inc(m.y_ready.sem, 1)

    turned(0, 0)
    turned(1, 1)
    each_slot(act, body)


def expert_vector(dve, m):
    mem = m.mem
    ps = mem.ps
    dve.sem_inc(m.mid_ready.sem, m.mid_ready.lead)
    dve.sem_inc(m.y_sum.sem, m.y_sum.lead)
    dve.wait_ge(m.experts.sem, 1)

    def hidden(s):
        for k in range(2):
            dve.wait_ge(m.h_ps.sem, m.h_ps.at(s, k + 1))
            if k == 0:
                dve.wait_ge(m.tm_ps.sem, m.tm_ps.at(s))
            dve.tensor_copy(mem.mid[:, k * 512:(k + 1) * 512], ps[:, UP[k], :]).then_inc(m.mid_ready.sem, 1)

    held = [None]

    def out(s, j, i):
        e = expert_of(dve, m, s) if j == 0 else held[0]
        held[0] = expert_of(dve, m, s + 1) if j < DEPTH - 1 and follows(s, 1) else None
        dve.wait_ge(m.y_ps.sem, m.y_ps.at(s, 1))
        if type(s) is not int or s >= DEPTH:
            dve.wait_ge(m.stored[j].sem, m.stored[j].at(i))
        bias = m.b2[:, bass.ds(e, 1), :].rearrange("p e d -> p (e d)")
        dve.tensor_tensor(mem.y[j], ps[:, DOWN[j % 2], 0:D], bias, ALU.add).then_inc(m.y_sum.sem, 1)

    def body(s, j, i):
        if m.hidden is not None and follows(s, 1):
            hidden(s + 1)
        out(s, j, i)

    if m.hidden is not None:
        hidden(0)
    each_slot(dve, body)


TX, UP, TM, DOWN = (0, 6), (1, 2), (3, 4), (5, 7)


def expert_tensor(pe, m):
    mem = m.mem
    ps = mem.ps
    pe.sem_inc(m.tm_ps.sem, m.tm_ps.lead)
    pe.sem_inc(m.y_ps.sem, m.y_ps.lead)
    pe.wait_ge(m.experts.sem, 1)
    pe.wait_ge(m.routed.sem, 2 if m.hidden is not None else 1)

    def turn_in(s, j, i):
        pe.wait_ge(m.gathered[j].sem, m.gathered[j].at(i, 16))
        pe.wait_ge(m.xT_ready.sem, m.xT_ready.at(s - 1))
        for c in range(C):
            ins = pe.transpose(ps[:, TX[j % 2], c * P:(c + 1) * P], mem.xg[j][:, c * P:(c + 1) * P], mem.ident[:, :])
        ins.then_inc(m.tx_ps.sem, 1)

    def up(s, j, e):
        pe.wait_ge(m.xT_ready.sem, m.xT_ready.at(s, 1))
        pe.wait_ge(m.mid_ready.sem, m.mid_ready.at(s))
        for k in range(2):
            for c in range(C):
                w = mem.w1[:, c, bass.ds(e, 1), k * 512:(k + 1) * 512].rearrange("p e f -> p (e f)")
                ins = pe.matmul(ps[:, UP[k], :], mem.xT[j % 2][:, c, :], w, start=(c == 0), stop=(c == C - 1))
            ins.then_inc(m.h_ps.sem, 1)

    def turn_mid(s):
        pe.wait_ge(m.midT_ready.sem, m.midT_ready.at(s))
        for f in range(FT):
            if f % 4 == 0:
                pe.wait_ge(m.mid_ready.sem, m.mid_ready.at(s, f // 4 + 1))
            ins = pe.transpose(ps[:, TM[f // 4], (f % 4) * P:(f % 4 + 1) * P], mem.mid[:, f * P:(f + 1) * P],
                               mem.ident[:, :])
            if f % 4 == 3:
                ins.then_inc(m.tm_ps.sem, 1)

    def down(s, j, e):
        pe.wait_ge(m.y_sum.sem, m.y_sum.at(s - 1))
        if m.hidden is None:
            pe.wait_ge(m.xT_ready.sem, m.xT_ready.at(s, 1))
            for c in range(C):
                w = mem.we[:, c, bass.ds(e, 1), :].rearrange("p e d -> p (e d)")
                ins = pe.matmul(ps[:, DOWN[j % 2], 0:D], mem.xT[j % 2][:, c, :], w, start=(c == 0), stop=(c == C - 1))
        else:
            for f in range(FT):
                if f % 4 == 0:
                    pe.wait_ge(m.midT_ready.sem, m.midT_ready.at(s, f // 4 + 1))
                w = mem.w2[:, f, bass.ds(e, 1), :].rearrange("p e d -> p (e d)")
                ins = pe.matmul(ps[:, DOWN[j % 2], 0:D], mem.midT[:, f, :], w, start=(f == 0), stop=(f == FT - 1))
        ins.then_inc(m.y_ps.sem, 1)

    held = {}

    def expert(s, j):
        if j not in held:
            held[j] = expert_of(pe, m, s)
        return held[j]

    def body(s, j, i):
        if j == 0:
            held.clear()
        ahead = 0
        if m.hidden is not None:
            ahead = 1
            if follows(s, 1):
                expert(s + 1, j + 1)
            turn_mid(s)
            if follows(s, 1):
                up(s + 1, j + 1, expert(s + 1, j + 1))
        down(s, j, expert(s, j))
        if j < DEPTH - 1 and follows(s, ahead + 1):
            expert(s + ahead + 1, j + ahead + 1)
        if follows(s, 2):
            turn_in(s + 2, (j + 2) % DEPTH, i + (j + 2) // DEPTH)

    turn_in(0, 0, 0)
    turn_in(1, 1, 0)
    pe.wait_ge(*m.weights)
    if m.hidden is not None:
        up(0, 0, expert_of(pe, m, 0))
    each_slot(pe, body)
    pe.wait_ge(m.y_sum.sem, m.y_sum.at(SLOTS))


def last_weights(sp, m):
    sp.wait_ge(*m.space)
    for dst, src in m.loads:
        sp.dma_start(dst, src).then_inc(m.weights[0], 16)


def combine_sync(sp, m, out, loaded, next_loads, meanwhile=None):
    mem = m.mem
    rows = m.dram["rows"].rearrange("(b t p) d -> b p t d", b=B, t=T)
    for b in range(B):
        sp.wait_ge(m.rn_ready.sem, m.rn_ready.at(b, 1))
        sp.dma_start(rows[b], mem.rn[:, b, :, :]).then_inc(m.rn_stored.sem, 16)
    sp.wait_ge(m.y_sum.sem, m.y_sum.at(DEPTH))
    if m.hidden is not None:
        sp.wait_ge(m.acc_stored.sem, m.acc_stored.at(B))
    for dst, src in next_loads:
        sp.dma_start(dst, src).then_inc(loaded, 16)
    if m.hidden is not None:
        for b in range(B):
            sp.dma_start(mem.x[:, b, :, :], m.dram["acc"][b]).then_inc(m.acc_loaded.sem, 16)
    if meanwhile is not None:
        sp.wait_ge(m.h_ps.sem, m.h_ps.at(SLOTS))
        meanwhile()
    if m.hidden is not None:
        all_stored(sp, m)
        y = m.dram["y"].rearrange("(b t p) d -> b p t d", b=B, t=T)
        for b in range(B):
            sp.dma_start(mem.yg[:, b * T:(b + 1) * T, :], y[b]).then_inc(m.fetched[b].sem, 16)
    else:
        def store(s, j, i):
            sp.wait_ge(m.y_ready.sem, m.y_ready.at(s, 1))
            sp.dma_start(m.dram["slots"][bass.ds(s * P, P), :], mem.y[j]).then_inc(m.stored[j].sem, 16)

        each_slot(sp, store)
    if out is not None:
        for b in range(B):
            sp.wait_ge(m.x_ready.sem, b + 1)
            sp.dma_start(out[b].rearrange("(t p) d -> p t d", p=P), mem.x[:, b, :, :]).then_inc(m.out_stored.sem, 16)
        sp.wait_ge(m.out_stored.sem, 16 * B)


def combine_vector(dve, m, between=()):
    mem = m.mem
    if m.hidden is not None:
        dve.wait_ge(m.acc_loaded.sem, 16 * B)
    for b in range(B):
        dve.wait_ge(m.fetched[b].sem, m.fetched[b].at(1))
        if m.hidden is not None:
            ins = dve.tensor_tensor(mem.x[:, b, :, :], mem.x[:, b, :, :], mem.yg[:, b * T:(b + 1) * T, :], ALU.add)
        else:
            for t in range(T):
                ins = dve.scalar_tensor_tensor(mem.x[:, b, t, :], mem.yg[:, b * T + t, :], mem.prob[:, b, t:t + 1],
                                               mem.x[:, b, t, :], ALU.mult, ALU.add)
        ins.then_inc(m.x_ready.sem, 1)
        if b < len(between):
            if b == 0:
                dve.wait_ge(m.x_ready.sem, 1)
            between[b]()



WA, WB, WC = 0, 1, 0


def program(nc, x, ctx_in, mask, wa, wb, wc, cols, rows, b1c, b2, gate0, w1, w2, gate1, we, be, out):
    dram = {
        "ctx": ctx_in.rearrange("b (t p) d -> b p t d", p=P),
        "mask": mask.rearrange("b o (t p) k -> b p (o t) k", p=P),
        "q": nc.dram_tensor("q_parts", (B, D, TERMS, S), BF16, kind="Internal").ap(),
        "k": nc.dram_tensor("k_parts", (B, D, TERMS, S), BF16, kind="Internal").ap(),
        "acc": nc.dram_tensor("residual", (B, P, T, D), F32, kind="Internal").ap(),
        "rows": nc.dram_tensor("token_rows", (NT * P, D), F32, kind="Internal").ap(),
        "slots": nc.dram_tensor("slot_rows", (SLOTS * P, D), F32, kind="Internal").ap(),
        "y": nc.dram_tensor("expert_rows", (NT * P, D), F32, kind="Internal").ap(),
    }
    with ExitStack() as ctx:
        mem = Memory(nc, ctx)
        def semaphore(name):
            return ctx.enter_context(nc.semaphore(name))

        x_first, x_rest, weights_a, weights_qo, loaded, setup, acc_stored = (semaphore(n) for n in (
            "x_first", "x_rest", "weights_a", "weights_qo", "loaded", "setup", "acc_stored"))
        weights = [semaphore(f"weights{i}") for i in range(2)]
        gathered, scattered, fetched = ([semaphore(f"{what}{j}") for j in range(n)] for what, n in (
            ("gathered", DEPTH), ("scattered", DEPTH), ("me1_fetched", B)))
        tokens = [(mem.x[:, b, :, :], x[b].rearrange("(t p) d -> p t d", p=P)) for b in range(B)]
        first = [(mem.rows[:, :, :], rows[0]), (mem.b1c[:, :], b1c), (mem.w[WB][:, :, :, :], wb),
                 (mem.gate[:, :, 0:E], gate0)]
        second = [(mem.w[WC][:, :, :, :], wc), (mem.gate[:, :, :], gate1), (mem.rows[:, :, :], rows[1])]

        def load_first(sp):
            sp.dma_start(mem.w[WA][:, 1:3, :, :], wa[:, 1:3, :, :]).then_inc(weights_a, 16)
            sp.dma_start(*tokens[0]).then_inc(x_first, 16)
            for i in (0, 3):
                sp.dma_start(mem.w[WA][:, i, :, :], wa[:, i, :, :]).then_inc(weights_qo, 16)

        def load_tokens(sp):
            for b in range(1, B):
                sp.dma_start(*tokens[b]).then_inc(x_rest, 16)

        def constants(pool):
            pool.memset(mem.neghalf[:, :], -0.5).then_inc(setup, 1)
            pool.memset(mem.ident[:, :], 0.0).then_inc(setup, 1)
            pool.memset(mem.identb[:, :], 0.0).then_inc(setup, 1)
            pool.memset(mem.ones[:, :], 1.0).then_inc(setup, 1)
            pool.memset(mem.tri[:, :], 1.0).then_inc(setup, 1)
            pool.memset(mem.onehot[:, NT, :], 0.0).then_inc(setup, 1)
            pool.iota(mem.count_i[:, :], [[1, P]], base=0, channel_multiplier=0).then_inc(setup, 1)
            pool.iota(mem.number_i[:, :], [[1, 1]], base=0, channel_multiplier=1).then_inc(setup, 1)
            pool.wait_ge(setup, 8)
            for eye in (mem.ident, mem.identb):
                pool.affine_select(out=eye[:, :], in_=eye[:, :], compare_op=ALU.not_equal, fill=1.0, base=0,
                                   pattern=[[-1, P]], channel_multiplier=1).then_inc(setup, 1)
            pool.affine_select(out=mem.tri[:, :], in_=mem.tri[:, :], compare_op=ALU.is_gt, fill=0.0, base=0,
                               pattern=[[1, P]], channel_multiplier=-1).then_inc(setup, 1)
            pool.tensor_copy(mem.count[:, :], mem.count_i[:, :]).then_inc(setup, 1)
            pool.tensor_copy(mem.number[:, :], mem.number_i[:, :]).then_inc(setup, 1)

        def other_loads(sp, b, g):
            if type(b) is int and b == 0:
                dst, src = first[g]
                sp.dma_start(dst, src).then_inc(loaded, 16)

        def first_weights(sp, b, g):
            G = NG * b + g
            sp.dma_start(mem.w1.rearrange("p c e f -> p (c e) f")[:, G, :],
                         w1.rearrange("p c e f -> p (c e) f")[:, G, :]).then_inc(weights[0], 16)

        def all_weights(sp, b, g):
            G = NG * b + g
            sp.dma_start(mem.we.rearrange("p c e d -> p (c e) d")[:, G, :],
                         we.rearrange("p c e d -> p (c e) d")[:, G, :]).then_inc(weights[1], 16)
            if type(b) is int and b == 0:
                some = slice(g * E // NG, (g + 1) * E // NG)
                sp.dma_start(mem.be[:, some, :], be[:, some, :]).then_inc(weights[1], 16)

        pieces = [(mem.b2, b2)] + [(mem.w2[:, f, :, :], w2[:, f, :, :]) for f in range(FT)]
        layer0, layer1 = (loaded, 16 * len(first)), (loaded, 16 * (len(first) + len(second)))

        with ExitStack() as again:
            xa0 = Attention(nc, again, mem, dram, "xa0", WA, True, 1, None, 0, None, True, False, True,
                            ((x_rest, 16 * (B - 1)), (weights_a, 32)), (x_first, 16), (weights_qo, 32))
            sa0 = Attention(nc, again, mem, dram, "sa0", WB, False, 2, 12, 4, 0, False, True, False,
                            (layer0,), acc_stored=acc_stored)
            me0 = Mixture(nc, ctx, mem, dram, "me0", 16, E, 4, F, mem.b2,
                          (weights[0], 16 * (C * E + len(pieces))), pieces,
                          sa0.x_done, (sa0.pv.sem, sa0.pv.at(B * NG)), sa0.acc_stored, gathered, 0, scattered=scattered)
        xa1 = Attention(nc, ctx, mem, dram, "xa1", WC, True, 1, None, 8, 2, False, False, True,
                        (layer1, (me0.x_ready.sem, me0.x_ready.at(B))))
        me1 = Mixture(nc, ctx, mem, dram, "me1", None, D, 4, None, mem.be, (weights[1], 16 * (C * E + NG)), (),
                      xa1.x_done, None, None, gathered, 1, fetched=fetched)

        with nc.Block() as block:

            @block.sync
            def _(sp):
                sp.dma_start(mem.cols[:, :], cols).then_inc(weights_a, 16)
                begin, rest = project_sync(sp, xa0)
                begin()
                load_first(sp)
                load_tokens(sp)
                rest()
                attend_sync(sp, xa0, other_loads)
                begin, rest = project_sync(sp, sa0)
                begin()
                rest()
                attend_sync(sp, sa0, first_weights, lambda: last_weights(sp, me0))
                begin, rest = project_sync(sp, xa1)
                combine_sync(sp, me0, None, loaded, second, begin)
                rest()
                attend_sync(sp, xa1, all_weights)
                combine_sync(sp, me1, out, loaded, ())

            @block.gpsimd
            def _(pool):
                constants(pool)
                project_gpsimd(pool, xa0)
                attend_gpsimd(pool, xa0)
                project_gpsimd(pool, sa0)
                attend_gpsimd(pool, sa0)
                gate_gpsimd(pool, me0)
                expert_gpsimd(pool, me0, (xa0, sa0))
                project_gpsimd(pool, xa1)
                attend_gpsimd(pool, xa1)
                gate_gpsimd(pool, me1)
                expert_gpsimd(pool, me1)

            @block.scalar
            def _(act):
                begin, rest = project_scalar(act, xa0)
                begin()
                act.wait_ge(weights_a, 32)
                rest()
                begin, rest = project_scalar(act, sa0)
                attend_scalar(act, xa0, begin)
                rest()
                begin, rest = gate_scalar(act, me0)
                attend_scalar(act, sa0, begin)
                rest()
                expert_scalar(act, me0)
                begin, rest = project_scalar(act, xa1)
                begin()
                rest()
                begin, rest = gate_scalar(act, me1)
                attend_scalar(act, xa1, begin)
                rest()
                expert_scalar(act, me1)

            @block.vector
            def _(dve):
                def last_values(a):
                    dve.wait_ge(a.vg_ready.sem, a.vg_ready.at(B * NG))

                start, begin, rest = project_vector(dve, xa0)
                start()
                begin()
                rest()
                start, begin, rest = project_vector(dve, sa0)
                attend_vector(dve, xa0, (lambda: start(xa0), begin))
                rest()
                start, begin, between, rest = gate_vector(dve, me0)
                attend_vector(dve, sa0, (lambda: start(sa0), lambda: (last_values(sa0), begin())), between)
                rest()
                route_vector(dve, me0)
                expert_vector(dve, me0)
                start, begin, rest = project_vector(dve, xa1)
                combine_vector(dve, me0, (start, begin))
                rest()
                start, begin, between, rest = gate_vector(dve, me1)
                attend_vector(dve, xa1, (lambda: start(xa1), lambda: (last_values(xa1), begin())), between)
                rest()
                route_vector(dve, me1)
                expert_vector(dve, me1)
                combine_vector(dve, me1)

            @block.tensor
            def _(pe):
                pe.wait_ge(setup, 13)
                begin, rest = project_tensor(pe, xa0)
                begin()
                pe.wait_ge(weights_a, 32)
                rest()
                begin, rest = project_tensor(pe, sa0)
                attend_tensor(pe, xa0, begin)
                pe.wait_ge(*layer0)
                rest()
                begin, rest = gate_tensor(pe, me0)
                attend_tensor(pe, sa0, begin)
                rest()
                route_tensor(pe, me0)
                expert_tensor(pe, me0)
                begin, rest = project_tensor(pe, xa1)
                begin()
                pe.wait_ge(*layer1)
                rest()
                begin, rest = gate_tensor(pe, me1)
                attend_tensor(pe, xa1, begin)
                rest()
                route_tensor(pe, me1)
                expert_tensor(pe, me1)


def kernel(**inputs):
    import concourse.bacc as bacc
    from concourse.bass_utils import run_bass_kernel_spmd

    a = {k: np.asarray(v) for k, v in inputs.items()}

    def weight(w):
        return w.reshape(C, P, -1).transpose(1, 0, 2)

    def weights(names, turned):
        return np.ascontiguousarray(np.stack([weight(a[n].T if turned else a[n]) for n in names], 1))

    def col(v):
        return v.reshape(C, P).T

    def row(v):
        return np.broadcast_to(np.pad(v, (0, D - v.size)), (P, D))

    zero = np.zeros(D, np.float32)
    f0, x1, f1 = "L0_ffn_", "L1_xattn_", "L1_ffn_"
    arrays = {
        "x": a["x"], "ctx": a["ctx_1024"], "mask": a["mask_Bx1xSxS2_ik0"],
        "wa": weights(["L0_xattn_W_Q", "L0_xattn_W_K", "L0_xattn_W_V", "L0_xattn_W_O"], True),
        "wb": weights([f0 + "wq", f0 + "wk", f0 + "wv", f0 + "wo"], False),
        "wc": weights([x1 + "Wq", x1 + "Wk", x1 + "Wv", x1 + "Wo"], True),
        "cols": np.concatenate([col(v) for v in (
            zero, zero, a[f0 + "bq"], a[f0 + "bk"], a[x1 + "bq"], a[x1 + "bk"],
            a[f0 + "ln1_g"], a[f0 + "ln1_b"], a[f0 + "ln2_g"], a[f0 + "ln2_b"])], 1),
        "rows": np.stack([
            np.stack([row(v) for v in (a[f0 + "bv"], a[f0 + "bo"], zero, zero, a[f0 + "gate_b"])], 1),
            np.stack([row(v) for v in (zero, zero, a[x1 + "bv"], a[x1 + "bo"], a[f1 + "bg"])], 1)]),
        "b1c": a[f0 + "b1"].reshape(E * FT, P).T,
        "b2": np.broadcast_to(a[f0 + "b2"], (P, E, D)),
        "gate0": weight(a[f0 + "gate_w"]),
        "w1": a[f0 + "w1"].reshape(E, C, P, F).transpose(2, 1, 0, 3),
        "w2": a[f0 + "w2"].reshape(E, FT, P, D).transpose(2, 1, 0, 3),
        "gate1": weight(a[f1 + "Wg"]),
        "we": a[f1 + "We"].reshape(E, C, P, D).transpose(2, 1, 0, 3),
        "be": np.broadcast_to(a[f1 + "be"], (P, E, D)),
    }
    arrays = {f"in_{k}": np.ascontiguousarray(v) for k, v in arrays.items()}
    nc = bacc.Bacc("TRN2", target_bir_lowering=False, num_devices=1)
    ins = [nc.dram_tensor(k, v.shape, mybir.dt.from_np(v.dtype), kind="ExternalInput").ap() for k, v in arrays.items()]
    out = nc.dram_tensor("out", (B, S, D), F32, kind="ExternalOutput").ap()
    program(nc, *ins, out)
    r = run_bass_kernel_spmd(nc, [arrays], core_ids=[0])
    return r.results[0]["out"]
```
